# Optimizing a Trainium2 kernel written in Bass

```python
import numpy as np
import jax
import jax.numpy as jnp

def _softmax(x, axis=-1):
    return jax.nn.softmax(x, axis=axis)

def _gelu(x):
    return jax.nn.gelu(x, approximate=True)

def _silu(x):
    return jax.nn.silu(x)

def _sigmoid(x):
    return jax.nn.sigmoid(x)

def _layernorm(x, axis=-1, eps=1e-05):
    m = jnp.mean(x, axis=axis, keepdims=True)
    v = jnp.var(x, axis=axis, keepdims=True)
    return (x - m) / jnp.sqrt(v + eps)

def _scatter_add(tgt, idx, src, axis=0):
    return tgt.at[idx].add(src)

def _segment_sum(src, seg, n):
    return jax.ops.segment_sum(src, seg, n)
kernel_name = 'mk_gnn_resnorm_d2_gnn_r8_1b3ecb'

def setup_inputs(seed: int=0):
    np.random.seed(seed)
    _w = jnp.asarray

    def _rec_inputs():
        import jax
        import jax.numpy as jnp
        _gk = jax.random.key(seed)
        x = -0.0005207 + 1.001 * jax.random.normal(jax.random.fold_in(_gk, 1), (6250, 256), jnp.float32)
        src = jax.random.randint(jax.random.fold_in(_gk, 2), (200000,), 0, 6250, jnp.int32)
        dst = jax.random.randint(jax.random.fold_in(_gk, 3), (200000,), 0, 6250, jnp.int32)
        _o = jnp.argsort(dst, stable=True)
        src = src[_o]
        dst = dst[_o]
        edge_weight = jax.random.uniform(jax.random.fold_in(_gk, 12), (200000,), jnp.float32, 0.0, 0.999998)
        node_vec = jax.random.uniform(jax.random.fold_in(_gk, 13), (6250,), jnp.float32, 0.0, 0.999833)
        return (x, src, dst, edge_weight, node_vec)
    x, src, dst, edge_weight, node_vec = _rec_inputs()

    def _L0_gnn_setup():
        import jax, jax.numpy as jnp
        import numpy as np
        from jax import lax
        N, E, D = (1024, 32768, 256)
        NH, FOUT = (4, 64)
        D_STATE, D_CONV, DT_RANK = (16, 4, 16)

        def _layer_norm(x, g, b, eps=1e-05):
            mu = jnp.mean(x, -1, keepdims=True)
            var = jnp.var(x, -1, keepdims=True)
            return (x - mu) * lax.rsqrt(var + eps) * g + b

        def _mamba(xs, in_proj_w, conv_w, conv_b, x_proj_w, dt_proj_w, dt_proj_b, A_log, D_param, out_proj_w):
            n = xs.shape[0]
            xz = xs @ in_proj_w.T
            xc, z = jnp.split(xz, 2, axis=-1)
            K = conv_w.shape[1]
            xp = jnp.pad(xc, ((K - 1, 0), (0, 0)))
            xc = sum((xp[k:k + n] * conv_w[:, k] for k in range(K))) + conv_b
            xc = jax.nn.silu(xc)
            dbc = xc @ x_proj_w.T
            dt = jax.nn.softplus(dbc[:, :DT_RANK] @ dt_proj_w.T + dt_proj_b)
            Bm = dbc[:, DT_RANK:DT_RANK + D_STATE]
            Cm = dbc[:, DT_RANK + D_STATE:]
            A = -jnp.exp(A_log)
            dA = jnp.exp(dt[:, :, None] * A)
            dBx = (dt * xc)[:, :, None] * Bm[:, None, :]

            def step(h, t):
                dA_t, dBx_t, C_t = t
                h = dA_t * h + dBx_t
                return (h, h @ C_t)
            _, y = lax.scan(step, jnp.zeros((xc.shape[1], D_STATE), xs.dtype), (dA, dBx, Cm))
            y = y + xc * D_param
            y = y * jax.nn.silu(z)
            return y @ out_proj_w.T

        def _forward(x, edge_index, deg_noise, gat_w, gat_a_src, gat_a_tgt, gat_b, ln_local_g, ln_local_b, ln_global_g, ln_global_b, ln2_g, ln2_b, in_proj_w, conv_w, conv_b, x_proj_w, dt_proj_w, dt_proj_b, A_log, D_param, out_proj_w, wl, wg, ff1_w, ff1_b, ff2_w, ff2_b):
            n = x.shape[0]
            src, tgt = (edge_index[0], edge_index[1])
            proj = (x @ gat_w.T).reshape(n, NH, FOUT)
            s_src = jnp.sum(proj * gat_a_src, -1)
            s_tgt = jnp.sum(proj * gat_a_tgt, -1)
            e = jax.nn.leaky_relu(s_src[src] + s_tgt[tgt], 0.2)
            exp_e = jnp.exp(e - jnp.max(e))
            denom = jax.ops.segment_sum(exp_e, tgt, num_segments=n)
            attn = exp_e / (denom[tgt] + 1e-16)
            agg = jax.ops.segment_sum(proj[src] * attn[:, :, None], tgt, num_segments=n)
            h_local = jax.nn.elu((agg + x.reshape(n, NH, FOUT)).reshape(n, NH * FOUT) + gat_b)
            h_local = _layer_norm(h_local, ln_local_g, ln_local_b)
            deg = jax.ops.segment_sum(jnp.ones((src.shape[0],), x.dtype), src, num_segments=n)
            perm = jnp.argsort(deg + deg_noise, stable=True)
            inv = jnp.argsort(perm)
            y = _mamba(x[perm], in_proj_w, conv_w, conv_b, x_proj_w, dt_proj_w, dt_proj_b, A_log, D_param, out_proj_w)
            h_attn = _layer_norm(x + y[inv], ln_global_g, ln_global_b)
            gate = jax.nn.sigmoid(h_local @ wl.T + h_attn @ wg.T)
            h = gate * h_local + (1.0 - gate) * h_attn
            ff = jax.nn.relu(h @ ff1_w.T + ff1_b) @ ff2_w.T + ff2_b
            return _layer_norm(h + ff, ln2_g, ln2_b)
        key = jax.random.key(seed)
        ks = jax.random.split(key, 24)
        w = lambda i, shape, s=0.05: jax.random.normal(ks[i], shape, dtype=jnp.float32) * s
        return {'x': jax.random.normal(ks[0], (N, D), dtype=jnp.float32), 'edge_index': jax.random.randint(ks[1], (2, E), 0, N, dtype=jnp.int32), 'edge_prob': jax.random.uniform(ks[2], (E,), dtype=jnp.float32), 'deg_noise': jax.random.uniform(ks[3], (N,), dtype=jnp.float32), 'gat_w': w(4, (NH * FOUT, D)), 'gat_a_src': w(5, (NH, FOUT)), 'gat_a_tgt': w(6, (NH, FOUT)), 'gat_b': jnp.zeros((NH * FOUT,), jnp.float32), 'ln_local_g': jnp.ones((D,), jnp.float32), 'ln_local_b': jnp.zeros((D,), jnp.float32), 'ln_global_g': jnp.ones((D,), jnp.float32), 'ln_global_b': jnp.zeros((D,), jnp.float32), 'ln2_g': jnp.ones((D,), jnp.float32), 'ln2_b': jnp.zeros((D,), jnp.float32), 'in_proj_w': w(7, (2 * D, D)), 'conv_w': w(8, (D, D_CONV), 0.2), 'conv_b': jnp.zeros((D,), jnp.float32), 'x_proj_w': w(9, (DT_RANK + 2 * D_STATE, D)), 'dt_proj_w': w(10, (D, DT_RANK)), 'dt_proj_b': w(11, (D,), 0.1) - 4.0, 'A_log': jnp.log(jnp.tile(jnp.arange(1, D_STATE + 1, dtype=jnp.float32), (D, 1))), 'D_param': jnp.ones((D,), jnp.float32), 'out_proj_w': w(12, (D, D)), 'wl': w(13, (D, D)), 'wg': w(14, (D, D)), 'ff1_w': w(15, (2 * D, D)), 'ff1_b': jnp.zeros((2 * D,), jnp.float32), 'ff2_w': w(16, (D, 2 * D)), 'ff2_b': jnp.zeros((D,), jnp.float32)}
    _L0_gnn_all = _L0_gnn_setup()
    _L0_gnn_in = {k: v for k, v in _L0_gnn_all.items() if k in ('gat_w', 'gat_a_src', 'gat_a_tgt', 'gat_b', 'ln_local_g', 'ln_local_b', 'ln_global_g', 'ln_global_b', 'ln2_g', 'ln2_b', 'in_proj_w', 'conv_w', 'conv_b', 'x_proj_w', 'dt_proj_w', 'dt_proj_b', 'A_log', 'D_param', 'out_proj_w', 'wl', 'wg', 'ff1_w', 'ff1_b', 'ff2_w', 'ff2_b')}
    del _L0_gnn_all

    def _L1_gnn_setup():
        import jax, jax.numpy as jnp
        import numpy as np
        N_NODES = 6250
        N_EDGES = 100000
        IN_DIM = 256
        OUT_DIM = 256
        BN_EPS = 1e-05
        key = jax.random.key(seed)
        k1, k2, k3, k4 = jax.random.split(key, 4)
        x = jax.random.normal(k1, (N_NODES, IN_DIM), dtype=jnp.float32)
        edge_index = jax.random.randint(k2, (2, N_EDGES), 0, N_NODES, dtype=jnp.int64)
        W = jax.random.normal(k3, (IN_DIM, OUT_DIM), dtype=jnp.float32) * 0.05
        b = jnp.zeros((OUT_DIM,), dtype=jnp.float32)
        gamma = jnp.ones((OUT_DIM,), dtype=jnp.float32)
        beta = jnp.zeros((OUT_DIM,), dtype=jnp.float32)
        return {'x': x, 'edge_index': edge_index, 'W': W, 'b': b, 'gamma': gamma, 'beta': beta}
    _L1_gnn_all = _L1_gnn_setup()
    _L1_gnn_in = {k: v for k, v in _L1_gnn_all.items() if k in ('W', 'b', 'gamma', 'beta')}
    del _L1_gnn_all
    return {'x': x, 'src': src, 'dst': dst, 'edge_weight': edge_weight, 'node_vec': node_vec, 'L0_gnn_gat_w': _L0_gnn_in['gat_w'], 'L0_gnn_gat_a_src': _L0_gnn_in['gat_a_src'], 'L0_gnn_gat_a_tgt': _L0_gnn_in['gat_a_tgt'], 'L0_gnn_gat_b': _L0_gnn_in['gat_b'], 'L0_gnn_ln_local_g': _L0_gnn_in['ln_local_g'], 'L0_gnn_ln_local_b': _L0_gnn_in['ln_local_b'], 'L0_gnn_ln_global_g': _L0_gnn_in['ln_global_g'], 'L0_gnn_ln_global_b': _L0_gnn_in['ln_global_b'], 'L0_gnn_ln2_g': _L0_gnn_in['ln2_g'], 'L0_gnn_ln2_b': _L0_gnn_in['ln2_b'], 'L0_gnn_in_proj_w': _L0_gnn_in['in_proj_w'], 'L0_gnn_conv_w': _L0_gnn_in['conv_w'], 'L0_gnn_conv_b': _L0_gnn_in['conv_b'], 'L0_gnn_x_proj_w': _L0_gnn_in['x_proj_w'], 'L0_gnn_dt_proj_w': _L0_gnn_in['dt_proj_w'], 'L0_gnn_dt_proj_b': _L0_gnn_in['dt_proj_b'], 'L0_gnn_A_log': _L0_gnn_in['A_log'], 'L0_gnn_D_param': _L0_gnn_in['D_param'], 'L0_gnn_out_proj_w': _L0_gnn_in['out_proj_w'], 'L0_gnn_wl': _L0_gnn_in['wl'], 'L0_gnn_wg': _L0_gnn_in['wg'], 'L0_gnn_ff1_w': _L0_gnn_in['ff1_w'], 'L0_gnn_ff1_b': _L0_gnn_in['ff1_b'], 'L0_gnn_ff2_w': _L0_gnn_in['ff2_w'], 'L0_gnn_ff2_b': _L0_gnn_in['ff2_b'], 'L1_gnn_W': _L1_gnn_in['W'], 'L1_gnn_b': _L1_gnn_in['b'], 'L1_gnn_gamma': _L1_gnn_in['gamma'], 'L1_gnn_beta': _L1_gnn_in['beta']}

def reference(x, src, dst, edge_weight, node_vec, L0_gnn_gat_w, L0_gnn_gat_a_src, L0_gnn_gat_a_tgt, L0_gnn_gat_b, L0_gnn_ln_local_g, L0_gnn_ln_local_b, L0_gnn_ln_global_g, L0_gnn_ln_global_b, L0_gnn_ln2_g, L0_gnn_ln2_b, L0_gnn_in_proj_w, L0_gnn_conv_w, L0_gnn_conv_b, L0_gnn_x_proj_w, L0_gnn_dt_proj_w, L0_gnn_dt_proj_b, L0_gnn_A_log, L0_gnn_D_param, L0_gnn_out_proj_w, L0_gnn_wl, L0_gnn_wg, L0_gnn_ff1_w, L0_gnn_ff1_b, L0_gnn_ff2_w, L0_gnn_ff2_b, L1_gnn_W, L1_gnn_b, L1_gnn_gamma, L1_gnn_beta):
    import jax
    import jax.numpy as jnp

    def _L0_gnn_ref(x, edge_index, edge_prob, deg_noise, gat_w, gat_a_src, gat_a_tgt, gat_b, ln_local_g, ln_local_b, ln_global_g, ln_global_b, ln2_g, ln2_b, in_proj_w, conv_w, conv_b, x_proj_w, dt_proj_w, dt_proj_b, A_log, D_param, out_proj_w, wl, wg, ff1_w, ff1_b, ff2_w, ff2_b):
        import jax, jax.numpy as jnp
        import numpy as np
        from jax import lax
        N, E, D = (1024, 32768, 256)
        NH, FOUT = (4, 64)
        D_STATE, D_CONV, DT_RANK = (16, 4, 16)

        def _layer_norm(x, g, b, eps=1e-05):
            mu = jnp.mean(x, -1, keepdims=True)
            var = jnp.var(x, -1, keepdims=True)
            return (x - mu) * lax.rsqrt(var + eps) * g + b

        def _mamba(xs, in_proj_w, conv_w, conv_b, x_proj_w, dt_proj_w, dt_proj_b, A_log, D_param, out_proj_w):
            n = xs.shape[0]
            xz = xs @ in_proj_w.T
            xc, z = jnp.split(xz, 2, axis=-1)
            K = conv_w.shape[1]
            xp = jnp.pad(xc, ((K - 1, 0), (0, 0)))
            xc = sum((xp[k:k + n] * conv_w[:, k] for k in range(K))) + conv_b
            xc = jax.nn.silu(xc)
            dbc = xc @ x_proj_w.T
            dt = jax.nn.softplus(dbc[:, :DT_RANK] @ dt_proj_w.T + dt_proj_b)
            Bm = dbc[:, DT_RANK:DT_RANK + D_STATE]
            Cm = dbc[:, DT_RANK + D_STATE:]
            A = -jnp.exp(A_log)
            dA = jnp.exp(dt[:, :, None] * A)
            dBx = (dt * xc)[:, :, None] * Bm[:, None, :]

            def step(h, t):
                dA_t, dBx_t, C_t = t
                h = dA_t * h + dBx_t
                return (h, h @ C_t)
            _, y = lax.scan(step, jnp.zeros((xc.shape[1], D_STATE), xs.dtype), (dA, dBx, Cm))
            y = y + xc * D_param
            y = y * jax.nn.silu(z)
            return y @ out_proj_w.T

        def _forward(x, edge_index, deg_noise, gat_w, gat_a_src, gat_a_tgt, gat_b, ln_local_g, ln_local_b, ln_global_g, ln_global_b, ln2_g, ln2_b, in_proj_w, conv_w, conv_b, x_proj_w, dt_proj_w, dt_proj_b, A_log, D_param, out_proj_w, wl, wg, ff1_w, ff1_b, ff2_w, ff2_b):
            n = x.shape[0]
            src, tgt = (edge_index[0], edge_index[1])
            proj = (x @ gat_w.T).reshape(n, NH, FOUT)
            s_src = jnp.sum(proj * gat_a_src, -1)
            s_tgt = jnp.sum(proj * gat_a_tgt, -1)
            e = jax.nn.leaky_relu(s_src[src] + s_tgt[tgt], 0.2)
            exp_e = jnp.exp(e - jnp.max(e))
            denom = jax.ops.segment_sum(exp_e, tgt, num_segments=n)
            attn = exp_e / (denom[tgt] + 1e-16)
            agg = jax.ops.segment_sum(proj[src] * attn[:, :, None], tgt, num_segments=n)
            h_local = jax.nn.elu((agg + x.reshape(n, NH, FOUT)).reshape(n, NH * FOUT) + gat_b)
            h_local = _layer_norm(h_local, ln_local_g, ln_local_b)
            deg = jax.ops.segment_sum(jnp.ones((src.shape[0],), x.dtype), src, num_segments=n)
            perm = jnp.argsort(deg + deg_noise, stable=True)
            inv = jnp.argsort(perm)
            y = _mamba(x[perm], in_proj_w, conv_w, conv_b, x_proj_w, dt_proj_w, dt_proj_b, A_log, D_param, out_proj_w)
            h_attn = _layer_norm(x + y[inv], ln_global_g, ln_global_b)
            gate = jax.nn.sigmoid(h_local @ wl.T + h_attn @ wg.T)
            h = gate * h_local + (1.0 - gate) * h_attn
            ff = jax.nn.relu(h @ ff1_w.T + ff1_b) @ ff2_w.T + ff2_b
            return _layer_norm(h + ff, ln2_g, ln2_b)
        return _forward(x, edge_index, deg_noise, gat_w, gat_a_src, gat_a_tgt, gat_b, ln_local_g, ln_local_b, ln_global_g, ln_global_b, ln2_g, ln2_b, in_proj_w, conv_w, conv_b, x_proj_w, dt_proj_w, dt_proj_b, A_log, D_param, out_proj_w, wl, wg, ff1_w, ff1_b, ff2_w, ff2_b)

    def _L1_gnn_ref(x, edge_index, W, b, gamma, beta):
        import jax, jax.numpy as jnp
        import numpy as np
        N_NODES = 6250
        N_EDGES = 100000
        IN_DIM = 256
        OUT_DIM = 256
        BN_EPS = 1e-05
        N = x.shape[0]
        loops = jnp.arange(N, dtype=edge_index.dtype)
        src = jnp.concatenate([edge_index[0], loops])
        dst = jnp.concatenate([edge_index[1], loops])
        ones = jnp.ones(src.shape[0], dtype=x.dtype)
        deg = jax.ops.segment_sum(ones, dst, num_segments=N)
        dinv = jnp.where(deg > 0, jax.lax.rsqrt(deg), jnp.zeros_like(deg))
        norm = dinv[src] * dinv[dst]
        h = x @ W
        msg = h[src] * norm[:, None]
        out = jax.ops.segment_sum(msg, dst, num_segments=N) + b
        mean = jnp.mean(out, axis=0)
        var = jnp.mean(jnp.square(out - mean), axis=0)
        out = (out - mean) * jax.lax.rsqrt(var + BN_EPS) * gamma + beta
        return jax.nn.relu(out)
    edge_index = jnp.stack([src, dst])
    x = _layernorm(x + _L0_gnn_ref(x, edge_index, edge_weight, node_vec, L0_gnn_gat_w, L0_gnn_gat_a_src, L0_gnn_gat_a_tgt, L0_gnn_gat_b, L0_gnn_ln_local_g, L0_gnn_ln_local_b, L0_gnn_ln_global_g, L0_gnn_ln_global_b, L0_gnn_ln2_g, L0_gnn_ln2_b, L0_gnn_in_proj_w, L0_gnn_conv_w, L0_gnn_conv_b, L0_gnn_x_proj_w, L0_gnn_dt_proj_w, L0_gnn_dt_proj_b, L0_gnn_A_log, L0_gnn_D_param, L0_gnn_out_proj_w, L0_gnn_wl, L0_gnn_wg, L0_gnn_ff1_w, L0_gnn_ff1_b, L0_gnn_ff2_w, L0_gnn_ff2_b), axis=-1)
    x = _layernorm(x + _L1_gnn_ref(x, edge_index, L1_gnn_W, L1_gnn_b, L1_gnn_gamma, L1_gnn_beta), axis=-1)
    return x

_drawn_inputs = setup_inputs


def setup_inputs(seed=0):
    import zlib

    import numpy as np

    out = dict(_drawn_inputs(seed))
    spreads = {'L0_gnn_gat_b': (0.0, 0.1),
     'L0_gnn_ln_local_g': (1.0, 0.2),
     'L0_gnn_ln_local_b': (0.0, 0.286),
     'L0_gnn_ln_global_g': (1.0, 0.2),
     'L0_gnn_ln_global_b': (0.0, 0.281),
     'L0_gnn_ln2_g': (1.0, 0.2),
     'L0_gnn_ln2_b': (0.0, 0.1),
     'L0_gnn_conv_b': (0.0, 0.8),
     'L0_gnn_D_param': (1.0, 0.6),
     'L0_gnn_ff1_b': (0.0, 0.1),
     'L0_gnn_ff2_b': (0.0, 0.1),
     'L1_gnn_b': (0.0, 0.8),
     'L1_gnn_gamma': (1.0, 0.2),
     'L1_gnn_beta': (0.0, 0.1)}
    factors = {'node_vec': 3.389,
     'L0_gnn_gat_a_src': 4.017,
     'L0_gnn_gat_a_tgt': 8.0,
     'L0_gnn_in_proj_w': 2.78,
     'L0_gnn_conv_w': 3.023,
     'L0_gnn_x_proj_w': 8.0,
     'L0_gnn_dt_proj_w': 8.0,
     'L0_gnn_dt_proj_b': 8.0,
     'L0_gnn_A_log': 8.0,
     'L0_gnn_out_proj_w': 2.787}
    for name, (base, spread) in spreads.items():
        noise = np.random.default_rng([zlib.crc32(name.encode()), seed]).standard_normal(out[name].shape)
        drawn = base * np.exp(spread * noise) if base else spread * noise
        out[name] = jnp.asarray(drawn.astype(out[name].dtype))
    for name, factor in factors.items():
        out[name] = (out[name] * factor).astype(out[name].dtype)
    return out
```

```python
from contextlib import ExitStack

import concourse.bass as bass
from concourse import mybir

F32 = mybir.dt.float32
BF16 = mybir.dt.bfloat16
I32 = mybir.dt.int32
ALU = mybir.AluOpType
ACT = mybir.ActivationFunctionType
AX = mybir.AxisListType

N, E, D = 6250, 200000, 256
HEADS, HD = 4, 64
TP = 125
TILES = N // TP
KB = 8
EDGES_SB = KB * TP
NSB = E // EDGES_SB
W = 48
NA = N + W + 6
ROW = D + HEADS
DSTATE, DCONV, DTR = 16, 4, 16
CH = 500
CT = CH // TP
NCH = -(-N // CH)
NP = NCH * CH
HI, LO = 98, 64
NHIST = HI * LO
SPLITS = 3
EPS = 1e-5
NEG = -3.0e38


class Link:

    def __init__(self, eng, sem):
        self.eng, self.sem, self.n = eng, sem, 0

    def __call__(self, ins):
        self.n += 1
        ins.then_inc(self.sem, 1)
        self.eng.wait_ge(self.sem, self.n)

    def restart(self):
        self.eng.sem_clear(self.sem)
        self.n = 0


class Parts:

    def __init__(self, nc, stack, prefix):
        self.nc, self.stack, self.prefix, self.sems = nc, stack, prefix, []

    def sb(self, name, shape, dt=F32):
        return self.stack.enter_context(self.nc.sbuf_tensor(self.prefix + name, shape, dt))

    def ps(self, name, shape, dt=F32):
        return self.stack.enter_context(self.nc.psum_tensor(self.prefix + name, shape, dt))

    def sem(self, name):
        self.sems.append(self.nc.alloc_semaphore(self.prefix + name))
        return self.sems[-1]

    def close(self):
        self.nc.clear_and_free_semaphores(self.sems)
        self.nc.all_engine_barrier()


def rsqrt(v, link, out, value, half, square):
    MAGIC, STEPS = float(0x5F3759DF), 3
    link(v.tensor_scalar(out.bitcast(I32), value.bitcast(I32), 1, None, ALU.logical_shift_right))
    v.tensor_scalar(half, value, -0.5, None, ALU.mult)
    link(v.tensor_scalar(out.bitcast(I32), out.bitcast(I32), -1.0, MAGIC, ALU.mult, ALU.add))
    for _ in range(STEPS):
        link(v.tensor_tensor(square, out, out, ALU.mult))
        link(v.tensor_tensor(square, square, half, ALU.mult))
        link(v.scalar_tensor_tensor(out, square, 1.5, out, ALU.add, ALU.mult))


def tables_block(nc, A, S, K):
    G = 5
    GN = G * TP
    HC = 16
    HSTEPS = E // TP // HC
    with ExitStack() as stack:
        M = Parts(nc, stack, "tab_")
        gatw = M.sb("gatw", [128, 2, D])
        ablk = M.sb("ablk", [128, 2, 2 * HEADS])
        waug = M.sb("waug", [128, 2, D + 2 * HEADS])
        xt = M.sb("xt", [128, 2, 2, GN])
        rows = M.sb("rows", [TP, 2, G, D + 2 * HEADS])
        split = M.sb("split", [TP, 2, G, SPLITS, HEADS], BF16)
        rest = M.sb("rest", [TP, G, HEADS])
        smax5 = M.sb("smax5", [TP, G, HEADS])
        smax1 = M.sb("smax1", [TP, HEADS])
        smaxall = M.sb("smaxall", [TP, TP * HEADS])
        dst2 = M.sb("dst2", [NSB // 2, 2, EDGES_SB], I32)
        lowhigh = M.sb("lowhigh", [NSB // 2, 2, 2])
        span = M.sb("span", [NSB // 2, 2])
        spanrow = M.sb("spanrow", [1, NSB])
        widest = M.sb("widest", [1, 1])
        reach = M.sb("reach", [1, 132])
        nrounds = M.sb("nrounds", [1, 1])
        srcs = M.sb("srcs", [TP, E // TP], I32)
        hi = M.sb("hi", [TP, E // TP], I32)
        lo = M.sb("lo", [TP, E // TP], I32)
        ohhi = M.sb("ohhi", [TP, 2, HC, HI], BF16)
        ohlo = M.sb("ohlo", [TP, 2, HC, LO], BF16)
        hist = M.sb("hist", [HI, LO])
        pad = M.sb("pad", [NA - N, SPLITS * HEADS], BF16)
        psw = M.ps("psw", [128, 2, 2 * HEADS])
        psr = [M.ps(f"psr{j}", [TP, D + 2 * HEADS]) for j in range(G)]
        psh = M.ps("psh", [HI, LO])

        const_in, weights_in, dst_in, src_in = (M.sem(n) for n in ("const_in", "weights_in", "dst_in", "src_in"))
        xt_in = [M.sem("xt_in0"), M.sem("xt_in1")]
        vw_done, vw_copied = M.sem("vw_done"), M.sem("vw_copied")
        proj_done, proj_copied, rows_maxed = M.sem("proj_done"), M.sem("proj_copied"), M.sem("rows_maxed")
        rows_out = [M.sem("rows_out0"), M.sem("rows_out1")]
        scores_out = [M.sem("scores_out0"), M.sem("scores_out1")]
        smax_ready, smax_out, smax_in = M.sem("smax_ready"), M.sem("smax_out"), M.sem("smax_in")
        span_ready, span_out, span_in, base_in = (M.sem(n) for n in ("span_ready", "span_out", "span_in", "base_in"))
        oh_ready, oh_used, hist_done, hist_ready, hist_out = (M.sem(n) for n in ("oh_ready", "oh_used", "hist_done", "hist_ready", "hist_out"))
        link_v, pad_ready, pad_out = M.sem("link_v"), M.sem("pad_ready"), M.sem("pad_out")

        PAIRS = TILES // G // 2

        with nc.Block() as block:
            @block.sync
            def _(sp):
                for t, a in ((K.ident, A.ident), (K.iota, A.iota), (K.pidx, A.pidx), (K.steps, A.steps)):
                    sp.dma_start(t[:, :], a).then_inc(const_in, 16)
                sp.dma_start(gatw[:, :, :], A.gat_w.rearrange("(k p) n -> p k n", p=128)).then_inc(weights_in, 16)
                sp.dma_start(ablk[:, :, :], A.a_blk.rearrange("(k p) n -> p k n", p=128)).then_inc(weights_in, 16)
                sp.dma_start(waug[:, :, 0:D], A.gat_wT.rearrange("(k p) n -> p k n", p=128)).then_inc(weights_in, 16)
                sp.dma_start(srcs[:, :], A.src.rearrange("(p c) -> p c", p=TP)).then_inc(src_in, 16)
                sp.dma_start(dst2[:, :, :], A.dst.rearrange("(p j e) -> p j e", j=2, e=EDGES_SB)).then_inc(dst_in, 16)
                xT = A.xT.rearrange("(k p) n -> p k n", p=128)
                rows_dram = S.proj.rearrange("(g j p) c -> g p j c", j=G, p=TP)
                scores_dram = S.stgt[0:N, :].rearrange("(g j p) c -> g p j c", j=G, p=TP)
                for par in range(2):
                    sp.dma_start(xt[:, par], xT[:, :, par * GN:(par + 1) * GN]).then_inc(xt_in[par], 16)

                def step(i, last):
                    for par in range(2):
                        sp.wait_ge(proj_copied, i * (2 * G) + (par + 1) * G)
                        sp.dma_start(rows_dram[bass.ds(i * 2 + par, 1)].rearrange("a p j c -> (a p) j c"),
                                     rows[:, par, :, 0:ROW]).then_inc(rows_out[par], 16)
                        sp.wait_ge(rows_maxed, i * 2 + par + 1)
                        sp.dma_start(scores_dram[bass.ds(i * 2 + par, 1)].rearrange("a p j c -> (a p) j c"),
                                     split[:, par].rearrange("p j s h -> p j (s h)")).then_inc(scores_out[par], 16)
                        if not last:
                            sp.dma_start(xt[:, par], xT[:, :, bass.ds((i * 2 + par + 2) * GN, GN)]).then_inc(xt_in[par], 16)

                with sp.Fori(0, PAIRS - 1) as i:
                    step(i, False)
                step(PAIRS - 1, True)
                sp.wait_ge(pad_ready, 1)
                sp.dma_start(S.stgt[N:NA, :], pad[:, :]).then_inc(pad_out, 16)
                sp.wait_ge(pad_out, 16)
                sp.wait_ge(smax_ready, 1)
                sp.dma_start(S.smax.rearrange("(p h) -> p h", h=HEADS), smax1[:, :]).then_inc(smax_out, 16)
                sp.wait_ge(smax_out, 16)
                sp.dma_start(smaxall[:, :], S.smax.partition_broadcast(TP)).then_inc(smax_in, 16)
                sp.wait_ge(span_ready, 1)
                sp.dma_start(S.low.rearrange("(p j) -> p j", j=2), lowhigh[:, 0]).then_inc(span_out, 16)
                sp.dma_start(S.span.rearrange("(p j) -> p j", j=2), span[:, :]).then_inc(span_out, 16)
                sp.wait_ge(span_out, 32)
                sp.dma_start(K.low[:, :], S.low.partition_broadcast(128)).then_inc(base_in, 16)
                sp.dma_start(spanrow[:, :], S.span.rearrange("(a n) -> a n", a=1)).then_inc(span_in, 16)
                sp.wait_ge(hist_ready, 1)
                sp.dma_start(S.deg.rearrange("(h l) -> h l", l=LO), hist[:, :]).then_inc(hist_out, 16)
                sp.wait_ge(hist_out, 16)
                sp.wait_ge(base_in, 16)
                for par in range(2):
                    sp.wait_ge(rows_out[par], 16 * PAIRS)
                    sp.wait_ge(scores_out[par], 16 * PAIRS)

            @block.tensor
            def _(pe):
                pe.wait_ge(weights_in, 48)
                for half in range(2):
                    for k in range(2):
                        last = nc.tensor.matmul(psw[:, half], gatw[:, k, half * 128:(half + 1) * 128], ablk[:, k],
                                                start=(k == 0), stop=(k == 1))
                last.then_inc(vw_done, 1)
                pe.wait_ge(vw_copied, 1)

                def step(i, first):
                    for par in range(2):
                        pe.wait_ge(xt_in[par], (i + 1) * 16)
                        for j in range(G):
                            if not (first and par == 0):
                                pe.wait_ge(proj_copied, i * (2 * G) + (par - 1) * G + j + 1)
                            for k in range(2):
                                last = nc.tensor.matmul(psr[j][:, :], xt[:, par, k, j * TP:(j + 1) * TP], waug[:, k],
                                                        start=(k == 0), stop=(k == 1))
                            last.then_inc(proj_done, 1)

                step(0, True)
                with pe.Fori(1, PAIRS) as i:
                    step(i, False)

                def hist_step(i, par, first, final):
                    pe.wait_ge(oh_ready, i * 2 + par + 1)
                    for c in range(HC):
                        last = nc.tensor.matmul(psh[:, :], ohhi[:, par, c], ohlo[:, par, c],
                                                start=(first and c == 0), stop=(final and c == HC - 1))
                    last.then_inc(oh_used, 1)

                for par in range(2):
                    hist_step(0, par, par == 0, False)
                with pe.Fori(1, HSTEPS // 2 - 1) as i:
                    for par in range(2):
                        hist_step(i, par, False, False)
                for par in range(2):
                    hist_step(HSTEPS // 2 - 1, par, False, par == 1)

            @block.scalar
            def _(act):
                act.wait_ge(vw_done, 1)
                act.wait_ge(weights_in, 48)
                act.copy(waug[:, :, D:], psw[:, :, :]).then_inc(vw_copied, 1)

                def step(i, first):
                    for par in range(2):
                        if not first:
                            act.wait_ge(rows_out[par], i * 16)
                            act.wait_ge(scores_out[par], i * 16)
                            act.wait_ge(rows_maxed, i * 2 + par - 1)
                        for j in range(G):
                            act.wait_ge(proj_done, i * (2 * G) + par * G + j + 1)
                            act.copy(rows[:, par, j], psr[j][:, :]).then_inc(proj_copied, 1)

                step(0, True)
                with act.Fori(1, PAIRS) as i:
                    step(i, False)
                act.wait_ge(oh_used, HSTEPS)
                act.copy(hist[:, :], psh[:, :]).then_inc(hist_ready, 1)

            @block.vector
            def _(v):
                link = Link(v, link_v)
                v.wait_ge(const_in, 64)
                v.wait_ge(dst_in, 16)
                v.tensor_reduce(lowhigh[:, 0], dst2[:, :, :], axis=AX.X, op=ALU.min)
                link(v.tensor_reduce(lowhigh[:, 1], dst2[:, :, :], axis=AX.X, op=ALU.max))
                v.tensor_tensor(span[:, :], lowhigh[:, 1], lowhigh[:, 0], ALU.subtract).then_inc(span_ready, 1)
                v.wait_ge(src_in, 16)
                v.tensor_scalar(hi[:, :], srcs[:, :], 6, None, ALU.logical_shift_right)
                link(v.tensor_scalar(lo[:, :], srcs[:, :], LO - 1, None, ALU.bitwise_and))
                link(v.memset(smax5[:, :, :], NEG))

                def row_max(i, first):
                    link.restart()
                    for par in range(2):
                        v.wait_ge(proj_copied, i * (2 * G) + (par + 1) * G)
                        if not first:
                            v.wait_ge(scores_out[par], i * 16)
                        left = rows[:, par, :, ROW:]
                        for c in range(SPLITS):
                            link(v.tensor_copy(split[:, par, :, c], left))
                            if c < SPLITS - 1:
                                link(v.tensor_tensor(rest[:, :, :], left, split[:, par, :, c], ALU.subtract))
                                left = rest[:, :, :]
                        v.tensor_tensor(smax5[:, :, :], smax5[:, :, :], rows[:, par, :, D:D + HEADS], ALU.max).then_inc(rows_maxed, 1)
                        v.wait_ge(rows_maxed, i * 2 + par + 1)

                v.memset(pad[:, :], 0.0).then_inc(pad_ready, 1)
                row_max(0, True)
                with v.Fori(1, PAIRS) as i:
                    row_max(i, False)
                link.restart()
                v.tensor_reduce(smax1[:, :], smax5[:, :, :].rearrange("p g h -> p h g"), axis=AX.X, op=ALU.max).then_inc(smax_ready, 1)

                def hist_step(i, par, first):
                    if not first:
                        v.wait_ge(oh_used, i * 2 + par - 1)
                    cols = bass.ds((i * 2 + par) * HC, HC)
                    v.tensor_tensor(ohhi[:, par], hi[:, cols].unsqueeze(2).to_broadcast([TP, HC, HI]),
                                    K.iota[0:TP, 0:HI].unsqueeze(1).to_broadcast([TP, HC, HI]), ALU.is_equal)
                    v.tensor_tensor(ohlo[:, par], lo[:, cols].unsqueeze(2).to_broadcast([TP, HC, LO]),
                                    K.iota[0:TP, 0:LO].unsqueeze(1).to_broadcast([TP, HC, LO]), ALU.is_equal).then_inc(oh_ready, 1)

                for par in range(2):
                    hist_step(0, par, True)
                with v.Fori(1, HSTEPS // 2) as i:
                    for par in range(2):
                        hist_step(i, par, False)
                v.wait_ge(smax_in, 16)
                v.tensor_reduce(K.smax[:, :], smaxall[:, :].rearrange("p (q h) -> p h q", h=HEADS), axis=AX.X, op=ALU.max)
                v.wait_ge(span_in, 16)
                link(v.tensor_reduce(widest[:, :], spanrow[:, :], axis=AX.X, op=ALU.max))
                link(v.tensor_scalar(reach[:, :], K.steps[:, :], widest[:, 0:1], None, ALU.is_le))
                link(v.tensor_reduce(nrounds[:, :], reach[:, :], axis=AX.X, op=ALU.add))
                link(v.tensor_copy(K.rounds[:, :], nrounds[:, :]))
        M.close()


def ranks_block(nc, A, S, K):
    PADT = (NP - N) // TP
    with ExitStack() as stack:
        M = Parts(nc, stack, "rank_")
        total = M.sb("total", [TP, TILES])
        xrows = M.sb("xrows", [TP, TILES, D])
        zrows = M.sb("zrows", [TP, PADT, D])
        x_in, z_ready, z_out, rank_ready, scattered, link_v = (
            M.sem(n) for n in ("x_in", "z_ready", "z_out", "rank_ready", "scattered", "link_v"))

        with nc.Block() as block:
            @block.sync
            def _(sp):
                sp.dma_start(xrows[:, :, :], A.x.rearrange("(t p) c -> p t c", p=TP)).then_inc(x_in, 16)
                sp.wait_ge(z_ready, 1)
                sp.dma_start(S.xs[N:NP, :].rearrange("(t p) c -> p t c", p=TP), zrows[:, :, :]).then_inc(z_out, 16)
                sp.wait_ge(z_out, 16)

            @block.gpsimd
            def _(pool):
                pool.memset(zrows[:, :, :], 0.0).then_inc(z_ready, 1)
                pool.wait_ge(x_in, 16)
                pool.wait_ge(rank_ready, 1)
                for t in range(TILES):
                    pool.indirect_dma_start(S.xs, bass.IndirectOffsetOnAxis(ap=K.rank[:, t:t + 1], axis=0),
                                            xrows[:, t, :], None).then_inc(scattered, 16)
                pool.wait_ge(scattered, 16 * TILES)

            @block.vector
            def _(v):
                link = Link(v, link_v)
                link(v.tensor_reduce(total[:, :], K.smaller[:, :].rearrange("p (t u) -> p t u", u=4), axis=AX.X, op=ALU.add))
                v.tensor_tensor(K.rank[:, :], total[:, :], K.ties[:, :], ALU.add).then_inc(rank_ready, 1)
        M.close()


def mamba_block(nc, A, S, K):
    ODD = [1.0 / 13, 1.0 / 11, 1.0 / 9, 1.0 / 7, 1.0 / 5, 1.0 / 3]
    with ExitStack() as stack:
        M = Parts(nc, stack, "mam_")
        in_w = M.sb("in_w", [128, 2, 2 * D])
        x_w = M.sb("x_w", [128, 2, DTR + 2 * DSTATE])
        dt_w = M.sb("dt_w", [DTR, D])
        out_w = M.sb("out_w", [128, 2, D])
        conv_w = M.sb("conv_w", [128, 2, DCONV])
        conv_b = M.sb("conv_b", [128, 2, 1])
        dt_b = M.sb("dt_b", [128, 2, 1])
        d_par = M.sb("d_par", [128, 2, 1])
        a_log = M.sb("a_log", [128, 2, DSTATE])
        a_neg = M.sb("a_neg", [128, 2, DSTATE])
        state = M.sb("state", [128, 2, DSTATE])
        xr = M.sb("xr", [TP, CT, D])
        xT = M.sb("xT", [128, 2, CH])
        xin = M.sb("xin", [128, 2, DCONV - 1 + CH])
        z = M.sb("z", [128, 2, CH])
        zexp = M.sb("zexp", [128, 2, CH])
        zs = M.sb("zs", [128, 2, CH])
        conv = M.sb("conv", [128, 2, CH])
        cexp = M.sb("cexp", [128, 2, CH])
        xc = M.sb("xc", [128, 2, CH])
        dbc = M.sb("dbc", [DTR + 2 * DSTATE, CH])
        mag = M.sb("mag", [128, 2, CH])
        mag2 = M.sb("mag2", [128, 2, CH])
        pos = M.sb("pos", [128, 2, CH])
        ratio = M.sb("ratio", [128, 2, CH])
        ratio2 = M.sb("ratio2", [128, 2, CH])
        series = M.sb("series", [128, 2, CH])
        dt = M.sb("dt", [128, 2, CH])
        dtx = M.sb("dtx", [128, 2, CH])
        decay = M.sb("decay", [128, 2, 2, CH])
        bx = M.sb("bx", [128, 2, CH])
        h = M.sb("h", [128, 2, CH])
        hc = M.sb("hc", [128, 2, 2, CH])
        y = M.sb("y", [128, 2, CH])
        yrows = M.sb("yrows", [TP, CT, D])
        psA = M.ps("psA", [128, 2, 512])
        psB = M.ps("psB", [128, 2, 512])
        psC = M.ps("psC", [128, 2, 512])
        psY = M.ps("psY", [128, 2, 512])

        params_in, x_in, x_turned, xT_ready = (M.sem(n) for n in ("params_in", "x_in", "x_turned", "xT_ready"))
        main_done, main_copied, z_done, z_copied = (M.sem(n) for n in ("main_done", "main_copied", "z_done", "z_copied"))
        conv_ready, cexp_ready, xc_ready = (M.sem(n) for n in ("conv_ready", "cexp_ready", "xc_ready"))
        dbc_done, dbc_ready, dt_done, mag_ready = (M.sem(n) for n in ("dbc_done", "dbc_ready", "dt_done", "mag_ready"))
        ratio_ready, ratio2_ready, dt_ready = (M.sem(n) for n in ("ratio_ready", "ratio2_ready", "dt_ready"))
        decay_ready, b_done, c_done, bx_ready, scanned, hc_ready, y_summed = (M.sem(n) for n in (
            "decay_ready", "b_done", "c_done", "bx_ready", "scanned", "hc_ready", "y_summed"))
        y_ready, out_done, out_copied, stored = (M.sem(n) for n in ("y_ready", "out_done", "out_copied", "stored"))
        a_ready, history, init_ready, link_v, link_a = (M.sem(n) for n in ("a_ready", "history", "init_ready", "link_v", "link_a"))

        with nc.Block() as block:
            @block.sync
            def _(sp):
                for t, a in ((in_w, A.in_wT), (x_w, A.x_wT), (out_w, A.out_wT)):
                    sp.dma_start(t[:, :, :], a.rearrange("(k p) n -> p k n", p=128)).then_inc(params_in, 16)
                sp.dma_start(dt_w[:, :], A.dt_wT).then_inc(params_in, 16)
                for t, a in ((conv_w, A.conv_w), (conv_b, A.conv_b), (dt_b, A.dt_b), (d_par, A.d_param), (a_log, A.a_log)):
                    sp.dma_start(t[:, :, :], a).then_inc(params_in, 16)
                xs = S.xs.rearrange("(c j p) f -> c p j f", j=CT, p=TP)
                ys = S.ys.rearrange("(c j p) f -> c p j f", j=CT, p=TP)
                sp.dma_start(xr[:, :, :], xs[0]).then_inc(x_in, 16)

                def step(c, last):
                    if not last:
                        sp.wait_ge(x_turned, c + 1)
                        sp.dma_start(xr[:, :, :], xs[bass.ds(c + 1, 1)].rearrange("a p j f -> (a p) j f")).then_inc(x_in, 16)
                    sp.wait_ge(out_copied, (c + 1) * CT)
                    sp.dma_start(ys[bass.ds(c, 1)].rearrange("a p j f -> (a p) j f"), yrows[:, :, :]).then_inc(stored, 16)

                with sp.Fori(0, NCH - 1) as c:
                    step(c, False)
                step(NCH - 1, True)
                sp.wait_ge(stored, 16 * NCH)

            @block.tensor
            def _(pe):
                pe.wait_ge(params_in, 144)

                def step(c, first):
                    pe.wait_ge(x_in, (c + 1) * 16)
                    if not first:
                        pe.wait_ge(out_copied, c * CT)
                    for j in range(CT):
                        for k in range(2):
                            last = nc.tensor.transpose(psA[:, k, j * TP:(j + 1) * TP], xr[:, j, k * 128:(k + 1) * 128],
                                                       K.ident[0:TP, 0:TP])
                    last.then_inc(x_turned, 1)
                    pe.wait_ge(xT_ready, c + 1)
                    for part, done in ((0, main_done), (1, z_done)):
                        if part:
                            pe.wait_ge(main_copied, c + 1)
                        for m in range(2):
                            for k in range(2):
                                last = nc.tensor.matmul(psA[:, m, 0:CH], in_w[:, k, (2 * part + m) * 128:(2 * part + m + 1) * 128],
                                                        xT[:, k], start=(k == 0), stop=(k == 1))
                        last.then_inc(done, 1)
                    pe.wait_ge(z_copied, c + 1)
                    pe.wait_ge(xc_ready, c + 1)
                    for k in range(2):
                        last = nc.tensor.matmul(psA[0:DTR + 2 * DSTATE, 0, 0:CH], x_w[:, k], xc[:, k], start=(k == 0), stop=(k == 1))
                    last.then_inc(dbc_done, 1)
                    pe.wait_ge(dbc_ready, c + 1)
                    for m in range(2):
                        last = nc.tensor.matmul(psA[:, m, 0:CH], dt_w[:, m * 128:(m + 1) * 128], dbc[0:DTR, :], start=True, stop=True)
                    last.then_inc(dt_done, 1)

                    def sum_state(n):
                        pe.wait_ge(hc_ready, c * DSTATE + n + 1)
                        for half in range(2):
                            last = nc.tensor.matmul(psY[:, half, 0:CH], K.ident[:, :], hc[:, n % 2, half],
                                                    start=(n == 0), stop=(n == DSTATE - 1), skip_group_check=True)
                        last.then_inc(y_summed, 1)

                    for n in range(DSTATE):
                        if n >= 2:
                            pe.wait_ge(bx_ready, c * DSTATE + n - 1)
                        nc.tensor.matmul(psB[:, n % 2, 0:CH], K.ident[0:48, DTR + n:DTR + n + 1].to_broadcast([48, 128]),
                                         dbc[:, :], start=True, stop=True).then_inc(b_done, 1)
                        if n >= 2:
                            pe.wait_ge(hc_ready, c * DSTATE + n - 1)
                        nc.tensor.matmul(psC[:, n % 2, 0:CH], K.ident[0:48, DTR + DSTATE + n:DTR + DSTATE + n + 1].to_broadcast([48, 128]),
                                         dbc[:, :], start=True, stop=True).then_inc(c_done, 1)
                        if n:
                            sum_state(n - 1)
                    sum_state(DSTATE - 1)
                    pe.wait_ge(y_ready, c + 1)
                    for j in range(CT):
                        if j >= 2:
                            pe.wait_ge(out_copied, c * CT + j - 1)
                        for k in range(2):
                            last = nc.tensor.matmul(psA[0:TP, j % 2, 0:D], y[:, k, j * TP:(j + 1) * TP], out_w[:, k],
                                                    start=(k == 0), stop=(k == 1))
                        last.then_inc(out_done, 1)

                step(0, True)
                with pe.Fori(1, NCH) as c:
                    step(c, False)

            @block.scalar
            def _(act):
                link = Link(act, link_a)
                act.wait_ge(params_in, 144)
                act.activation(a_neg[:, :, :], a_log[:, :, :], ACT.Exp).then_inc(a_ready, 1)
                act.wait_ge(init_ready, 1)

                def step(c, first):
                    link.restart()
                    act.wait_ge(x_turned, c + 1)
                    act.copy(xT[:, :, :], psA[:, :, 0:CH]).then_inc(xT_ready, 1)
                    if not first:
                        act.wait_ge(conv_ready, c)
                        link(act.copy(xin[:, :, 0:DCONV - 1], xin[:, :, CH:]))
                    act.wait_ge(main_done, c + 1)
                    act.copy(xin[:, :, DCONV - 1:], psA[:, :, 0:CH]).then_inc(main_copied, 1)
                    act.wait_ge(z_done, c + 1)
                    act.copy(z[:, :, :], psA[:, :, 0:CH])
                    link(act.activation(zexp[:, :, :], psA[:, :, 0:CH], ACT.Exp, scale=-1.0))
                    act.activation(zexp[:, :, :], zexp[:, :, :], ACT.Copy, bias=1.0).then_inc(z_copied, 1)
                    act.wait_ge(conv_ready, c + 1)
                    link(act.activation(cexp[:, :, :], conv[:, :, :], ACT.Exp, scale=-1.0))
                    act.activation(cexp[:, :, :], cexp[:, :, :], ACT.Copy, bias=1.0).then_inc(cexp_ready, 1)
                    act.wait_ge(dbc_done, c + 1)
                    act.copy(dbc[:, :], psA[0:DTR + 2 * DSTATE, 0, 0:CH]).then_inc(dbc_ready, 1)
                    act.wait_ge(dt_done, c + 1)
                    for half in range(2):
                        act.activation(mag[:, half], psA[:, half, 0:CH], ACT.Abs, bias=dt_b[:, half])
                        link(act.activation(pos[:, half], psA[:, half, 0:CH], ACT.Relu, bias=dt_b[:, half]))
                    link(act.activation(mag[:, :, :], mag[:, :, :], ACT.Exp, scale=-1.0))
                    act.activation(mag2[:, :, :], mag[:, :, :], ACT.Copy, bias=2.0).then_inc(mag_ready, 1)
                    act.wait_ge(ratio_ready, c + 1)
                    link(act.activation(ratio2[:, :, :], ratio[:, :, :], ACT.Square))
                    act.activation(series[:, :, :], ratio2[:, :, :], ACT.Copy, scale=ODD[0]).then_inc(ratio2_ready, 1)
                    act.wait_ge(dt_ready, c + 1)
                    for n in range(DSTATE):
                        if n >= 2:
                            act.wait_ge(scanned, c * DSTATE + n - 1)
                        for half in range(2):
                            last = act.activation(decay[:, n % 2, half], dt[:, half], ACT.Exp, scale=a_neg[:, half, n:n + 1])
                        last.then_inc(decay_ready, 1)
                    if not first:
                        act.wait_ge(stored, c * 16)
                    for j in range(CT):
                        act.wait_ge(out_done, c * CT + j + 1)
                        act.copy(yrows[:, j], psA[0:TP, j % 2, 0:D]).then_inc(out_copied, 1)

                step(0, True)
                with act.Fori(1, NCH) as c:
                    step(c, False)

            @block.vector
            def _(v):
                link = Link(v, link_v)
                v.memset(state[:, :, :], 0.0)
                v.memset(xin[:, :, 0:DCONV - 1], 0.0)
                v.wait_ge(a_ready, 1)
                v.tensor_scalar(a_neg[:, :, :], a_neg[:, :, :], -1.0, None, ALU.mult).then_inc(init_ready, 1)
                v.wait_ge(init_ready, 1)

                def step(c):
                    link.restart()
                    v.wait_ge(main_copied, c + 1)
                    for half in range(2):
                        last = v.tensor_scalar(conv[:, half], xin[:, half, 3:3 + CH], conv_w[:, half, 3:4], conv_b[:, half], ALU.mult, ALU.add)
                    link(last)
                    for k in range(DCONV - 1):
                        for half in range(2):
                            last = v.scalar_tensor_tensor(conv[:, half], xin[:, half, k:k + CH], conv_w[:, half, k:k + 1], conv[:, half],
                                                          ALU.mult, ALU.add)
                        if k < DCONV - 2:
                            link(last)
                    last.then_inc(conv_ready, 1)
                    v.wait_ge(z_copied, c + 1)
                    link(v.reciprocal(zexp[:, :, :], zexp[:, :, :]))
                    v.tensor_tensor(zs[:, :, :], z[:, :, :], zexp[:, :, :], ALU.mult)
                    v.wait_ge(cexp_ready, c + 1)
                    link(v.reciprocal(cexp[:, :, :], cexp[:, :, :]))
                    v.tensor_tensor(xc[:, :, :], conv[:, :, :], cexp[:, :, :], ALU.mult).then_inc(xc_ready, 1)
                    v.wait_ge(mag_ready, c + 1)
                    link(v.reciprocal(mag2[:, :, :], mag2[:, :, :]))
                    v.tensor_tensor(ratio[:, :, :], mag[:, :, :], mag2[:, :, :], ALU.mult).then_inc(ratio_ready, 1)
                    v.wait_ge(ratio2_ready, c + 1)
                    for coeff in ODD[1:]:
                        link(v.scalar_tensor_tensor(series[:, :, :], series[:, :, :], coeff, ratio2[:, :, :], ALU.add, ALU.mult))
                    link(v.scalar_tensor_tensor(series[:, :, :], series[:, :, :], 1.0, ratio[:, :, :], ALU.add, ALU.mult))
                    v.scalar_tensor_tensor(dt[:, :, :], series[:, :, :], 2.0, pos[:, :, :], ALU.mult, ALU.add).then_inc(dt_ready, 1)
                    v.wait_ge(dt_ready, c + 1)
                    link(v.tensor_tensor(dtx[:, :, :], dt[:, :, :], xc[:, :, :], ALU.mult))
                    for n in range(DSTATE):
                        at = c * DSTATE + n + 1
                        v.wait_ge(b_done, at)
                        v.tensor_tensor(bx[:, :, :], dtx[:, :, :], psB[:, n % 2, 0:CH].unsqueeze(1).to_broadcast([128, 2, CH]), ALU.mult
                                        ).then_inc(bx_ready, 1)
                        v.wait_ge(bx_ready, at)
                        v.wait_ge(decay_ready, at)
                        for half in range(2):
                            last = v.tensor_tensor_scan(h[:, half], decay[:, n % 2, half], bx[:, half], state[:, half, n:n + 1], ALU.mult, ALU.add)
                        last.then_inc(scanned, 1)
                        v.wait_ge(scanned, at)
                        v.tensor_copy(state[:, :, n:n + 1], h[:, :, CH - 1:CH])
                        v.wait_ge(c_done, at)
                        if n >= 2:
                            v.wait_ge(y_summed, c * DSTATE + n - 1)
                        v.tensor_tensor(hc[:, n % 2], h[:, :, :], psC[:, n % 2, 0:CH].unsqueeze(1).to_broadcast([128, 2, CH]), ALU.mult
                                        ).then_inc(hc_ready, 1)
                    v.wait_ge(y_summed, (c + 1) * DSTATE)
                    for half in range(2):
                        last = v.scalar_tensor_tensor(y[:, half], xc[:, half], d_par[:, half], psY[:, half, 0:CH], ALU.mult, ALU.add)
                    link(last)
                    v.tensor_tensor(y[:, :, :], y[:, :, :], zs[:, :, :], ALU.mult).then_inc(y_ready, 1)

                with v.Fori(0, NCH) as c:
                    step(c)
        M.close()


def edge_pass(nc, A, S, K, weighted):
    CREDIT = 4
    DONE = lambda n: n + 1 + CREDIT
    QUADS = NSB // 4
    PIECES = [(0, 1562), (1562, 3124), (3124, 4686), (4686, N)]
    assert QUADS == TILES
    table = S.proj if weighted else S.x1d
    width = ROW if weighted else D
    cols = ROW + 1 if weighted else D
    with ExitStack() as stack:
        M = Parts(nc, stack, "gat_" if weighted else "gcn_")
        base = M.sb("base", [128, NSB])
        base_i = M.sb("base_i", [1, NSB], I32)
        src = M.sb("src", [TP, 4, KB], I32)
        dst = M.sb("dst", [TP, 4, KB], I32)
        rows = M.sb("rows", [TP, 4, KB, width])
        rel = M.sb("rel", [TP, 4, KB])
        sel = M.sb("sel", [TP, 4, KB, W])
        part = M.sb("part", [W, 2, cols])
        psA = [M.ps(f"psA{i}", [W, 512]) for i in range(2)]
        psT = [M.ps(f"psT{i}", [128, 512]) for i in range(2)]
        if weighted:
            dstrow = M.sb("dstrow", [W, 2, EDGES_SB], I32)
            tscore = M.sb("tscore", [W, 2, SPLITS * HEADS], BF16)
            selT = M.sb("selT", [W, 2, EDGES_SB], BF16)
            tsum = M.sb("tsum", [TP, KB, HEADS])
            wrows = M.sb("wrows", [TP, 2, KB, cols])
            below = M.sb("below", [TP, KB])
            above = M.sb("above", [TP, KB])
            outside = M.sb("outside", [TP, 4, KB])
            score = M.sb("score", [TP, KB, HEADS])
            bound = M.sb("bound", [TP, KB, HEADS])
            masked = M.sb("masked", [TP, KB, HEADS])
            expo = M.sb("expo", [TP, 2, KB, HEADS])
            emax = M.sb("emax", [TP, KB, HEADS])
            emax1 = M.sb("emax1", [TP, 1])
            emaxall = M.sb("emaxall", [TP, TP])
            degrow = M.sb("degrow", [TILES, TP])
            noise = M.sb("noise", [TILES, TP])
            keyrow = M.sb("keyrow", [TILES, TP])
            keycol = M.sb("keycol", [TP, TILES])
            keys = M.sb("keys", [TP, N])
            tri = M.sb("tri", [TP, TP])
            seen = M.sb("seen", [TP, PIECES[-1][1] - PIECES[-1][0]], BF16)
            lowered = M.sb("lowered", [TP, 2, TP])
            psb = [M.ps(f"psb{i}", [TP, KB, SPLITS, HEADS]) for i in range(2)]

        src_in = [M.sem(f"src_in{i}") for i in range(4)]
        dst_in = [M.sem(f"dst_in{i}") for i in range(4)]
        dstrow_in = [M.sem(f"dstrow_in{i}") for i in range(2)]
        tscore_in = [M.sem(f"tscore_in{i}") for i in range(2)]
        rows_in = [M.sem(f"rows_in{i}") for i in range(4)]
        base_ready, sel_ready, b_done, scored, w_ready, weighed = (
            M.sem(n) for n in ("base_ready", "sel_ready", "b_done", "scored", "w_ready", "weighed"))
        summed, copied, turned, added = (M.sem(n) for n in ("summed", "copied", "turned", "added"))
        emax_ready, emax_out, emax_in = (M.sem(n) for n in ("emax_ready", "emax_out", "emax_in"))
        link_v, ticks, credited = M.sem("link_v"), M.sem("ticks"), M.sem("credited")
        key_parts_in, key_ready, key_out, keys_in, col_done, col_copied = (
            M.sem(n) for n in ("key_parts_in", "key_ready", "key_out", "keys_in", "col_done", "col_copied"))
        rows_used = weighed if weighted else summed

        def in_rounds(eng, before, step, after):
            turns = eng.value_load(K.rounds[0:1, 0:1], min_val=1, max_val=-(-N // W))
            with eng.Fori(0, turns) as r:
                before(r)
                for u in range(4):
                    step(r * QUADS, 0, u)
                with eng.Fori(1, QUADS - 1) as q:
                    for u in range(4):
                        step(r * QUADS + q, q, u)
                for u in range(4):
                    step(r * QUADS + QUADS - 1, QUADS - 1, u)
                after(r)

        def nothing(r):
            pass

        def hold(eng, sem, value):
            eng.wait_ge(sem, value)
            eng.sem_inc(ticks, 1)

        with nc.Block() as block:
            @block.sync
            def _(sp):
                if weighted:
                    sp.dma_start(degrow[:, :], S.deg[0:N].rearrange("(t p) -> t p", p=TP)).then_inc(key_parts_in, 16)
                    sp.dma_start(noise[:, :], A.node_vec.rearrange("(t p) -> t p", p=TP)).then_inc(key_parts_in, 16)
                    sp.dma_start(tri[:, :], A.tri).then_inc(key_parts_in, 16)
                    sp.wait_ge(key_ready, 1)
                    sp.dma_start(S.key.rearrange("(t p) -> t p", p=TP), keyrow[:, :]).then_inc(key_out, 16)
                    sp.wait_ge(key_out, 16)
                sp.wait_ge(credited, 1)

                def before(r):
                    hold(sp, base_ready, r + 1)
                    if weighted:
                        sp.dma_start(keys[:, :], S.key.partition_broadcast(TP)).then_inc(keys_in, 16)

                def step(m, q, u):
                    s = q * 4 + u
                    n = m * 4 + u
                    hold(sp, summed, DONE(n - 4))
                    sp.dma_start(src[:, u], A.src_cols[bass.ds(s, 1)].rearrange("a p k -> (a p) k")).then_inc(src_in[u], 16)
                    sp.dma_start(dst[:, u], A.dst_cols[bass.ds(s, 1)].rearrange("a p k -> (a p) k")).then_inc(dst_in[u], 16)
                    if weighted:
                        hold(sp, b_done, DONE(n - 2))
                        at = sp.value_load(base_i[0:1, bass.ds(s, 1)], min_val=0, max_val=N)
                        sp.dma_start(dstrow[:, u % 2], A.dst[bass.ds(s * EDGES_SB, EDGES_SB)].partition_broadcast(W)
                                     ).then_inc(dstrow_in[u % 2], 16)
                        sp.dma_start(tscore[:, u % 2], S.stgt[bass.ds(at, W), :]).then_inc(tscore_in[u % 2], 16)

                in_rounds(sp, before, step, nothing)
                if weighted:
                    sp.wait_ge(emax_ready, 1)
                    sp.dma_start(S.emax.rearrange("(p a) -> p a", a=1), emax1[:, :]).then_inc(emax_out, 16)
                    sp.wait_ge(emax_out, 16)
                    sp.dma_start(emaxall[:, :], S.emax.partition_broadcast(TP)).then_inc(emax_in, 16)

            @block.gpsimd
            def _(pool):
                pool.wait_ge(credited, 1)

                def step(m, q, u):
                    s = q * 4 + u
                    hold(pool, src_in[u], (m + 1) * 16)
                    hold(pool, rows_used, DONE(m * 4 + u - 4))
                    for k in range(KB):
                        pool.indirect_dma_start(rows[:, u, k, :], None, table,
                                                bass.IndirectOffsetOnAxis(ap=src[:, u, k:k + 1], axis=0)).then_inc(rows_in[u], 16)

                in_rounds(pool, nothing, step, nothing)

            @block.tensor
            def _(pe):
                if weighted:
                    pe.wait_ge(key_ready, 1)
                    nc.tensor.transpose(psT[0][0:TP, 0:TILES], keyrow[:, :],
                                        K.ident[0:TILES, 0:TILES]).then_inc(col_done, 1)
                    pe.wait_ge(col_copied, 1)
                pe.wait_ge(credited, 1)

                def target_scores(m, u):
                    n = m * 4 + u
                    pe.wait_ge(sel_ready, n + 1)
                    pe.wait_ge(tscore_in[u % 2], (m * 2 + u // 2 + 1) * 16)
                    pe.wait_ge(scored, DONE(n - 2))
                    for k in range(KB):
                        last = nc.tensor.matmul(psb[u % 2][:, k], selT[:, u % 2, k * TP:(k + 1) * TP],
                                                tscore[:, u % 2], start=True, stop=True)
                    last.then_inc(b_done, 1)

                def before(r):
                    if weighted:
                        target_scores(r * QUADS, 0)

                def step(m, q, u):
                    s = q * 4 + u
                    n = m * 4 + u
                    if weighted and not (isinstance(s, int) and s == NSB - 1):
                        target_scores(m + (u + 1) // 4, (u + 1) % 4)
                    if weighted:
                        pe.wait_ge(weighed, DONE(n))
                    else:
                        pe.wait_ge(sel_ready, n + 1)
                        pe.wait_ge(rows_in[u], (m + 1) * 16 * KB)
                    pe.wait_ge(copied, DONE(n - 2))
                    for k in range(KB):
                        right = wrows[:, u % 2, k] if weighted else rows[:, u, k]
                        last = nc.tensor.matmul(psA[u % 2][:, 0:cols], sel[:, u, k], right, start=(k == 0), stop=(k == KB - 1))
                    last.then_inc(summed, 1)
                    hold(pe, added, DONE(n - 2))
                    hold(pe, copied, DONE(n))
                    for half in range(2):
                        last = nc.tensor.transpose(psT[u % 2][:, half * W:(half + 1) * W], part[:, u % 2, half * 128:(half + 1) * 128],
                                                   K.ident[0:W, 0:W])
                    if weighted:
                        last = nc.tensor.transpose(psT[u % 2][0:HEADS + 1, 2 * W:3 * W], part[:, u % 2, D:], K.ident[0:W, 0:W])
                    last.then_inc(turned, 1)

                in_rounds(pe, before, step, nothing)

            @block.scalar
            def _(act):
                if weighted:
                    act.wait_ge(col_done, 1)
                    act.copy(keycol[:, :], psT[0][0:TP, 0:TILES]).then_inc(col_copied, 1)
                act.wait_ge(credited, 1)

                def copy_sums(n, u):
                    act.wait_ge(summed, DONE(n))
                    act.wait_ge(turned, DONE(n - 2))
                    act.copy(part[:, u % 2], psA[u % 2][:, 0:cols]).then_inc(copied, 1)

                def step(m, q, u):
                    n = m * 4 + u
                    if weighted:
                        act.wait_ge(scored, DONE(n))
                        act.wait_ge(summed, DONE(n - 2))
                        act.activation(wrows[:, u % 2, :, D:ROW], expo[:, u % 2], ACT.Exp).then_inc(w_ready, 1)
                    if not (isinstance(q, int) and q == 0 and u == 0):
                        copy_sums(n - 1, (u - 1) % 4)

                def after(r):
                    copy_sums((r + 1) * NSB - 1, 3)

                in_rounds(act, nothing, step, after)

            @block.vector
            def _(v):
                link = Link(v, link_v)
                for sem in (summed, b_done, copied, turned, added, scored, w_ready, weighed):
                    v.sem_inc(sem, CREDIT)
                link(v.tensor_copy(base[:, :], K.low[:, :]))
                if weighted:
                    v.memset(wrows[:, :, :, ROW:], 1.0)
                    v.memset(emax[:, :, :], NEG)
                    v.memset(K.den[:, :], 0.0)
                    link(v.memset(K.sums[:, :, :], 0.0))
                link(v.tensor_copy(base_i[:, :], base[0:1, :]))
                v.sem_inc(base_ready, 1)
                v.sem_inc(credited, 1)
                if weighted:
                    v.wait_ge(key_parts_in, 48)
                    v.tensor_tensor(keyrow[:, :], degrow[:, :], noise[:, :], ALU.add).then_inc(key_ready, 1)
                    v.wait_ge(col_copied, 1)

                def rank_piece(t, u):
                    a, b = PIECES[u]
                    key = keycol[:, bass.ds(t, 1)]
                    link(v.tensor_scalar(seen[:, 0:b - a], keys[:, a:b], key, 0.0, ALU.is_lt, ALU.add,
                                         accum_out=K.smaller[:, bass.ds(t * 4 + u, 1)]))
                    if u == 3:
                        own = keys[:, bass.ds(t * TP, TP)]
                        v.tensor_scalar(lowered[:, 0], own, 2.0 ** -24, None, ALU.mult)
                        v.tensor_scalar(lowered[:, 1], own, 0.0, -1e-30, ALU.is_equal, ALU.mult)
                        link(v.scalar_tensor_tensor(seen[:, 0:TP], own, key, tri[:, :], ALU.is_equal, ALU.mult,
                                                    accum_out=K.ties[:, bass.ds(t, 1)]))
                        link(v.scalar_tensor_tensor(lowered[:, 0], own, -2.0 ** -24, lowered[:, 0], ALU.mult, ALU.min))
                        link(v.tensor_tensor(own, own, lowered[:, 0], ALU.add))
                        link(v.tensor_tensor(own, own, lowered[:, 1], ALU.add))

                def select(m, s, u):
                    n = m * 4 + u
                    v.wait_ge(dst_in[u], (m + 1) * 16)
                    v.wait_ge(summed, DONE(n - 4))
                    link(v.tensor_scalar(rel[:, u], dst[:, u], base[0:TP, bass.ds(s, 1)], None, ALU.subtract))
                    out = v.tensor_tensor(sel[:, u], rel[:, u].unsqueeze(2).to_broadcast([TP, KB, W]),
                                          K.iota[0:TP, 0:W].unsqueeze(1).to_broadcast([TP, KB, W]), ALU.is_equal)
                    if weighted:
                        v.tensor_scalar(below[:, :], rel[:, u], 0.0, NEG / 4, ALU.is_lt, ALU.mult)
                        link(v.tensor_scalar(above[:, :], rel[:, u], float(W - 1), NEG / 4, ALU.is_gt, ALU.mult))
                        v.tensor_tensor(outside[:, u], below[:, :], above[:, :], ALU.add)
                        v.wait_ge(dstrow_in[u % 2], (m * 2 + u // 2 + 1) * 16)
                        v.wait_ge(b_done, DONE(n - 2))
                        out = v.tensor_scalar(selT[:, u % 2], dstrow[:, u % 2], base[0:W, bass.ds(s, 1)], K.pidx[0:W, 0:1],
                                              ALU.subtract, ALU.is_equal)
                    out.then_inc(sel_ready, 1)

                def scores(m, s, u):
                    n = m * 4 + u
                    v.wait_ge(b_done, DONE(n))
                    b = psb[u % 2]
                    link(v.tensor_reduce(tsum[:, :, :], b[:, :, :, :].rearrange("p k c h -> p k h c"), axis=AX.X, op=ALU.add))
                    b = tsum[:, :, :]
                    v.tensor_tensor(bound[:, :, :], b, K.smax[:, :].unsqueeze(1).to_broadcast([TP, KB, HEADS]), ALU.add)
                    v.wait_ge(rows_in[u], (m + 1) * 16 * KB)
                    link(v.tensor_tensor(score[:, :, :], rows[:, u, :, D:ROW], b, ALU.add))
                    v.scalar_tensor_tensor(bound[:, :, :], bound[:, :, :], 0.2, bound[:, :, :], ALU.mult, ALU.max)
                    link(v.scalar_tensor_tensor(score[:, :, :], score[:, :, :], 0.2, score[:, :, :], ALU.mult, ALU.max))
                    v.wait_ge(w_ready, DONE(n - 2))
                    v.tensor_tensor(expo[:, u % 2], score[:, :, :], bound[:, :, :], ALU.subtract).then_inc(scored, 1)
                    link(v.tensor_tensor(masked[:, :, :], score[:, :, :], outside[:, u].unsqueeze(2).to_broadcast([TP, KB, HEADS]), ALU.add))
                    link(v.tensor_tensor(emax[:, :, :], emax[:, :, :], masked[:, :, :], ALU.max))

                def window(s):
                    return v.value_load(base_i[0:1, bass.ds(s, 1)], min_val=0, max_val=N)

                def add_sums(m, u, at):
                    n = m * 4 + u
                    hold(v, turned, DONE(n))
                    there = K.sums[:, :, bass.ds(at, W)]
                    if weighted:
                        v.tensor_tensor(K.den[:, bass.ds(at, W)], K.den[:, bass.ds(at, W)], psT[u % 2][0:HEADS + 1, 2 * W:3 * W], ALU.add)
                    v.tensor_tensor(there, there, psT[u % 2][:, 0:2 * W].rearrange("p (k w) -> p k w", k=2), ALU.add).then_inc(added, 1)
                    hold(v, added, DONE(n))

                def weigh(m, s, u):
                    v.wait_ge(w_ready, DONE(m * 4 + u))
                    v.tensor_tensor(wrows[:, u % 2, :, 0:D].rearrange("p k (h f) -> p k h f", h=HEADS),
                                    rows[:, u, :, 0:D].rearrange("p k (h f) -> p k h f", h=HEADS),
                                    wrows[:, u % 2, :, D:ROW].unsqueeze(3).to_broadcast([TP, KB, HEADS, HD]), ALU.mult).then_inc(weighed, 1)

                def before(r):
                    link.restart()
                    select(r * QUADS, 0, 0)
                    select(r * QUADS, 1, 1)
                    if weighted:
                        hold(v, keys_in, (r + 1) * 16)

                def step(m, q, u):
                    s = q * 4 + u
                    known = isinstance(s, int)
                    if u == 0:
                        link.restart()
                    if weighted:
                        scores(m, s, u)
                    if not (known and s >= NSB - 2):
                        select(m + (u + 2) // 4, s + 2, (u + 2) % 4)
                    if weighted:
                        weigh(m, s, u)
                    at = None if known and s == 0 else window(s - 1)
                    if weighted:
                        rank_piece(q, u)
                    if at is not None:
                        add_sums(m - (1 if u == 0 else 0), (u - 1) % 4, at)
                    if known and s == NSB - 1:
                        add_sums(m, u, window(s))

                def after(r):
                    link.restart()
                    link(v.tensor_scalar(base[:, :], base[:, :], float(W), float(N), ALU.add, ALU.min))
                    v.tensor_copy(base_i[:, :], base[0:1, :]).then_inc(base_ready, 1)

                in_rounds(v, before, step, after)
                if weighted:
                    link.restart()
                    v.tensor_reduce(emax1[:, :], emax[:, :, :], axis=AX.XY, op=ALU.max).then_inc(emax_ready, 1)
                    v.wait_ge(emax_in, 16)
                    link(v.tensor_reduce(K.emax[:, :], emaxall[:, :], axis=AX.X, op=ALU.max))
        M.close()


def nodes_block(nc, A, S, K):
    G = 2
    GN = G * TP
    GROUPS = N // GN
    with ExitStack() as stack:
        M = Parts(nc, stack, "node_")
        wgate = M.sb("wgate", [128, 4, D])
        ff1 = M.sb("ff1", [128, 2, 2 * D])
        ff2 = M.sb("ff2", [128, 4, D])
        ff1_b = M.sb("ff1_b", [128, 4])
        vecs = M.sb("vecs", [TP, 8, D])
        x = M.sb("x", [TP, G, D])
        ym = M.sb("ym", [TP, G, D])
        tsc = M.sb("tsc", [TP, G, SPLITS, HEADS], BF16)
        rank = M.sb("rank", [TP, G], I32)
        sumsT = M.sb("sumsT", [128, 2, GN])
        denT = M.sb("denT", [HEADS + 1, GN])
        eps_e = M.sb("eps_e", [TP, G, HEADS])
        den = M.sb("den", [TP, G, HEADS])
        count = M.sb("count", [TP, G])
        dinv = M.sb("dinv", [TP, G])
        pre = M.sb("pre", [TP, G, D])
        low = M.sb("low", [TP, G, D])
        pos = M.sb("pos", [TP, G, D])
        hl = M.sb("hl", [TP, G, D])
        ha = M.sb("ha", [TP, G, D])
        gate = M.sb("gate", [TP, G, D])
        h = M.sb("h", [TP, G, D])
        f = M.sb("f", [TP, G, D])
        x1 = M.sb("x1", [TP, G, D])
        x1d = M.sb("x1d", [TP, G, D])
        hT = M.sb("hT", [128, 4, GN])
        rT = M.sb("rT", [128, 4, GN])
        stats = M.sb("stats", [TP, G, 6])
        mv = M.sb("mv", [TP, G, 2])
        var, rstd, half, square = (M.sb(n, [TP, G]) for n in ("var", "rstd", "half", "square"))
        psR = M.ps("psR", [TP, G, 512])
        psT = M.ps("psT", [128, 2, 512])
        psG = M.ps("psG", [TP, G, 512])
        psF = M.ps("psF", [128, 2, 512])
        GAT_B, LL_G, LL_B, LG_G, LG_B, L2_G, L2_B, FF2_B = range(8)

        weights_in, x_in, rank_ready, ym_in = (M.sem(n) for n in ("weights_in", "x_in", "rank_ready", "ym_in"))
        slices_ready, rows_turned, bound_ready, eps_ready = (M.sem(n) for n in ("slices_ready", "rows_turned", "bound_ready", "eps_ready"))
        pre_ready, elu_ready, normed, hT_done, hT_ready = (M.sem(n) for n in ("pre_ready", "elu_ready", "normed", "hT_done", "hT_ready"))
        gate_done, gate_ready, h_ready, h_turned, h_copied = (M.sem(n) for n in ("gate_done", "gate_ready", "h_ready", "h_turned", "h_copied"))
        ff1_done, relu_ready, ff2_done, x1_ready, x1_turned, x1_copied = (M.sem(n) for n in (
            "ff1_done", "relu_ready", "ff2_done", "x1_ready", "x1_turned", "x1_copied"))
        stored, link_v, link_a, ticks, sums_taken = (M.sem(n) for n in ("stored", "link_v", "link_a", "ticks", "sums_taken"))

        def hold(eng, sem, value):
            eng.wait_ge(sem, value)
            eng.sem_inc(ticks, 1)

        def groups(eng, step):
            step(0, True)
            with eng.Fori(1, GROUPS) as g:
                step(g, False)

        def by_group(dram):
            return dram.rearrange("(g j p) c -> g p j c", j=G, p=TP)

        with nc.Block() as block:
            @block.sync
            def _(sp):
                for t, a in ((wgate[:, 0:2], A.wlT), (wgate[:, 2:4], A.wgT), (ff1[:, :, :], A.ff1_wT), (ff2[:, :, :], A.ff2_wT)):
                    sp.dma_start(t, a.rearrange("(k p) n -> p k n", p=128)).then_inc(weights_in, 16)
                sp.dma_start(ff1_b[:, :], A.ff1_b).then_inc(weights_in, 16)
                sp.dma_start(vecs[:, :, :], A.rowvecs.partition_broadcast(TP)).then_inc(weights_in, 16)

                def step(g, first):
                    if not first:
                        hold(sp, x1_ready, g)
                    sp.dma_start(x[:, :, :], by_group(A.x)[bass.ds(g, 1)].rearrange("a p j c -> (a p) j c")).then_inc(x_in, 16)
                    sp.dma_start(tsc[:, :, :, :].rearrange("p j s h -> p j (s h)"), by_group(S.stgt[0:N])[bass.ds(g, 1)].rearrange("a p j c -> (a p) j c")).then_inc(x_in, 16)
                    hold(sp, x1_ready, g + 1)
                    sp.dma_start(by_group(S.x1)[bass.ds(g, 1)].rearrange("a p j c -> (a p) j c"), x1[:, :, :]).then_inc(stored, 16)
                    sp.dma_start(by_group(S.x1d)[bass.ds(g, 1)].rearrange("a p j c -> (a p) j c"), x1d[:, :, :]).then_inc(stored, 16)
                    with nc.allow_non_contiguous_dma(reason="one value a node"):
                        sp.dma_start(by_group(S.dinv.rearrange("(n c) -> n c", c=1))[bass.ds(g, 1)].rearrange("a p j c -> (a p) j c"),
                                     dinv[:, :].unsqueeze(2)).then_inc(stored, 16)

                groups(sp, step)
                sp.wait_ge(stored, 48 * GROUPS)

            @block.gpsimd
            def _(pool):
                def step(g, first):
                    if not first:
                        hold(pool, x1_ready, g)
                    pool.tensor_copy(rank[:, :], K.rank[:, bass.ds(g * G, G)]).then_inc(rank_ready, 1)
                    hold(pool, rank_ready, g + 1)
                    for j in range(G):
                        pool.indirect_dma_start(ym[:, j, :], None, S.ys, bass.IndirectOffsetOnAxis(ap=rank[:, j:j + 1], axis=0)).then_inc(ym_in, 16)

                groups(pool, step)

            @block.tensor
            def _(pe):
                pe.wait_ge(weights_in, 96)

                def step(g, first):
                    hold(pe, slices_ready, g + 1)
                    if not first:
                        pe.wait_ge(x1_copied, g)
                    for j in range(G):
                        for half in range(2):
                            nc.tensor.transpose(psR[:, j, half * 128:(half + 1) * 128], sumsT[:, half, j * TP:(j + 1) * TP], K.ident[:, :])
                        last = nc.tensor.transpose(psR[:, j, D:D + HEADS + 1], denT[:, j * TP:(j + 1) * TP], K.ident[0:HEADS + 1, 0:HEADS + 1])
                    last.then_inc(rows_turned, 1)
                    hold(pe, normed, g + 1)
                    for j in range(G):
                        for k in range(4):
                            row = (hl, ha)[k // 2][:, j, (k % 2) * 128:(k % 2 + 1) * 128]
                            last = nc.tensor.transpose(psT[:, k // 2, (k % 2) * GN + j * TP:(k % 2) * GN + (j + 1) * TP], row, K.ident[0:TP, 0:TP])
                    last.then_inc(hT_done, 1)
                    hold(pe, hT_ready, g + 1)
                    for j in range(G):
                        for k in range(4):
                            last = nc.tensor.matmul(psG[:, j, 0:D], hT[:, k, j * TP:(j + 1) * TP], wgate[:, k], start=(k == 0), stop=(k == 3))
                    last.then_inc(gate_done, 1)
                    hold(pe, h_ready, g + 1)
                    for j in range(G):
                        for k in range(2):
                            last = nc.tensor.transpose(psT[:, 0, k * GN + j * TP:k * GN + (j + 1) * TP], h[:, j, k * 128:(k + 1) * 128], K.ident[0:TP, 0:TP])
                    last.then_inc(h_turned, 1)
                    hold(pe, h_copied, g + 1)
                    for m in range(4):
                        for k in range(2):
                            last = nc.tensor.matmul(psF[:, m // 2, (m % 2) * GN:(m % 2 + 1) * GN], ff1[:, k, m * 128:(m + 1) * 128], hT[:, k],
                                                    start=(k == 0), stop=(k == 1))
                    last.then_inc(ff1_done, 1)
                    hold(pe, relu_ready, g + 1)
                    for j in range(G):
                        for k in range(4):
                            last = nc.tensor.matmul(psG[:, j, 0:D], rT[:, k, j * TP:(j + 1) * TP], ff2[:, k], start=(k == 0), stop=(k == 3))
                    last.then_inc(ff2_done, 1)
                    hold(pe, x1_ready, g + 1)
                    for j in range(G):
                        for k in range(2):
                            last = nc.tensor.transpose(psT[:, 0, k * GN + j * TP:k * GN + (j + 1) * TP], x1d[:, j, k * 128:(k + 1) * 128], K.ident[0:TP, 0:TP])
                    last.then_inc(x1_turned, 1)

                groups(pe, step)

            @block.scalar
            def _(act):
                link = Link(act, link_a)
                halves = lambda t: t.rearrange("p (k n) -> p k n", k=2)
                act.wait_ge(weights_in, 96)

                def step(g, first):
                    link.restart()
                    act.copy(sumsT[:, :, :], K.sums[:, :, bass.ds(g * GN, GN)])
                    act.copy(denT[:, :], K.den[:, bass.ds(g * GN, GN)]).then_inc(slices_ready, 1)
                    act.wait_ge(bound_ready, g + 1)
                    act.activation(eps_e[:, :, :], den[:, :, :], ACT.Exp, scale=-1.0, bias=K.emax[:, 0:1]).then_inc(eps_ready, 1)
                    act.wait_ge(pre_ready, g + 1)
                    act.activation(pos[:, :, :], pre[:, :, :], ACT.Relu)
                    act.activation(low[:, :, :], low[:, :, :], ACT.Exp).then_inc(elu_ready, 1)
                    act.wait_ge(hT_done, g + 1)
                    for kk in range(2):
                        last = act.copy(hT[:, 2 * kk:2 * kk + 2], halves(psT[:, kk, 0:2 * GN]))
                    last.then_inc(hT_ready, 1)
                    act.wait_ge(gate_done, g + 1)
                    link(act.activation(gate[:, :, :], psG[:, :, 0:D], ACT.Exp, scale=-1.0))
                    act.activation(gate[:, :, :], gate[:, :, :], ACT.Copy, bias=1.0).then_inc(gate_ready, 1)
                    act.wait_ge(h_turned, g + 1)
                    act.copy(hT[:, 0:2], halves(psT[:, 0, 0:2 * GN])).then_inc(h_copied, 1)
                    act.wait_ge(ff1_done, g + 1)
                    for m in range(4):
                        last = act.activation(rT[:, m], psF[:, m // 2, (m % 2) * GN:(m % 2 + 1) * GN], ACT.Relu, bias=ff1_b[:, m:m + 1])
                    last.then_inc(relu_ready, 1)
                    hold(act, x1_turned, g + 1)
                    act.copy(K.sums[:, :, bass.ds(g * GN, GN)], halves(psT[:, 0, 0:2 * GN])).then_inc(x1_copied, 1)

                groups(act, step)

            @block.vector
            def _(v):
                link = Link(v, link_v)
                v.wait_ge(weights_in, 96)

                def vec(n):
                    return vecs[:, n].unsqueeze(1).to_broadcast([TP, G, D])

                def layer_norm(out, t, gain=None, shift=None, signal=None):
                    for j in range(G):
                        last = v.bn_stats(stats[:, j], t[:, j])
                    link(last)
                    for j in range(G):
                        last = v.bn_aggr(mv[:, j], stats[:, j])
                    link(last)
                    link(v.tensor_scalar(var[:, :], mv[:, :, 1], EPS, None, ALU.add))
                    rsqrt(v, link, rstd[:, :], var[:, :], half[:, :], square[:, :])
                    for j in range(G):
                        last = v.tensor_scalar(out[:, j], t[:, j], mv[:, j, 0:1], rstd[:, j:j + 1], ALU.subtract, ALU.mult)
                    link(last)
                    if gain is not None:
                        link(v.tensor_tensor(out[:, :, :], out[:, :, :], vec(gain), ALU.mult))
                        last = v.tensor_tensor(out[:, :, :], out[:, :, :], vec(shift), ALU.add)
                        last.then_inc(signal, 1) if signal is not None else link(last)

                def step(g, first):
                    link.restart()
                    v.wait_ge(x_in, (g + 1) * 32)
                    link(v.tensor_reduce(den[:, :, :], tsc[:, :, :, :].rearrange("p j s h -> p j h s"), axis=AX.X, op=ALU.add))
                    link(v.tensor_tensor(den[:, :, :], den[:, :, :], K.smax[:, :].unsqueeze(1).to_broadcast([TP, G, HEADS]), ALU.add))
                    v.scalar_tensor_tensor(den[:, :, :], den[:, :, :], 0.2, den[:, :, :], ALU.mult, ALU.max).then_inc(bound_ready, 1)
                    v.wait_ge(ym_in, (g + 1) * 16 * G)
                    link(v.tensor_tensor(ha[:, :, :], x[:, :, :], ym[:, :, :], ALU.add))
                    layer_norm(ha, ha, LG_G, LG_B)
                    v.wait_ge(rows_turned, g + 1)
                    v.wait_ge(eps_ready, g + 1)
                    if not first:
                        v.wait_ge(stored, g * 48)
                    link(v.scalar_tensor_tensor(den[:, :, :], eps_e[:, :, :], 1e-16, psR[:, :, D:D + HEADS], ALU.mult, ALU.add))
                    link(v.tensor_scalar(var[:, :], psR[:, :, D + HEADS], 1.0, None, ALU.add))
                    rsqrt(v, link, dinv[:, :], var[:, :], half[:, :], square[:, :])
                    link(v.tensor_scalar(den[:, :, :], den[:, :, :], 1e-37, None, ALU.max))
                    link(v.reciprocal(den[:, :, :], den[:, :, :]))
                    link(v.tensor_tensor(pre[:, :, :].rearrange("p j (h f) -> p j h f", h=HEADS),
                                         psR[:, :, 0:D].rearrange("p j (h f) -> p j h f", h=HEADS),
                                         den[:, :, :].unsqueeze(3).to_broadcast([TP, G, HEADS, HD]), ALU.mult))
                    link(v.tensor_tensor(pre[:, :, :], pre[:, :, :], x[:, :, :], ALU.add))
                    link(v.tensor_tensor(pre[:, :, :], pre[:, :, :], vec(GAT_B), ALU.add))
                    v.tensor_scalar(low[:, :, :], pre[:, :, :], 0.0, None, ALU.min).then_inc(pre_ready, 1)
                    v.wait_ge(elu_ready, g + 1)
                    link(v.scalar_tensor_tensor(hl[:, :, :], low[:, :, :], -1.0, pos[:, :, :], ALU.add, ALU.add))
                    layer_norm(hl, hl, LL_G, LL_B, normed)
                    v.wait_ge(normed, g + 1)
                    link(v.tensor_tensor(h[:, :, :], hl[:, :, :], ha[:, :, :], ALU.subtract))
                    v.wait_ge(gate_ready, g + 1)
                    link(v.reciprocal(gate[:, :, :], gate[:, :, :]))
                    link(v.tensor_tensor(h[:, :, :], h[:, :, :], gate[:, :, :], ALU.mult))
                    v.tensor_tensor(h[:, :, :], h[:, :, :], ha[:, :, :], ALU.add).then_inc(h_ready, 1)
                    v.wait_ge(h_ready, g + 1)
                    link(v.tensor_tensor(x1[:, :, :], h[:, :, :], vec(FF2_B), ALU.add))
                    v.wait_ge(ff2_done, g + 1)
                    link(v.tensor_tensor(f[:, :, :], x1[:, :, :], psG[:, :, 0:D], ALU.add))
                    layer_norm(f, f, L2_G, L2_B)
                    link(v.tensor_tensor(f[:, :, :], f[:, :, :], x[:, :, :], ALU.add))
                    layer_norm(x1, f)
                    for j in range(G):
                        last = v.tensor_scalar(x1d[:, j], x1[:, j], dinv[:, j:j + 1], None, ALU.mult)
                    last.then_inc(x1_ready, 1)

                groups(v, step)
        M.close()


def output_block(nc, A, S, K, out):
    CN = 2 * TP
    CHUNKS = N // CN
    with ExitStack() as stack:
        M = Parts(nc, stack, "out_")
        w = M.sb("w", [128, 2, D])
        vec = M.sb("vec", [128, 3, 2])
        dinv = M.sb("dinv", [128, N])
        g = M.sb("g", [128, 2, CN])
        o = M.sb("o", [128, 2, N])
        stats = M.sb("stats", [128, 2, CHUNKS, 6])
        mv = M.sb("mv", [128, 2, 2])
        gain = M.sb("gain", [128, 2])
        shift = M.sb("shift", [128, 2])
        act_o = M.sb("act_o", [128, 2, CN])
        x1 = M.sb("x1", [TP, 2, D])
        res = M.sb("res", [TP, 2, D])
        stat1 = M.sb("stat1", [TP, 2, 6])
        mv1 = M.sb("mv1", [TP, 2, 2])
        y = M.sb("y", [TP, 2, D])
        var, half, square = (M.sb(n, [128, 2]) for n in ("var", "half", "square"))
        rstd = M.sb("rstd", [TP, 2])
        psO = M.ps("psO", [128, 2, 512])
        psT = M.ps("psT", [TP, 2, 512])
        weights_in, dinv_in, g_ready, o_done, scaled, o_ready = (M.sem(n) for n in ("weights_in", "dinv_in", "g_ready", "o_done", "scaled", "o_ready"))
        norm_ready, relu_ready, turned, x1_in, y_ready, stored = (M.sem(n) for n in ("norm_ready", "relu_ready", "turned", "x1_in", "y_ready", "stored"))
        stat_ready, link_v, link_a, ticks = (M.sem(n) for n in ("stat_ready", "link_v", "link_a", "ticks"))

        def hold(eng, sem, value):
            eng.wait_ge(sem, value)
            eng.sem_inc(ticks, 1)

        def chunks(eng, step):
            step(0, True)
            with eng.Fori(1, CHUNKS) as c:
                step(c, False)

        def by_chunk(dram, c):
            return dram.rearrange("(g j p) c -> g p j c", j=2, p=TP)[bass.ds(c, 1)].rearrange("a p j c -> (a p) j c")

        with nc.Block() as block:
            @block.sync
            def _(sp):
                sp.dma_start(w[:, :, :], A.gcn_w.rearrange("(k p) n -> p k n", p=128)).then_inc(weights_in, 16)
                sp.dma_start(vec[:, :, :], A.colvecs).then_inc(weights_in, 16)
                sp.dma_start(dinv[:, :], S.dinv.partition_broadcast(128)).then_inc(dinv_in, 16)

                def step(c, first):
                    if not first:
                        hold(sp, y_ready, c)
                    sp.dma_start(x1[:, :, :], by_chunk(S.x1, c)).then_inc(x1_in, 16)
                    hold(sp, y_ready, c + 1)
                    sp.dma_start(by_chunk(out, c), y[:, :, :]).then_inc(stored, 16)

                chunks(sp, step)
                sp.wait_ge(stored, 16 * CHUNKS)

            @block.tensor
            def _(pe):
                pe.wait_ge(weights_in, 32)

                def product(c, first):
                    if not first:
                        hold(pe, scaled, c)
                    for m in range(2):
                        for k in range(2):
                            last = nc.tensor.matmul(psO[:, m, 0:CN], w[:, k, m * 128:(m + 1) * 128], K.sums[:, k, bass.ds(c * CN, CN)],
                                                    start=(k == 0), stop=(k == 1))
                    last.then_inc(o_done, 1)

                def turn(c, first):
                    hold(pe, relu_ready, c + 1)
                    if not first:
                        hold(pe, y_ready, c)
                    for j in range(2):
                        for k in range(2):
                            last = nc.tensor.transpose(psT[:, j, k * 128:(k + 1) * 128], act_o[:, k, j * TP:(j + 1) * TP], K.ident[:, :])
                    last.then_inc(turned, 1)

                chunks(pe, product)
                chunks(pe, turn)

            @block.scalar
            def _(act):
                def bias(c, first):
                    act.wait_ge(scaled, c + 1)
                    for k in range(2):
                        last = act.activation(o[:, k, bass.ds(c * CN, CN)], o[:, k, bass.ds(c * CN, CN)], ACT.Identity, bias=vec[:, 0, k:k + 1])
                    last.then_inc(o_ready, 1)

                def relu(c, first):
                    if not first:
                        act.wait_ge(turned, c)
                    for k in range(2):
                        last = act.activation(act_o[:, k], o[:, k, bass.ds(c * CN, CN)], ACT.Relu, scale=gain[:, k:k + 1], bias=shift[:, k:k + 1])
                    last.then_inc(relu_ready, 1)

                act.wait_ge(weights_in, 32)
                chunks(act, bias)
                act.wait_ge(norm_ready, 1)
                chunks(act, relu)

            @block.vector
            def _(v):
                link = Link(v, link_v)
                v.wait_ge(dinv_in, 16)

                def scale(c, first):
                    v.wait_ge(o_done, c + 1)
                    v.tensor_tensor(o[:, :, bass.ds(c * CN, CN)], psO[:, :, 0:CN],
                                    dinv[:, bass.ds(c * CN, CN)].unsqueeze(1).to_broadcast([128, 2, CN]), ALU.mult).then_inc(scaled, 1)

                chunks(v, scale)
                for c in range(CHUNKS):
                    v.wait_ge(o_ready, c + 1)
                    for k in range(2):
                        last = v.bn_stats(stats[:, k, c], o[:, k, c * CN:(c + 1) * CN])
                link(last)
                for k in range(2):
                    last = v.bn_aggr(mv[:, k], stats[:, k])
                link(last)
                link(v.tensor_scalar(var[:, :], mv[:, :, 1], EPS, None, ALU.add))
                rsqrt(v, link, gain[:, :], var[:, :], half[:, :], square[:, :])
                link(v.tensor_tensor(gain[:, :], gain[:, :], vec[:, 1], ALU.mult))
                link(v.tensor_tensor(shift[:, :], mv[:, :, 0], gain[:, :], ALU.mult))
                v.tensor_tensor(shift[:, :], vec[:, 2], shift[:, :], ALU.subtract).then_inc(norm_ready, 1)
                link.restart()

                def last_norm(c, first):
                    link.restart()
                    v.wait_ge(turned, c + 1)
                    v.wait_ge(x1_in, (c + 1) * 16)
                    link(v.tensor_tensor(res[:, :, :], x1[:, :, :], psT[:, :, 0:D], ALU.add))
                    for j in range(2):
                        last = v.bn_stats(stat1[:, j], res[:, j])
                    link(last)
                    for j in range(2):
                        last = v.bn_aggr(mv1[:, j], stat1[:, j])
                    link(last)
                    link(v.tensor_scalar(var[0:TP, :], mv1[:, :, 1], EPS, None, ALU.add))
                    rsqrt(v, link, rstd[:, :], var[0:TP, :], half[0:TP, :], square[0:TP, :])
                    if not first:
                        v.wait_ge(stored, c * 16)
                    for j in range(2):
                        last = v.tensor_scalar(y[:, j], res[:, j], mv1[:, j, 0:1], rstd[:, j:j + 1], ALU.subtract, ALU.mult)
                    last.then_inc(y_ready, 1)

                chunks(v, last_norm)
        M.close()


def build(nc, A, out):
    S, K = Named(), Named()
    S.proj = nc.dram_tensor("proj_rows", (N, ROW), F32).ap()
    S.stgt = nc.dram_tensor("target_scores", (NA, SPLITS * HEADS), BF16).ap()
    S.smax = nc.dram_tensor("source_maxima", (TP * HEADS,), F32).ap()
    S.low = nc.dram_tensor("window_lows", (NSB,), F32).ap()
    S.span = nc.dram_tensor("superblock_widths", (NSB,), F32).ap()
    S.deg = nc.dram_tensor("out_degrees", (NHIST,), F32).ap()
    S.key = nc.dram_tensor("keys", (N,), F32).ap()
    S.rank = nc.dram_tensor("ranks", (N,), I32).ap()
    S.xs = nc.dram_tensor("ordered_rows", (NP, D), F32).ap()
    S.ys = nc.dram_tensor("mamba_rows", (NP, D), F32).ap()
    S.x1 = nc.dram_tensor("x1_rows", (N, D), F32).ap()
    S.x1d = nc.dram_tensor("x1_scaled_rows", (N, D), F32).ap()
    S.dinv = nc.dram_tensor("degree_scales", (N,), F32).ap()
    S.emax = nc.dram_tensor("score_maxima", (TP,), F32).ap()
    with ExitStack() as stack:
        P = Parts(nc, stack, "")
        K.ident = P.sb("ident", [128, 128])
        K.iota = P.sb("iota", [128, 128])
        K.pidx = P.sb("pidx", [128, 1])
        K.steps = P.sb("steps", [1, 132])
        K.low = P.sb("low", [128, NSB])
        K.smax = P.sb("smax", [TP, HEADS])
        K.rounds = P.sb("rounds", [1, 1], I32)
        K.rank = P.sb("rank", [TP, TILES], I32)
        K.smaller = P.sb("smaller", [TP, 4 * TILES])
        K.ties = P.sb("ties", [TP, TILES])
        K.sums = P.sb("sums", [128, 2, NA])
        K.den = P.sb("den", [HEADS + 1, NA])
        K.emax = P.sb("emax", [TP, 1])
        tables_block(nc, A, S, K)
        edge_pass(nc, A, S, K, True)
        ranks_block(nc, A, S, K)
        mamba_block(nc, A, S, K)
        nodes_block(nc, A, S, K)
        edge_pass(nc, A, S, K, False)
        output_block(nc, A, S, K, out)


class Named:
    pass




def layout(inputs):
    import numpy as np

    g = {k: np.asarray(v) for k, v in inputs.items()}
    w = {k.split("_gnn_")[1] if "_gnn_" in k else k: v for k, v in g.items()}
    t = lambda a: np.ascontiguousarray(a.T)
    a_blk = np.zeros((D, 2 * HEADS), w["gat_a_src"].dtype)
    for h in range(HEADS):
        a_blk[h * HD:(h + 1) * HD, h] = w["gat_a_src"][h]
        a_blk[h * HD:(h + 1) * HD, HEADS + h] = w["gat_a_tgt"][h]
    halves = lambda a: np.ascontiguousarray(a.reshape(2, 128, -1).transpose(1, 0, 2))
    return {
        "x": w["x"], "xT": t(w["x"]), "src": w["src"], "dst": w["dst"], "node_vec": w["node_vec"],
        "src_cols": np.ascontiguousarray(w["src"].reshape(NSB, KB, TP).transpose(0, 2, 1)),
        "dst_cols": np.ascontiguousarray(w["dst"].reshape(NSB, KB, TP).transpose(0, 2, 1)),
        "gat_w": w["gat_w"], "gat_wT": t(w["gat_w"]), "a_blk": a_blk,
        "in_wT": t(w["in_proj_w"]), "x_wT": t(w["x_proj_w"]), "dt_wT": t(w["dt_proj_w"]), "out_wT": t(w["out_proj_w"]),
        "conv_w": halves(w["conv_w"]), "conv_b": halves(w["conv_b"]), "dt_b": halves(w["dt_proj_b"]),
        "a_log": halves(w["A_log"]), "d_param": halves(w["D_param"]),
        "wlT": t(w["wl"]), "wgT": t(w["wg"]), "ff1_wT": t(w["ff1_w"]), "ff2_wT": t(w["ff2_w"]),
        "ff1_b": t(w["ff1_b"].reshape(4, 128)),
        "rowvecs": np.stack([w[k] for k in ("gat_b", "ln_local_g", "ln_local_b", "ln_global_g", "ln_global_b",
                                            "ln2_g", "ln2_b", "ff2_b")]),
        "gcn_w": w["W"], "colvecs": np.ascontiguousarray(np.stack([w[k].reshape(2, 128) for k in ("b", "gamma", "beta")]).transpose(2, 0, 1)),
        "ident": np.eye(128, dtype=np.float32),
        "iota": np.tile(np.arange(128, dtype=np.float32), (128, 1)),
        "pidx": np.arange(128, dtype=np.float32)[:, None],
        "steps": (W * np.arange(132, dtype=np.float32))[None],
        "tri": np.tril(np.ones((TP, TP), np.float32), -1),
    }


def kernel(**inputs):
    import concourse.bacc as bacc
    from concourse.bass_utils import run_bass_kernel_spmd

    arrays = {k + "_d": v for k, v in layout(inputs).items()}
    nc = bacc.Bacc("TRN2", target_bir_lowering=False, num_devices=1)
    args = Named()
    for name, a in arrays.items():
        args.__dict__[name[:-2]] = nc.dram_tensor(name, a.shape, mybir.dt.from_np(a.dtype), kind="ExternalInput").ap()
    out = nc.dram_tensor("out_d", (N, D), F32, kind="ExternalOutput").ap()
    build(nc, args, out)
    r = run_bass_kernel_spmd(nc, [arrays], core_ids=[0])
    return r.results[0]["out_d"]
```

```python
from contextlib import ExitStack

import concourse.bass as bass
from concourse import mybir

F32 = mybir.dt.float32
BF16 = mybir.dt.bfloat16
I32 = mybir.dt.int32
ALU = mybir.AluOpType
ACT = mybir.ActivationFunctionType
AX = mybir.AxisListType

N, E, D = 6250, 200000, 256
HEADS, HD = 4, 64
TP = 125
TILES = N // TP
KB = 8
EDGES_SB = KB * TP
NSB = E // EDGES_SB
W = 48
NA = N + W + 6
ROW = D + HEADS
DSTATE, DCONV, DTR = 16, 4, 16
CH = 500
CT = CH // TP
NCH = -(-N // CH)
HI, LO = 98, 64
NHIST = HI * LO
SPLITS = 3
EPS = 1e-5
NEG = -3.0e38


class Link:

    def __init__(self, eng, sem):
        self.eng, self.sem, self.n = eng, sem, 0

    def __call__(self, ins):
        self.n += 1
        ins.then_inc(self.sem, 1)
        self.eng.wait_ge(self.sem, self.n)

    def restart(self):
        self.eng.sem_clear(self.sem)
        self.n = 0


class Parts:

    def __init__(self, nc, stack, prefix):
        self.nc, self.stack, self.prefix, self.sems = nc, stack, prefix, []

    def sb(self, name, shape, dt=F32):
        return self.stack.enter_context(self.nc.sbuf_tensor(self.prefix + name, shape, dt))

    def ps(self, name, shape, dt=F32):
        return self.stack.enter_context(self.nc.psum_tensor(self.prefix + name, shape, dt))

    def sem(self, name):
        self.sems.append(self.nc.alloc_semaphore(self.prefix + name))
        return self.sems[-1]

    def close(self):
        self.nc.clear_and_free_semaphores(self.sems)
        self.nc.all_engine_barrier()


def rsqrt(v, link, out, value, half, square):
    MAGIC, STEPS = float(0x5F3759DF), 3
    link(v.tensor_scalar(out.bitcast(I32), value.bitcast(I32), 1, None, ALU.logical_shift_right))
    v.tensor_scalar(half, value, -0.5, None, ALU.mult)
    link(v.tensor_scalar(out.bitcast(I32), out.bitcast(I32), -1.0, MAGIC, ALU.mult, ALU.add))
    for _ in range(STEPS):
        link(v.tensor_tensor(square, out, out, ALU.mult))
        link(v.tensor_tensor(square, square, half, ALU.mult))
        link(v.scalar_tensor_tensor(out, square, 1.5, out, ALU.add, ALU.mult))


def tables_block(nc, A, S, K):
    G = 5
    GN = G * TP
    HC = 16
    HSTEPS = E // TP // HC
    with ExitStack() as stack:
        M = Parts(nc, stack, "tab_")
        gatw = M.sb("gatw", [128, 2, D])
        ablk = M.sb("ablk", [128, 2, 2 * HEADS])
        waug = M.sb("waug", [128, 2, D + 2 * HEADS])
        xt = M.sb("xt", [128, 2, 2, GN])
        rows = M.sb("rows", [TP, 2, G, D + 2 * HEADS])
        split = M.sb("split", [TP, 2, G, SPLITS, HEADS], BF16)
        rest = M.sb("rest", [TP, G, HEADS])
        smax5 = M.sb("smax5", [TP, G, HEADS])
        smax1 = M.sb("smax1", [TP, HEADS])
        smaxall = M.sb("smaxall", [TP, TP * HEADS])
        dst2 = M.sb("dst2", [NSB // 2, 2, EDGES_SB], I32)
        lowhigh = M.sb("lowhigh", [NSB // 2, 2, 2])
        span = M.sb("span", [NSB // 2, 2])
        spanrow = M.sb("spanrow", [1, NSB])
        widest = M.sb("widest", [1, 1])
        reach = M.sb("reach", [1, 132])
        nrounds = M.sb("nrounds", [1, 1])
        srcs = M.sb("srcs", [TP, E // TP], I32)
        hi = M.sb("hi", [TP, E // TP], I32)
        lo = M.sb("lo", [TP, E // TP], I32)
        ohhi = M.sb("ohhi", [TP, 2, HC, HI], BF16)
        ohlo = M.sb("ohlo", [TP, 2, HC, LO], BF16)
        hist = M.sb("hist", [HI, LO])
        pad = M.sb("pad", [NA - N, SPLITS * HEADS], BF16)
        psw = M.ps("psw", [128, 2, 2 * HEADS])
        psr = [M.ps(f"psr{j}", [TP, D + 2 * HEADS]) for j in range(G)]
        psh = M.ps("psh", [HI, LO])

        const_in, weights_in, dst_in, src_in = (M.sem(n) for n in ("const_in", "weights_in", "dst_in", "src_in"))
        xt_in = [M.sem("xt_in0"), M.sem("xt_in1")]
        vw_done, vw_copied = M.sem("vw_done"), M.sem("vw_copied")
        proj_done, proj_copied, rows_maxed = M.sem("proj_done"), M.sem("proj_copied"), M.sem("rows_maxed")
        rows_out = [M.sem("rows_out0"), M.sem("rows_out1")]
        scores_out = [M.sem("scores_out0"), M.sem("scores_out1")]
        smax_ready, smax_out, smax_in = M.sem("smax_ready"), M.sem("smax_out"), M.sem("smax_in")
        span_ready, span_out, span_in, base_in = (M.sem(n) for n in ("span_ready", "span_out", "span_in", "base_in"))
        oh_ready, oh_used, hist_done, hist_ready, hist_out = (M.sem(n) for n in ("oh_ready", "oh_used", "hist_done", "hist_ready", "hist_out"))
        link_v, pad_ready, pad_out = M.sem("link_v"), M.sem("pad_ready"), M.sem("pad_out")

        PAIRS = TILES // G // 2

        with nc.Block() as block:
            @block.sync
            def _(sp):
                for t, a in ((K.ident, A.ident), (K.iota, A.iota), (K.pidx, A.pidx), (K.steps, A.steps)):
                    sp.dma_start(t[:, :], a).then_inc(const_in, 16)
                sp.dma_start(gatw[:, :, :], A.gat_w.rearrange("(k p) n -> p k n", p=128)).then_inc(weights_in, 16)
                sp.dma_start(ablk[:, :, :], A.a_blk.rearrange("(k p) n -> p k n", p=128)).then_inc(weights_in, 16)
                sp.dma_start(waug[:, :, 0:D], A.gat_wT.rearrange("(k p) n -> p k n", p=128)).then_inc(weights_in, 16)
                sp.dma_start(srcs[:, :], A.src.rearrange("(p c) -> p c", p=TP)).then_inc(src_in, 16)
                sp.dma_start(dst2[:, :, :], A.dst.rearrange("(p j e) -> p j e", j=2, e=EDGES_SB)).then_inc(dst_in, 16)
                xT = A.xT.rearrange("(k p) n -> p k n", p=128)
                rows_dram = S.proj.rearrange("(g j p) c -> g p j c", j=G, p=TP)
                scores_dram = S.stgt[0:N, :].rearrange("(g j p) c -> g p j c", j=G, p=TP)
                for par in range(2):
                    sp.dma_start(xt[:, par], xT[:, :, par * GN:(par + 1) * GN]).then_inc(xt_in[par], 16)

                def step(i, last):
                    for par in range(2):
                        sp.wait_ge(proj_copied, i * (2 * G) + (par + 1) * G)
                        sp.dma_start(rows_dram[bass.ds(i * 2 + par, 1)].rearrange("a p j c -> (a p) j c"),
                                     rows[:, par, :, 0:ROW]).then_inc(rows_out[par], 16)
                        sp.wait_ge(rows_maxed, i * 2 + par + 1)
                        sp.dma_start(scores_dram[bass.ds(i * 2 + par, 1)].rearrange("a p j c -> (a p) j c"),
                                     split[:, par].rearrange("p j s h -> p j (s h)")).then_inc(scores_out[par], 16)
                        if not last:
                            sp.dma_start(xt[:, par], xT[:, :, bass.ds((i * 2 + par + 2) * GN, GN)]).then_inc(xt_in[par], 16)

                with sp.Fori(0, PAIRS - 1) as i:
                    step(i, False)
                step(PAIRS - 1, True)
                sp.wait_ge(pad_ready, 1)
                sp.dma_start(S.stgt[N:NA, :], pad[:, :]).then_inc(pad_out, 16)
                sp.wait_ge(pad_out, 16)
                sp.wait_ge(smax_ready, 1)
                sp.dma_start(S.smax.rearrange("(p h) -> p h", h=HEADS), smax1[:, :]).then_inc(smax_out, 16)
                sp.wait_ge(smax_out, 16)
                sp.dma_start(smaxall[:, :], S.smax.partition_broadcast(TP)).then_inc(smax_in, 16)
                sp.wait_ge(span_ready, 1)
                sp.dma_start(S.low.rearrange("(p j) -> p j", j=2), lowhigh[:, 0]).then_inc(span_out, 16)
                sp.dma_start(S.span.rearrange("(p j) -> p j", j=2), span[:, :]).then_inc(span_out, 16)
                sp.wait_ge(span_out, 32)
                sp.dma_start(K.low[:, :], S.low.partition_broadcast(128)).then_inc(base_in, 16)
                sp.dma_start(spanrow[:, :], S.span.rearrange("(a n) -> a n", a=1)).then_inc(span_in, 16)
                sp.wait_ge(hist_ready, 1)
                sp.dma_start(S.deg.rearrange("(h l) -> h l", l=LO), hist[:, :]).then_inc(hist_out, 16)
                sp.wait_ge(hist_out, 16)
                sp.wait_ge(base_in, 16)
                for par in range(2):
                    sp.wait_ge(rows_out[par], 16 * PAIRS)
                    sp.wait_ge(scores_out[par], 16 * PAIRS)

            @block.tensor
            def _(pe):
                pe.wait_ge(weights_in, 48)
                for half in range(2):
                    for k in range(2):
                        last = nc.tensor.matmul(psw[:, half], gatw[:, k, half * 128:(half + 1) * 128], ablk[:, k],
                                                start=(k == 0), stop=(k == 1))
                last.then_inc(vw_done, 1)
                pe.wait_ge(vw_copied, 1)

                def step(i, first):
                    for par in range(2):
                        pe.wait_ge(xt_in[par], (i + 1) * 16)
                        for j in range(G):
                            if not (first and par == 0):
                                pe.wait_ge(proj_copied, i * (2 * G) + (par - 1) * G + j + 1)
                            for k in range(2):
                                last = nc.tensor.matmul(psr[j][:, :], xt[:, par, k, j * TP:(j + 1) * TP], waug[:, k],
                                                        start=(k == 0), stop=(k == 1))
                            last.then_inc(proj_done, 1)

                step(0, True)
                with pe.Fori(1, PAIRS) as i:
                    step(i, False)

                def hist_step(i, par, first, final):
                    pe.wait_ge(oh_ready, i * 2 + par + 1)
                    for c in range(HC):
                        last = nc.tensor.matmul(psh[:, :], ohhi[:, par, c], ohlo[:, par, c],
                                                start=(first and c == 0), stop=(final and c == HC - 1))
                    last.then_inc(oh_used, 1)

                for par in range(2):
                    hist_step(0, par, par == 0, False)
                with pe.Fori(1, HSTEPS // 2 - 1) as i:
                    for par in range(2):
                        hist_step(i, par, False, False)
                for par in range(2):
                    hist_step(HSTEPS // 2 - 1, par, False, par == 1)

            @block.scalar
            def _(act):
                act.wait_ge(vw_done, 1)
                act.wait_ge(weights_in, 48)
                act.copy(waug[:, :, D:], psw[:, :, :]).then_inc(vw_copied, 1)

                def step(i, first):
                    for par in range(2):
                        if not first:
                            act.wait_ge(rows_out[par], i * 16)
                            act.wait_ge(scores_out[par], i * 16)
                            act.wait_ge(rows_maxed, i * 2 + par - 1)
                        for j in range(G):
                            act.wait_ge(proj_done, i * (2 * G) + par * G + j + 1)
                            act.copy(rows[:, par, j], psr[j][:, :]).then_inc(proj_copied, 1)

                step(0, True)
                with act.Fori(1, PAIRS) as i:
                    step(i, False)
                act.wait_ge(oh_used, HSTEPS)
                act.copy(hist[:, :], psh[:, :]).then_inc(hist_ready, 1)

            @block.vector
            def _(v):
                link = Link(v, link_v)
                v.wait_ge(const_in, 64)
                v.wait_ge(dst_in, 16)
                v.tensor_reduce(lowhigh[:, 0], dst2[:, :, :], axis=AX.X, op=ALU.min)
                link(v.tensor_reduce(lowhigh[:, 1], dst2[:, :, :], axis=AX.X, op=ALU.max))
                v.tensor_tensor(span[:, :], lowhigh[:, 1], lowhigh[:, 0], ALU.subtract).then_inc(span_ready, 1)
                v.wait_ge(src_in, 16)
                v.tensor_scalar(hi[:, :], srcs[:, :], 6, None, ALU.logical_shift_right)
                link(v.tensor_scalar(lo[:, :], srcs[:, :], LO - 1, None, ALU.bitwise_and))
                link(v.memset(smax5[:, :, :], NEG))

                def row_max(i, first):
                    link.restart()
                    for par in range(2):
                        v.wait_ge(proj_copied, i * (2 * G) + (par + 1) * G)
                        if not first:
                            v.wait_ge(scores_out[par], i * 16)
                        left = rows[:, par, :, ROW:]
                        for c in range(SPLITS):
                            link(v.tensor_copy(split[:, par, :, c], left))
                            if c < SPLITS - 1:
                                link(v.tensor_tensor(rest[:, :, :], left, split[:, par, :, c], ALU.subtract))
                                left = rest[:, :, :]
                        v.tensor_tensor(smax5[:, :, :], smax5[:, :, :], rows[:, par, :, D:D + HEADS], ALU.max).then_inc(rows_maxed, 1)
                        v.wait_ge(rows_maxed, i * 2 + par + 1)

                v.memset(pad[:, :], 0.0).then_inc(pad_ready, 1)
                row_max(0, True)
                with v.Fori(1, PAIRS) as i:
                    row_max(i, False)
                link.restart()
                v.tensor_reduce(smax1[:, :], smax5[:, :, :].rearrange("p g h -> p h g"), axis=AX.X, op=ALU.max).then_inc(smax_ready, 1)

                def hist_step(i, par, first):
                    if not first:
                        v.wait_ge(oh_used, i * 2 + par - 1)
                    cols = bass.ds((i * 2 + par) * HC, HC)
                    v.tensor_tensor(ohhi[:, par], hi[:, cols].unsqueeze(2).to_broadcast([TP, HC, HI]),
                                    K.iota[0:TP, 0:HI].unsqueeze(1).to_broadcast([TP, HC, HI]), ALU.is_equal)
                    v.tensor_tensor(ohlo[:, par], lo[:, cols].unsqueeze(2).to_broadcast([TP, HC, LO]),
                                    K.iota[0:TP, 0:LO].unsqueeze(1).to_broadcast([TP, HC, LO]), ALU.is_equal).then_inc(oh_ready, 1)

                for par in range(2):
                    hist_step(0, par, True)
                with v.Fori(1, HSTEPS // 2) as i:
                    for par in range(2):
                        hist_step(i, par, False)
                v.wait_ge(smax_in, 16)
                v.tensor_reduce(K.smax[:, :], smaxall[:, :].rearrange("p (q h) -> p h q", h=HEADS), axis=AX.X, op=ALU.max)
                v.wait_ge(span_in, 16)
                link(v.tensor_reduce(widest[:, :], spanrow[:, :], axis=AX.X, op=ALU.max))
                link(v.tensor_scalar(reach[:, :], K.steps[:, :], widest[:, 0:1], None, ALU.is_le))
                link(v.tensor_reduce(nrounds[:, :], reach[:, :], axis=AX.X, op=ALU.add))
                link(v.tensor_copy(K.rounds[:, :], nrounds[:, :]))
        M.close()


def ranks_block(nc, A, S, K):
    with ExitStack() as stack:
        M = Parts(nc, stack, "rank_")
        total = M.sb("total", [TP, TILES])
        xrows = M.sb("xrows", [TP, TILES, D])
        x_in, rank_ready, scattered, link_v = (M.sem(n) for n in ("x_in", "rank_ready", "scattered", "link_v"))

        with nc.Block() as block:
            @block.sync
            def _(sp):
                sp.dma_start(xrows[:, :, :], A.x.rearrange("(t p) c -> p t c", p=TP)).then_inc(x_in, 16)

            @block.gpsimd
            def _(pool):
                pool.wait_ge(x_in, 16)
                pool.wait_ge(rank_ready, 1)
                for t in range(TILES):
                    pool.indirect_dma_start(S.xs, bass.IndirectOffsetOnAxis(ap=K.rank[:, t:t + 1], axis=0),
                                            xrows[:, t, :], None).then_inc(scattered, 16)
                pool.wait_ge(scattered, 16 * TILES)

            @block.vector
            def _(v):
                link = Link(v, link_v)
                link(v.tensor_reduce(total[:, :], K.smaller[:, :].rearrange("p (t u) -> p t u", u=4), axis=AX.X, op=ALU.add))
                v.tensor_tensor(K.rank[:, :], total[:, :], K.ties[:, :], ALU.add).then_inc(rank_ready, 1)
        M.close()


def mamba_block(nc, A, S, K):
    LOG1P = [-0.0031760570127516985, 0.019542528316378593, -0.05637361481785774, 0.10543623566627502, -0.1526966691017151,
             0.1966327428817749, -0.24951615929603577, 0.33329710364341736, -0.49999892711639404, 1.0]
    PROJECT, GATES, SCAN, LEAVE = range(4)
    TURNS = NCH + LEAVE
    PEEL = LEAVE + 1
    LOOPS = (NCH - 2 - PEEL) // 2
    assert PEEL % 2 == 0
    BC = 32
    with ExitStack() as stack:
        M = Parts(nc, stack, "mam_")
        in_w = M.sb("in_w", [128, 2, 2 * D])
        x_w = M.sb("x_w", [128, 2, 128])
        dt_w = M.sb("dt_w", [DTR, D])
        out_w = M.sb("out_w", [128, 2, D])
        conv_w = M.sb("conv_w", [128, 2, DCONV])
        conv_b = M.sb("conv_b", [128, 2, 1])
        dt_b = M.sb("dt_b", [128, 2, 1])
        d_par = M.sb("d_par", [128, 2, 1])
        a_log = M.sb("a_log", [128, 2, DSTATE])
        a_neg = M.sb("a_neg", [128, 2, DSTATE])
        state = M.sb("state", [128, 2, DSTATE])
        pick = M.sb("pick", [128, BC], BF16)
        xr = M.sb("xr", [TP, CT, D])
        xT = M.sb("xT", [128, 2, 2, CH])
        xin = M.sb("xin", [128, 2, DCONV - 1 + CH])
        conv = M.sb("conv", [128, 2, CH])
        tconv = M.sb("tconv", [128, 2, CH])
        xc = M.sb("xc", [128, 2, 2, CH])
        z = M.sb("z", [128, 2, CH])
        tz = M.sb("tz", [128, 2, CH])
        zs = M.sb("zs", [128, 2, 2, CH])
        dt_rows = M.sb("dt_rows", [DTR, CH])
        parts = M.sb("parts", [128, 2, CH], BF16)
        rest = M.sb("rest", [128, CH])
        mag = M.sb("mag", [128, 2, CH])
        pos = M.sb("pos", [128, 2, CH])
        series = M.sb("series", [128, 2, CH])
        square = M.sb("square", [128, 2, CH])
        pair = K.den_room[:, 0:4 * 2 * CH].rearrange("p (q k n) -> p q k n", q=4, k=2)
        h = [K.den_room[:, at * 2 * CH:(at + 1) * 2 * CH].rearrange("p (k n) -> p k n", k=2) for at in (4, 5)]
        dt = M.sb("dt", [128, 2, 2, CH])
        dtx = M.sb("dtx", [128, 2, 2, CH])
        decay = M.sb("decay", [128, 2, 2, CH])
        bx = M.sb("bx", [128, 2, 2, CH])
        hc = M.sb("hc", [128, 2, 2, CH])
        y = M.sb("y", [128, 2, CH])
        yrows = M.sb("yrows", [TP, CT, D])
        psA = M.ps("psA", [128, 2, 512])
        psB = M.ps("psB", [128, 512])
        psC = M.ps("psC", [128, 512])
        psY = M.ps("psY", [128, 2, 512])
        psO = M.ps("psO", [TP, CT, D])

        sems = lambda *names: (M.sem(n) for n in names)
        params_in, pad_ready, init_ready, a_ready = sems("params_in", "pad_ready", "init_ready", "a_ready")
        x_in, x_turned, xT_ready, main_done, main_copied = sems("x_in", "x_turned", "xT_ready", "main_done", "main_copied")
        z_done, z_left, z_copied, zs_ready, conv_ready, tanh_ready, xc_ready = sems(
            "z_done", "z_left", "z_copied", "zs_ready", "conv_ready", "tanh_ready", "xc_ready")
        dbc_done, part1_ready, rest1_ready, part2_ready, rest2_ready, parts_ready = sems(
            "dbc_done", "part1_ready", "rest1_ready", "part2_ready", "rest2_ready", "parts_ready")
        dt_done, mag_ready, pair_ready, dt_ready, dtx_ready = sems("dt_done", "mag_ready", "pair_ready", "dt_ready", "dtx_ready")
        decay_ready, b_done, c_done, bx_ready, scanned, hc_ready, y_summed = sems(
            "decay_ready", "b_done", "c_done", "bx_ready", "scanned", "hc_ready", "y_summed")
        y_left, y_ready, out_done, out_copied, stored = sems("y_left", "y_ready", "out_done", "out_copied", "stored")
        den_out, den_back = sems("den_out", "den_back")
        link_v, link_a, link_g, ticks = sems("link_v", "link_a", "link_g", "ticks")

        def hold(eng, sem, value):
            eng.wait_ge(sem, value)
            eng.sem_inc(ticks, 1)

        def turns(eng, turn):
            def run(i, u):
                known = isinstance(i, int)
                turn(i, u, lambda lag: not known or 0 <= i - lag < NCH,
                     lambda lag: N - (NCH - 1) * CH if known and i - lag == NCH - 1 else CH)

            for i in range(PEEL):
                run(i, i % 2)
            with eng.Fori(0, LOOPS) as q:
                for u in range(2):
                    run(q * 2 + (PEEL + u), u)
            for i in range(PEEL + 2 * LOOPS, TURNS):
                run(i, i % 2)

        def later(i, n):
            return not isinstance(i, int) or i >= n

        with nc.Block() as block:
            @block.sync
            def _(sp):
                sp.dma_start(S.den, K.den[:, :]).then_inc(den_out, 16)
                for t, a in ((in_w, A.in_wT), (out_w, A.out_wT)):
                    sp.dma_start(t[:, :, :], a.rearrange("(k p) n -> p k n", p=128)).then_inc(params_in, 16)
                x_cols = A.x_wT.rearrange("(k p) n -> p k n", p=128)
                sp.wait_ge(pad_ready, 1)
                sp.dma_start(x_w[:, :, 0:DTR], x_cols[:, :, 0:DTR]).then_inc(params_in, 16)
                for place in (32, 64, 96):
                    sp.dma_start(x_w[:, :, place:place + BC], x_cols[:, :, DTR:DTR + BC]).then_inc(params_in, 16)
                sp.dma_start(dt_w[:, :], A.dt_wT).then_inc(params_in, 16)
                for t, a in ((conv_w, A.conv_w), (conv_b, A.conv_b), (dt_b, A.dt_b), (d_par, A.d_param), (a_log, A.a_log)):
                    sp.dma_start(t[:, :, :], a).then_inc(params_in, 16)

                def rows_of(dram, c, tiles):
                    return dram[bass.ds(c * CH, tiles * TP)].rearrange("(j p) f -> p j f", p=TP)

                sp.dma_start(xr[:, :, :], rows_of(S.xs, 0, CT)).then_inc(x_in, 16)

                def turn(i, u, on, width):
                    if on(PROJECT) and not (isinstance(i, int) and i + 1 >= NCH):
                        tiles = width(PROJECT - 1) // TP
                        hold(sp, x_turned, i + 1)
                        sp.dma_start(xr[:, 0:tiles], rows_of(S.xs, i + 1, tiles)).then_inc(x_in, 16)
                    if on(LEAVE):
                        tiles = width(LEAVE) // TP
                        hold(sp, out_copied, i - LEAVE + 1)
                        sp.dma_start(rows_of(S.ys, i - LEAVE, tiles), yrows[:, 0:tiles]).then_inc(stored, 16)

                turns(sp, turn)
                sp.wait_ge(stored, 16 * NCH)
                sp.wait_ge(dtx_ready, NCH)
                sp.dma_start(K.den[:, :], S.den).then_inc(den_back, 16)
                sp.wait_ge(den_back, 16)

            @block.tensor
            def _(pe):
                pe.wait_ge(params_in, 16 * 12)
                pe.wait_ge(init_ready, 1)

                def turn(i, u, on, width):
                    a, b, c, e = (i - lag for lag in range(4))

                    def turn_rows():
                        w = width(PROJECT)
                        pe.wait_ge(x_in, (a + 1) * 16)
                        if later(i, 2):
                            pe.wait_ge(z_left, i - 1)
                        elif i == 1:
                            pe.wait_ge(main_copied, 1)
                        for j in range(w // TP):
                            for k in range(2):
                                last = nc.tensor.transpose(psA[:, k, j * TP:(j + 1) * TP], xr[:, j, k * 128:(k + 1) * 128],
                                                           K.ident[0:TP, 0:TP])
                        last.then_inc(x_turned, 1)

                    def project(part, m, slot, w):
                        for k in range(2):
                            last = nc.tensor.matmul(psA[:, m, 0:w], in_w[:, k, (2 * part + m) * 128:(2 * part + m + 1) * 128],
                                                    xT[:, slot, k, 0:w], start=(k == 0), stop=(k == 1))
                        return last

                    def project_main_0():
                        pe.wait_ge(xT_ready, a + 1)
                        project(0, 0, u, width(PROJECT))

                    def project_main_1():
                        project(0, 1, u, width(PROJECT)).then_inc(main_done, 1)

                    def project_z_0():
                        pe.wait_ge(mag_ready, b + 1)
                        project(1, 0, 1 - u, width(GATES))

                    def project_z_1():
                        project(1, 1, 1 - u, width(GATES)).then_inc(z_done, 1)

                    def project_dbc():
                        w = width(GATES)
                        if on(PROJECT):
                            pe.wait_ge(main_copied, a + 1)
                        elif on(GATES):
                            pe.wait_ge(z_left, b)
                        pe.wait_ge(xc_ready, b + 1)
                        for k in range(2):
                            last = nc.tensor.matmul(psA[:, 0, 0:w], x_w[:, k], xc[:, 1 - u, k, 0:w], start=(k == 0), stop=(k == 1))
                        last.then_inc(dbc_done, 1)

                    def project_dt():
                        w = width(GATES)
                        pe.wait_ge(rest1_ready, b + 1)
                        for m in range(2):
                            last = nc.tensor.matmul(psA[:, m, 0:w], dt_w[:, m * 128:(m + 1) * 128], dt_rows[:, 0:w], start=True, stop=True)
                        last.then_inc(dt_done, 1)

                    def project_out(j):
                        for k in range(2):
                            last = nc.tensor.matmul(psO[:, j], y[:, k, j * TP:(j + 1) * TP], out_w[:, k], start=(k == 0), stop=(k == 1))
                        return last

                    def project_out_first():
                        pe.wait_ge(y_ready, e + 1)
                        if later(i, LEAVE + 1):
                            pe.wait_ge(out_copied, e)
                        for j in range(width(LEAVE) // TP // 2):
                            project_out(j)

                    def project_out_last():
                        tiles = width(LEAVE) // TP
                        for j in range(tiles // 2, tiles):
                            last = project_out(j)
                        last.then_inc(out_done, 1)

                    def spread(bank, n, row, w, done):
                        nc.tensor.matmul(bank[:, 0:w], pick[:, row:row + 1].to_broadcast([128, 128]),
                                         parts[:, u, 0:w], start=True, stop=True).then_inc(done, 1)

                    def spread_b(n):
                        if n or later(i, SCAN + 1):
                            pe.wait_ge(bx_ready, c * DSTATE + n)
                        spread(psB, n, n, width(SCAN), b_done)

                    def sum_state(chunk, n, w):
                        pe.wait_ge(hc_ready, chunk * DSTATE + n + 1)
                        for half in range(2):
                            last = nc.tensor.matmul(psY[:, half, 0:w], K.ident[:, :], hc[:, n % 2, half, 0:w],
                                                    start=(n == 0), stop=(n == DSTATE - 1), skip_group_check=True)
                        last.then_inc(y_summed, 1)

                    pieces = {n: [] for n in range(DSTATE)}
                    if on(PROJECT):
                        pieces[0].append(turn_rows)
                        pieces[2].append(project_main_0)
                        pieces[3].append(project_main_1)
                    if on(GATES):
                        pieces[5].append(project_dbc)
                        pieces[7].append(project_dt)
                        pieces[11].append(project_z_0)
                        pieces[12].append(project_z_1)
                    if on(LEAVE):
                        pieces[8].append(project_out_first)
                        pieces[10].append(project_out_last)
                    if on(SCAN):
                        pe.wait_ge(parts_ready, c + 1)
                        spread_b(0)
                    if on(LEAVE):
                        sum_state(e, DSTATE - 1, width(LEAVE))
                    for n in range(DSTATE):
                        if on(SCAN):
                            if n + 1 < DSTATE:
                                spread_b(n + 1)
                            if n or later(i, SCAN + 1):
                                pe.wait_ge(hc_ready, c * DSTATE + n)
                            spread(psC, n, DSTATE + n, width(SCAN), c_done)
                            if n:
                                if n == 1 and later(i, SCAN + 1):
                                    pe.wait_ge(y_left, c)
                                sum_state(c, n - 1, width(SCAN))
                        for piece in pieces[n]:
                            piece()

                turns(pe, turn)

            @block.scalar
            def _(act):
                link = Link(act, link_a)
                act.wait_ge(params_in, 16 * 12)
                act.wait_ge(den_out, 16)
                act.activation(a_neg[:, :, :], a_log[:, :, :], ACT.Exp).then_inc(a_ready, 1)
                act.wait_ge(init_ready, 1)

                def turn(i, u, on, width):
                    a, b, c, e = (i - lag for lag in range(4))
                    link.restart()

                    def copy_rows():
                        w = width(PROJECT)
                        act.wait_ge(x_turned, a + 1)
                        act.copy(xT[:, u, :, 0:w], psA[:, :, 0:w]).then_inc(xT_ready, 1)

                    def copy_main():
                        w = width(PROJECT)
                        if later(i, 1):
                            act.wait_ge(conv_ready, a)
                            link(act.copy(xin[:, :, 0:DCONV - 1], xin[:, :, CH:]))
                        act.wait_ge(main_done, a + 1)
                        act.copy(xin[:, :, DCONV - 1:DCONV - 1 + w], psA[:, :, 0:w]).then_inc(main_copied, 1)

                    def gate_conv():
                        w = width(GATES)
                        act.wait_ge(conv_ready, b + 1)
                        if later(i, 2):
                            act.wait_ge(xc_ready, b)
                        link(act.activation(tconv[:, :, 0:w], conv[:, :, 0:w], ACT.Tanh))
                        act.activation(tconv[:, :, 0:w], tconv[:, :, 0:w], ACT.Copy, bias=1.0).then_inc(tanh_ready, 1)

                    def copy_z():
                        w = width(GATES)
                        act.wait_ge(z_done, b + 1)
                        if later(i, 2):
                            act.wait_ge(zs_ready, b)
                        link(act.activation(tz[:, :, 0:w], psA[:, :, 0:w], ACT.Tanh, scale=0.5))
                        act.activation(z[:, :, 0:w], psA[:, :, 0:w], ACT.Copy, scale=0.5).then_inc(z_left, 1)
                        act.activation(tz[:, :, 0:w], tz[:, :, 0:w], ACT.Copy, bias=1.0).then_inc(z_copied, 1)

                    def part1():
                        w = width(GATES)
                        act.wait_ge(dbc_done, b + 1)
                        act.copy(dt_rows[:, 0:w], psA[0:DTR, 0, 0:w])
                        act.copy(parts[:, 1 - u, 0:w], psA[:, 0, 0:w]).then_inc(part1_ready, 1)

                    def part2():
                        w = width(GATES)
                        act.wait_ge(rest1_ready, b + 1)
                        act.copy(parts[64:128, 1 - u, 0:w], rest[64:128, 0:w]).then_inc(part2_ready, 1)

                    def part3():
                        w = width(GATES)
                        act.wait_ge(rest2_ready, b + 1)
                        act.copy(parts[96:128, 1 - u, 0:w], rest[96:128, 0:w]).then_inc(parts_ready, 1)

                    def magnitude():
                        w = width(GATES)
                        act.wait_ge(dt_done, b + 1)
                        if later(i, 2):
                            act.wait_ge(dt_ready, b)
                        for half in range(2):
                            last = act.activation(mag[:, half, 0:w], psA[:, half, 0:w], ACT.Abs, bias=dt_b[:, half])
                        link(last)
                        for half in range(2):
                            act.activation(pos[:, half, 0:w], psA[:, half, 0:w], ACT.Relu, bias=dt_b[:, half])
                        link(act.activation(mag[:, :, 0:w], mag[:, :, 0:w], ACT.Exp, scale=-1.0))
                        act.activation(square[:, :, 0:w], mag[:, :, 0:w], ACT.Square)
                        act.activation(series[:, :, 0:w], mag[:, :, 0:w], ACT.Copy, scale=LOG1P[0], bias=LOG1P[1]).then_inc(mag_ready, 1)

                    def pairs(degrees):
                        w = width(GATES)
                        for q in degrees:
                            act.activation(pair[:, q, :, 0:w], mag[:, :, 0:w], ACT.Copy, scale=LOG1P[8 - 2 * q], bias=LOG1P[9 - 2 * q]
                                           ).then_inc(pair_ready, 1)

                    def copy_out():
                        tiles = width(LEAVE) // TP
                        act.wait_ge(out_done, e + 1)
                        if later(i, LEAVE + 1):
                            act.wait_ge(stored, e * 16)
                        act.copy(yrows[:, 0:tiles], psO[:, 0:tiles]).then_inc(out_copied, 1)

                    pieces = {n: [] for n in range(DSTATE)}
                    if on(PROJECT):
                        pieces[2].append(copy_rows)
                        pieces[5].append(copy_main)
                    if on(LEAVE):
                        pieces[12].append(copy_out)
                    if on(GATES):
                        for n, piece in ((1, gate_conv), (7, part1), (8, part2), (9, magnitude), (10, lambda: pairs((3, 2))), (11, lambda: pairs((1, 0))),
                                         (11, part3), (14, copy_z)):
                            pieces[n].append(piece)
                    for n in range(DSTATE):
                        if on(SCAN):
                            w = width(SCAN)
                            if n == 0:
                                act.wait_ge(dt_ready, c + 1)
                            if n >= 2 or later(i, SCAN + 1):
                                act.wait_ge(scanned, c * DSTATE + n - 1)
                            for half in range(2):
                                last = act.activation(decay[:, n % 2, half, 0:w], dt[:, u, half, 0:w], ACT.Exp, scale=a_neg[:, half, n:n + 1])
                            last.then_inc(decay_ready, 1)
                        for piece in pieces[n]:
                            piece()

                turns(act, turn)

            @block.gpsimd
            def _(pool):
                link = Link(pool, link_g)
                pool.memset(x_w[:, :, :], 0.0).then_inc(pad_ready, 1)
                pool.wait_ge(init_ready, 1)
                pool.wait_ge(den_out, 16)

                def turn(i, u, on, width):
                    a, b, c, e = (i - lag for lag in range(4))
                    link.restart()
                    if on(GATES):
                        w = width(GATES)
                        hold(pool, tanh_ready, b + 1)
                        if later(i, LEAVE):
                            hold(pool, y_ready, b - 1)
                        pool.tensor_tensor(xc[:, 1 - u, :, 0:w], tconv[:, :, 0:w], conv[:, :, 0:w], ALU.mult).then_inc(xc_ready, 1)
                        hold(pool, mag_ready, b + 1)
                        s = series[:, :, 0:w]
                        for q in (3, 2, 1, 0):
                            link(pool.tensor_tensor(s, s, square[:, :, 0:w], ALU.mult))
                            hold(pool, pair_ready, b * 4 + 4 - q)
                            link(pool.tensor_tensor(s, s, pair[:, q, :, 0:w], ALU.add))
                        link(pool.tensor_tensor(s, s, mag[:, :, 0:w], ALU.mult))
                        if later(i, LEAVE):
                            hold(pool, decay_ready, (b - 1) * DSTATE)
                            hold(pool, bx_ready, (b - 1) * DSTATE)
                        pool.tensor_tensor(dt[:, 1 - u, :, 0:w], s, pos[:, :, 0:w], ALU.add).then_inc(dt_ready, 1)
                        hold(pool, dt_ready, b + 1)
                        pool.tensor_tensor(dtx[:, 1 - u, :, 0:w], dt[:, 1 - u, :, 0:w], xc[:, 1 - u, :, 0:w], ALU.mult).then_inc(dtx_ready, 1)
                        hold(pool, z_copied, b + 1)
                        pool.tensor_tensor(zs[:, 1 - u, :, 0:w], tz[:, :, 0:w], z[:, :, 0:w], ALU.mult).then_inc(zs_ready, 1)

                turns(pool, turn)

            @block.vector
            def _(v):
                link = Link(v, link_v)
                v.memset(state[:, :, :], 0.0)
                v.memset(xin[:, :, 0:DCONV - 1], 0.0)
                link(v.tensor_tensor(rest[:, 0:BC], K.ident[:, 32:64], K.ident[:, 64:96], ALU.add))
                v.tensor_tensor(pick[:, :], rest[:, 0:BC], K.ident[:, 96:128], ALU.add)
                v.wait_ge(params_in, 16 * 12)
                v.tensor_scalar(conv_w[:, :, :], conv_w[:, :, :], 0.5, None, ALU.mult)
                v.tensor_scalar(conv_b[:, :, :], conv_b[:, :, :], 0.5, None, ALU.mult)
                v.wait_ge(a_ready, 1)
                v.tensor_scalar(a_neg[:, :, :], a_neg[:, :, :], -1.0, None, ALU.mult).then_inc(init_ready, 1)
                v.wait_ge(init_ready, 1)

                def turn(i, u, on, width):
                    a, b, c, e = (i - lag for lag in range(4))
                    link.restart()

                    def rest1():
                        w = width(GATES)
                        v.wait_ge(part1_ready, b + 1)
                        v.tensor_tensor(rest[64:128, 0:w], psA[64:128, 0, 0:w], parts[64:128, 1 - u, 0:w], ALU.subtract).then_inc(rest1_ready, 1)

                    def rest2():
                        w = width(GATES)
                        v.wait_ge(part2_ready, b + 1)
                        v.tensor_tensor(rest[96:128, 0:w], rest[96:128, 0:w], parts[96:128, 1 - u, 0:w], ALU.subtract).then_inc(rest2_ready, 1)

                    def convolve():
                        w = width(PROJECT)
                        v.wait_ge(main_copied, a + 1)
                        if on(GATES):
                            v.wait_ge(xc_ready, b + 1)
                        for half in range(2):
                            last = v.tensor_scalar(conv[:, half, 0:w], xin[:, half, 3:3 + w], conv_w[:, half, 3:4], conv_b[:, half], ALU.mult, ALU.add)
                        link(last)
                        for k in range(DCONV - 1):
                            for half in range(2):
                                last = v.scalar_tensor_tensor(conv[:, half, 0:w], xin[:, half, k:k + w], conv_w[:, half, k:k + 1],
                                                              conv[:, half, 0:w], ALU.mult, ALU.add)
                            if k < DCONV - 2:
                                link(last)
                        last.then_inc(conv_ready, 1)

                    def finish():
                        w = width(LEAVE)
                        v.wait_ge(y_summed, (e + 1) * DSTATE)
                        v.wait_ge(zs_ready, e + 1)
                        if later(i, LEAVE + 1):
                            v.wait_ge(out_done, e)
                        for half in range(2):
                            last = v.scalar_tensor_tensor(y[:, half, 0:w], xc[:, 1 - u, half, 0:w], d_par[:, half], psY[:, half, 0:w], ALU.mult, ALU.add)
                        last.then_inc(y_left, 1)
                        v.wait_ge(y_left, e + 1)
                        v.tensor_tensor(y[:, :, 0:w], y[:, :, 0:w], zs[:, 1 - u, :, 0:w], ALU.mult).then_inc(y_ready, 1)

                    def drive(n):
                        w = width(SCAN)
                        v.wait_ge(b_done, c * DSTATE + n + 1)
                        v.tensor_tensor(bx[:, n % 2, :, 0:w], dtx[:, u, :, 0:w], psB[:, 0:w].unsqueeze(1).to_broadcast([128, 2, w]), ALU.mult
                                        ).then_inc(bx_ready, 1)

                    if on(SCAN):
                        v.wait_ge(dtx_ready, c + 1)
                        drive(0)
                    for n in range(DSTATE):
                        if on(SCAN):
                            w = width(SCAN)
                            at = c * DSTATE + n + 1
                            v.wait_ge(bx_ready, at)
                            v.wait_ge(decay_ready, at)
                            if n >= 2 or later(i, SCAN + 1):
                                v.wait_ge(hc_ready, at - 2)
                            for half in range(2):
                                last = v.tensor_tensor_scan(h[n % 2][:, half, 0:w], decay[:, n % 2, half, 0:w], bx[:, n % 2, half, 0:w],
                                                            state[:, half, n:n + 1], ALU.mult, ALU.add)
                            last.then_inc(scanned, 1)
                            if n + 1 < DSTATE:
                                drive(n + 1)
                        if n == 0 and on(LEAVE):
                            finish()
                        if n == 5 and on(PROJECT):
                            convolve()
                        if n == 7 and on(GATES):
                            rest1()
                        if n == 9 and on(GATES):
                            rest2()
                        if on(SCAN):
                            v.wait_ge(scanned, at)
                            v.tensor_copy(state[:, :, n:n + 1], h[n % 2][:, :, w - 1:w])
                            v.wait_ge(c_done, at)
                            if n >= 2 or later(i, SCAN + 1):
                                v.wait_ge(y_summed, at - 2)
                            v.tensor_tensor(hc[:, n % 2, :, 0:w], h[n % 2][:, :, 0:w], psC[:, 0:w].unsqueeze(1).to_broadcast([128, 2, w]), ALU.mult
                                            ).then_inc(hc_ready, 1)

                turns(v, turn)
        M.close()


def edge_pass(nc, A, S, K, weighted):
    CREDIT = 4
    DONE = lambda n: n + 1 + CREDIT
    QUADS = NSB // 4
    PIECES = [(0, 1562), (1562, 3124), (3124, 4686), (4686, N)]
    assert QUADS == TILES
    table = S.proj if weighted else S.x1d
    width = ROW if weighted else D
    cols = ROW + 1 if weighted else D
    with ExitStack() as stack:
        M = Parts(nc, stack, "gat_" if weighted else "gcn_")
        base = M.sb("base", [128, NSB])
        base_i = M.sb("base_i", [1, NSB], I32)
        src = M.sb("src", [TP, 4, KB], I32)
        dst = M.sb("dst", [TP, 4, KB], I32)
        rows = M.sb("rows", [TP, 4, KB, width])
        rel = M.sb("rel", [TP, 4, KB])
        sel = M.sb("sel", [TP, 4, KB, W])
        part = M.sb("part", [W, 2, cols])
        psA = [M.ps(f"psA{i}", [W, 512]) for i in range(2)]
        psT = [M.ps(f"psT{i}", [128, 512]) for i in range(2)]
        if weighted:
            dstrow = M.sb("dstrow", [W, 2, EDGES_SB], I32)
            tscore = M.sb("tscore", [W, 2, SPLITS * HEADS], BF16)
            selT = M.sb("selT", [W, 2, EDGES_SB], BF16)
            tsum = M.sb("tsum", [TP, KB, HEADS])
            wrows = M.sb("wrows", [TP, 2, KB, cols])
            below = M.sb("below", [TP, KB])
            above = M.sb("above", [TP, KB])
            outside = M.sb("outside", [TP, 4, KB])
            score = M.sb("score", [TP, KB, HEADS])
            bound = M.sb("bound", [TP, KB, HEADS])
            masked = M.sb("masked", [TP, KB, HEADS])
            expo = M.sb("expo", [TP, 2, KB, HEADS])
            emax = M.sb("emax", [TP, KB, HEADS])
            emax1 = M.sb("emax1", [TP, 1])
            emaxall = M.sb("emaxall", [TP, TP])
            degrow = M.sb("degrow", [TILES, TP])
            noise = M.sb("noise", [TILES, TP])
            keyrow = M.sb("keyrow", [TILES, TP])
            keycol = M.sb("keycol", [TP, TILES])
            keys = M.sb("keys", [TP, N])
            tri = M.sb("tri", [TP, TP])
            seen = M.sb("seen", [TP, PIECES[-1][1] - PIECES[-1][0]], BF16)
            lowered = M.sb("lowered", [TP, 2, TP])
            psb = [M.ps(f"psb{i}", [TP, KB, SPLITS, HEADS]) for i in range(2)]

        src_in = [M.sem(f"src_in{i}") for i in range(4)]
        dst_in = [M.sem(f"dst_in{i}") for i in range(4)]
        dstrow_in = [M.sem(f"dstrow_in{i}") for i in range(2)]
        tscore_in = [M.sem(f"tscore_in{i}") for i in range(2)]
        rows_in = [M.sem(f"rows_in{i}") for i in range(4)]
        base_ready, sel_ready, b_done, scored, w_ready, weighed = (
            M.sem(n) for n in ("base_ready", "sel_ready", "b_done", "scored", "w_ready", "weighed"))
        summed, copied, turned, added = (M.sem(n) for n in ("summed", "copied", "turned", "added"))
        emax_ready, emax_out, emax_in = (M.sem(n) for n in ("emax_ready", "emax_out", "emax_in"))
        link_v, ticks, credited = M.sem("link_v"), M.sem("ticks"), M.sem("credited")
        key_parts_in, key_ready, key_out, keys_in, col_done, col_copied = (
            M.sem(n) for n in ("key_parts_in", "key_ready", "key_out", "keys_in", "col_done", "col_copied"))
        rows_used = weighed if weighted else summed

        def in_rounds(eng, before, step, after):
            turns = eng.value_load(K.rounds[0:1, 0:1], min_val=1, max_val=-(-N // W))
            with eng.Fori(0, turns) as r:
                before(r)
                for u in range(4):
                    step(r * QUADS, 0, u)
                with eng.Fori(1, QUADS - 1) as q:
                    for u in range(4):
                        step(r * QUADS + q, q, u)
                for u in range(4):
                    step(r * QUADS + QUADS - 1, QUADS - 1, u)
                after(r)

        def nothing(r):
            pass

        def hold(eng, sem, value):
            eng.wait_ge(sem, value)
            eng.sem_inc(ticks, 1)

        with nc.Block() as block:
            @block.sync
            def _(sp):
                if weighted:
                    sp.dma_start(degrow[:, :], S.deg[0:N].rearrange("(t p) -> t p", p=TP)).then_inc(key_parts_in, 16)
                    sp.dma_start(noise[:, :], A.node_vec.rearrange("(t p) -> t p", p=TP)).then_inc(key_parts_in, 16)
                    sp.dma_start(tri[:, :], A.tri).then_inc(key_parts_in, 16)
                    sp.wait_ge(key_ready, 1)
                    sp.dma_start(S.key.rearrange("(t p) -> t p", p=TP), keyrow[:, :]).then_inc(key_out, 16)
                    sp.wait_ge(key_out, 16)
                sp.wait_ge(credited, 1)

                def before(r):
                    hold(sp, base_ready, r + 1)
                    if weighted:
                        sp.dma_start(keys[:, :], S.key.partition_broadcast(TP)).then_inc(keys_in, 16)

                def step(m, q, u):
                    s = q * 4 + u
                    n = m * 4 + u
                    hold(sp, summed, DONE(n - 4))
                    sp.dma_start(src[:, u], A.src_cols[bass.ds(s, 1)].rearrange("a p k -> (a p) k")).then_inc(src_in[u], 16)
                    sp.dma_start(dst[:, u], A.dst_cols[bass.ds(s, 1)].rearrange("a p k -> (a p) k")).then_inc(dst_in[u], 16)
                    if weighted:
                        hold(sp, b_done, DONE(n - 2))
                        at = sp.value_load(base_i[0:1, bass.ds(s, 1)], min_val=0, max_val=N)
                        sp.dma_start(dstrow[:, u % 2], A.dst[bass.ds(s * EDGES_SB, EDGES_SB)].partition_broadcast(W)
                                     ).then_inc(dstrow_in[u % 2], 16)
                        sp.dma_start(tscore[:, u % 2], S.stgt[bass.ds(at, W), :]).then_inc(tscore_in[u % 2], 16)

                in_rounds(sp, before, step, nothing)
                if weighted:
                    sp.wait_ge(emax_ready, 1)
                    sp.dma_start(S.emax.rearrange("(p a) -> p a", a=1), emax1[:, :]).then_inc(emax_out, 16)
                    sp.wait_ge(emax_out, 16)
                    sp.dma_start(emaxall[:, :], S.emax.partition_broadcast(TP)).then_inc(emax_in, 16)

            @block.gpsimd
            def _(pool):
                pool.wait_ge(credited, 1)

                def step(m, q, u):
                    s = q * 4 + u
                    hold(pool, src_in[u], (m + 1) * 16)
                    hold(pool, rows_used, DONE(m * 4 + u - 4))
                    for k in range(KB):
                        pool.indirect_dma_start(rows[:, u, k, :], None, table,
                                                bass.IndirectOffsetOnAxis(ap=src[:, u, k:k + 1], axis=0)).then_inc(rows_in[u], 16)

                in_rounds(pool, nothing, step, nothing)

            @block.tensor
            def _(pe):
                if weighted:
                    pe.wait_ge(key_ready, 1)
                    nc.tensor.transpose(psT[0][0:TP, 0:TILES], keyrow[:, :],
                                        K.ident[0:TILES, 0:TILES]).then_inc(col_done, 1)
                    pe.wait_ge(col_copied, 1)
                pe.wait_ge(credited, 1)

                def target_scores(m, u):
                    n = m * 4 + u
                    pe.wait_ge(sel_ready, n + 1)
                    pe.wait_ge(tscore_in[u % 2], (m * 2 + u // 2 + 1) * 16)
                    pe.wait_ge(scored, DONE(n - 2))
                    for k in range(KB):
                        last = nc.tensor.matmul(psb[u % 2][:, k], selT[:, u % 2, k * TP:(k + 1) * TP],
                                                tscore[:, u % 2], start=True, stop=True)
                    last.then_inc(b_done, 1)

                def before(r):
                    if weighted:
                        target_scores(r * QUADS, 0)

                def step(m, q, u):
                    s = q * 4 + u
                    n = m * 4 + u
                    if weighted and not (isinstance(s, int) and s == NSB - 1):
                        target_scores(m + (u + 1) // 4, (u + 1) % 4)
                    if weighted:
                        pe.wait_ge(weighed, DONE(n))
                    else:
                        pe.wait_ge(sel_ready, n + 1)
                        pe.wait_ge(rows_in[u], (m + 1) * 16 * KB)
                    pe.wait_ge(copied, DONE(n - 2))
                    for k in range(KB):
                        right = wrows[:, u % 2, k] if weighted else rows[:, u, k]
                        last = nc.tensor.matmul(psA[u % 2][:, 0:cols], sel[:, u, k], right, start=(k == 0), stop=(k == KB - 1))
                    last.then_inc(summed, 1)
                    hold(pe, added, DONE(n - 2))
                    hold(pe, copied, DONE(n))
                    for half in range(2):
                        last = nc.tensor.transpose(psT[u % 2][:, half * W:(half + 1) * W], part[:, u % 2, half * 128:(half + 1) * 128],
                                                   K.ident[0:W, 0:W])
                    if weighted:
                        last = nc.tensor.transpose(psT[u % 2][0:HEADS + 1, 2 * W:3 * W], part[:, u % 2, D:], K.ident[0:W, 0:W])
                    last.then_inc(turned, 1)

                in_rounds(pe, before, step, nothing)

            @block.scalar
            def _(act):
                if weighted:
                    act.wait_ge(col_done, 1)
                    act.copy(keycol[:, :], psT[0][0:TP, 0:TILES]).then_inc(col_copied, 1)
                act.wait_ge(credited, 1)

                def copy_sums(n, u):
                    act.wait_ge(summed, DONE(n))
                    act.wait_ge(turned, DONE(n - 2))
                    act.copy(part[:, u % 2], psA[u % 2][:, 0:cols]).then_inc(copied, 1)

                def step(m, q, u):
                    n = m * 4 + u
                    if weighted:
                        act.wait_ge(scored, DONE(n))
                        act.wait_ge(summed, DONE(n - 2))
                        act.activation(wrows[:, u % 2, :, D:ROW], expo[:, u % 2], ACT.Exp).then_inc(w_ready, 1)
                    if not (isinstance(q, int) and q == 0 and u == 0):
                        copy_sums(n - 1, (u - 1) % 4)

                def after(r):
                    copy_sums((r + 1) * NSB - 1, 3)

                in_rounds(act, nothing, step, after)

            @block.vector
            def _(v):
                link = Link(v, link_v)
                for sem in (summed, b_done, copied, turned, added, scored, w_ready, weighed):
                    v.sem_inc(sem, CREDIT)
                link(v.tensor_copy(base[:, :], K.low[:, :]))
                if weighted:
                    v.memset(wrows[:, :, :, ROW:], 1.0)
                    v.memset(emax[:, :, :], NEG)
                    v.memset(K.den[:, :], 0.0)
                    link(v.memset(K.sums[:, :, :], 0.0))
                link(v.tensor_copy(base_i[:, :], base[0:1, :]))
                v.sem_inc(base_ready, 1)
                v.sem_inc(credited, 1)
                if weighted:
                    v.wait_ge(key_parts_in, 48)
                    v.tensor_tensor(keyrow[:, :], degrow[:, :], noise[:, :], ALU.add).then_inc(key_ready, 1)
                    v.wait_ge(col_copied, 1)

                def rank_piece(t, u):
                    a, b = PIECES[u]
                    key = keycol[:, bass.ds(t, 1)]
                    link(v.tensor_scalar(seen[:, 0:b - a], keys[:, a:b], key, 0.0, ALU.is_lt, ALU.add,
                                         accum_out=K.smaller[:, bass.ds(t * 4 + u, 1)]))
                    if u == 3:
                        own = keys[:, bass.ds(t * TP, TP)]
                        v.tensor_scalar(lowered[:, 0], own, 2.0 ** -24, None, ALU.mult)
                        v.tensor_scalar(lowered[:, 1], own, 0.0, -1e-30, ALU.is_equal, ALU.mult)
                        link(v.scalar_tensor_tensor(seen[:, 0:TP], own, key, tri[:, :], ALU.is_equal, ALU.mult,
                                                    accum_out=K.ties[:, bass.ds(t, 1)]))
                        link(v.scalar_tensor_tensor(lowered[:, 0], own, -2.0 ** -24, lowered[:, 0], ALU.mult, ALU.min))
                        link(v.tensor_tensor(own, own, lowered[:, 0], ALU.add))
                        link(v.tensor_tensor(own, own, lowered[:, 1], ALU.add))

                def select(m, s, u):
                    n = m * 4 + u
                    v.wait_ge(dst_in[u], (m + 1) * 16)
                    v.wait_ge(summed, DONE(n - 4))
                    link(v.tensor_scalar(rel[:, u], dst[:, u], base[0:TP, bass.ds(s, 1)], None, ALU.subtract))
                    out = v.tensor_tensor(sel[:, u], rel[:, u].unsqueeze(2).to_broadcast([TP, KB, W]),
                                          K.iota[0:TP, 0:W].unsqueeze(1).to_broadcast([TP, KB, W]), ALU.is_equal)
                    if weighted:
                        v.tensor_scalar(below[:, :], rel[:, u], 0.0, NEG / 4, ALU.is_lt, ALU.mult)
                        link(v.tensor_scalar(above[:, :], rel[:, u], float(W - 1), NEG / 4, ALU.is_gt, ALU.mult))
                        v.tensor_tensor(outside[:, u], below[:, :], above[:, :], ALU.add)
                        v.wait_ge(dstrow_in[u % 2], (m * 2 + u // 2 + 1) * 16)
                        v.wait_ge(b_done, DONE(n - 2))
                        out = v.tensor_scalar(selT[:, u % 2], dstrow[:, u % 2], base[0:W, bass.ds(s, 1)], K.pidx[0:W, 0:1],
                                              ALU.subtract, ALU.is_equal)
                    out.then_inc(sel_ready, 1)

                def scores(m, s, u):
                    n = m * 4 + u
                    v.wait_ge(b_done, DONE(n))
                    b = psb[u % 2]
                    link(v.tensor_reduce(tsum[:, :, :], b[:, :, :, :].rearrange("p k c h -> p k h c"), axis=AX.X, op=ALU.add))
                    b = tsum[:, :, :]
                    v.tensor_tensor(bound[:, :, :], b, K.smax[:, :].unsqueeze(1).to_broadcast([TP, KB, HEADS]), ALU.add)
                    v.wait_ge(rows_in[u], (m + 1) * 16 * KB)
                    link(v.tensor_tensor(score[:, :, :], rows[:, u, :, D:ROW], b, ALU.add))
                    v.scalar_tensor_tensor(bound[:, :, :], bound[:, :, :], 0.2, bound[:, :, :], ALU.mult, ALU.max)
                    link(v.scalar_tensor_tensor(score[:, :, :], score[:, :, :], 0.2, score[:, :, :], ALU.mult, ALU.max))
                    v.wait_ge(w_ready, DONE(n - 2))
                    v.tensor_tensor(expo[:, u % 2], score[:, :, :], bound[:, :, :], ALU.subtract).then_inc(scored, 1)
                    link(v.tensor_tensor(masked[:, :, :], score[:, :, :], outside[:, u].unsqueeze(2).to_broadcast([TP, KB, HEADS]), ALU.add))
                    link(v.tensor_tensor(emax[:, :, :], emax[:, :, :], masked[:, :, :], ALU.max))

                def window(s):
                    return v.value_load(base_i[0:1, bass.ds(s, 1)], min_val=0, max_val=N)

                def add_sums(m, u, at):
                    n = m * 4 + u
                    hold(v, turned, DONE(n))
                    there = K.sums[:, :, bass.ds(at, W)]
                    if weighted:
                        v.tensor_tensor(K.den[:, bass.ds(at, W)], K.den[:, bass.ds(at, W)], psT[u % 2][0:HEADS + 1, 2 * W:3 * W], ALU.add)
                    v.tensor_tensor(there, there, psT[u % 2][:, 0:2 * W].rearrange("p (k w) -> p k w", k=2), ALU.add).then_inc(added, 1)
                    hold(v, added, DONE(n))

                def weigh(m, s, u):
                    v.wait_ge(w_ready, DONE(m * 4 + u))
                    v.tensor_tensor(wrows[:, u % 2, :, 0:D].rearrange("p k (h f) -> p k h f", h=HEADS),
                                    rows[:, u, :, 0:D].rearrange("p k (h f) -> p k h f", h=HEADS),
                                    wrows[:, u % 2, :, D:ROW].unsqueeze(3).to_broadcast([TP, KB, HEADS, HD]), ALU.mult).then_inc(weighed, 1)

                def before(r):
                    link.restart()
                    select(r * QUADS, 0, 0)
                    select(r * QUADS, 1, 1)
                    if weighted:
                        hold(v, keys_in, (r + 1) * 16)

                def step(m, q, u):
                    s = q * 4 + u
                    known = isinstance(s, int)
                    if u == 0:
                        link.restart()
                    if weighted:
                        scores(m, s, u)
                    if not (known and s >= NSB - 2):
                        select(m + (u + 2) // 4, s + 2, (u + 2) % 4)
                    if weighted:
                        weigh(m, s, u)
                    at = None if known and s == 0 else window(s - 1)
                    if weighted:
                        rank_piece(q, u)
                    if at is not None:
                        add_sums(m - (1 if u == 0 else 0), (u - 1) % 4, at)
                    if known and s == NSB - 1:
                        add_sums(m, u, window(s))

                def after(r):
                    link.restart()
                    link(v.tensor_scalar(base[:, :], base[:, :], float(W), float(N), ALU.add, ALU.min))
                    v.tensor_copy(base_i[:, :], base[0:1, :]).then_inc(base_ready, 1)

                in_rounds(v, before, step, after)
                if weighted:
                    link.restart()
                    v.tensor_reduce(emax1[:, :], emax[:, :, :], axis=AX.XY, op=ALU.max).then_inc(emax_ready, 1)
                    v.wait_ge(emax_in, 16)
                    link(v.tensor_reduce(K.emax[:, :], emaxall[:, :], axis=AX.X, op=ALU.max))
        M.close()


def nodes_block(nc, A, S, K):
    G = 2
    GN = G * TP
    GROUPS = N // GN
    ENTER, MIX, FEED, LEAVE = range(4)
    TURNS = GROUPS + LEAVE
    assert TURNS % 4 == 0
    with ExitStack() as stack:
        M = Parts(nc, stack, "node_")
        wgate = M.sb("wgate", [128, 4, D])
        ff1 = M.sb("ff1", [128, 2, 2 * D])
        ff2 = M.sb("ff2", [128, 4, D])
        ff1_b = M.sb("ff1_b", [128, 4])
        vecs = M.sb("vecs", [TP, 8, D])
        x = M.sb("x", [TP, 4, G, D])
        ym = M.sb("ym", [TP, 2, G, D])
        tsc = M.sb("tsc", [TP, 2, G, SPLITS, HEADS], BF16)
        rank = M.sb("rank", [TP, 2, G], I32)
        sumsT = M.sb("sumsT", [128, 2, GN])
        denT = M.sb("denT", [HEADS + 1, GN])
        eps_e = M.sb("eps_e", [TP, G, HEADS])
        den = M.sb("den", [TP, G, HEADS])
        dinv = M.sb("dinv", [TP, 4, G])
        pre = M.sb("pre", [TP, G, D])
        low = M.sb("low", [TP, G, D])
        pos = M.sb("pos", [TP, G, D])
        hl = M.sb("hl", [TP, 2, G, D])
        ha = M.sb("ha", [TP, 2, G, D])
        gate = M.sb("gate", [TP, G, D])
        h = M.sb("h", [TP, 2, G, D])
        f = M.sb("f", [TP, G, D])
        x1 = M.sb("x1", [TP, 2, G, D])
        x1d = M.sb("x1d", [TP, 2, G, D])
        gT = M.sb("gT", [128, 4, GN])
        hT = M.sb("hT", [128, 2, GN])
        rT = M.sb("rT", [128, 4, GN])
        stats = M.sb("stats", [TP, G, 6])
        mv = M.sb("mv", [TP, G, 2])
        var, rstd, half, square = (M.sb(n, [TP, G]) for n in ("var", "rstd", "half", "square"))
        psR = M.ps("psR", [TP, G, 512])
        psT = M.ps("psT", [128, 2, 512])
        psG = M.ps("psG", [TP, G, 512])
        psF = M.ps("psF", [128, 2, 512])
        GAT_B, LL_G, LL_B, LG_G, LG_B, L2_G, L2_B, FF2_B = range(8)

        weights_in, rank_ready = (M.sem(n) for n in ("weights_in", "rank_ready"))
        stored = [M.sem(f"stored{i}") for i in range(2)]
        x_in = [M.sem(f"x_in{i}") for i in range(4)]
        tsc_in = [M.sem(f"tsc_in{i}") for i in range(2)]
        ym_in = [M.sem(f"ym_in{i}") for i in range(2)]
        slices_ready, rows_turned, bound_ready, eps_ready, rows_used = (
            M.sem(n) for n in ("slices_ready", "rows_turned", "bound_ready", "eps_ready", "rows_used"))
        pre_ready, elu_ready, normed, g_turned, g_copied = (M.sem(n) for n in ("pre_ready", "elu_ready", "normed", "g_turned", "g_copied"))
        gate_done, gate_ready, h_ready, h_turned, h_copied = (M.sem(n) for n in ("gate_done", "gate_ready", "h_ready", "h_turned", "h_copied"))
        ff1_done, relu_ready, ff2_done, ff2_used, x1_ready, x1_turned, x1_copied = (M.sem(n) for n in (
            "ff1_done", "relu_ready", "ff2_done", "ff2_used", "x1_ready", "x1_turned", "x1_copied"))
        link_v, link_a, ticks = (M.sem(n) for n in ("link_v", "link_a", "ticks"))

        def hold(eng, sem, value):
            eng.wait_ge(sem, value)
            eng.sem_inc(ticks, 1)

        def turns(eng, turn):
            def run(i, u):
                known = isinstance(i, int)
                turn(i, u, lambda lag: not known or 0 <= i - lag < GROUPS)

            for u in range(4):
                run(u, u)
            with eng.Fori(1, TURNS // 4 - 1) as q:
                for u in range(4):
                    run(q * 4 + u, u)
            for u in range(4):
                run(TURNS - 4 + u, u)

        def by_group(dram, g):
            return dram.rearrange("(g j p) c -> g p j c", j=G, p=TP)[bass.ds(g, 1)].rearrange("a p j c -> (a p) j c")

        def later(i, n):
            return not isinstance(i, int) or i >= n

        with nc.Block() as block:
            @block.sync
            def _(sp):
                for t, a in ((wgate[:, 0:2], A.wlT), (wgate[:, 2:4], A.wgT), (ff1[:, :, :], A.ff1_wT), (ff2[:, :, :], A.ff2_wT)):
                    sp.dma_start(t, a.rearrange("(k p) n -> p k n", p=128)).then_inc(weights_in, 16)
                sp.dma_start(ff1_b[:, :], A.ff1_b).then_inc(weights_in, 16)
                sp.dma_start(vecs[:, :, :], A.rowvecs.partition_broadcast(TP)).then_inc(weights_in, 16)

                def load(g, u):
                    sp.dma_start(x[:, u], by_group(A.x, g)).then_inc(x_in[u], 16)
                    sp.dma_start(tsc[:, u % 2].rearrange("p j s h -> p j (s h)"), by_group(S.stgt[0:N], g)).then_inc(tsc_in[u % 2], 16)

                load(0, 0)

                def turn(i, u, on):
                    if on(ENTER) and not (isinstance(i, int) and i + 1 >= GROUPS):
                        if later(i, 1):
                            hold(sp, bound_ready, i)
                        if later(i, 3):
                            hold(sp, x1_ready, i - 2)
                        load(i + 1, (u + 1) % 4)
                    if on(FEED):
                        g = i - FEED
                        hold(sp, x1_ready, g + 1)
                        sp.dma_start(by_group(S.x1, g), x1[:, u % 2]).then_inc(stored[(u - FEED) % 2], 16)
                        sp.dma_start(by_group(S.x1d, g), x1d[:, u % 2]).then_inc(stored[(u - FEED) % 2], 16)
                        with nc.allow_non_contiguous_dma(reason="one value a node"):
                            sp.dma_start(by_group(S.dinv.rearrange("(n c) -> n c", c=1), g),
                                         dinv[:, (u - FEED) % 4].unsqueeze(2)).then_inc(stored[(u - FEED) % 2], 16)

                turns(sp, turn)
                sp.wait_ge(stored[0], 48 * ((GROUPS + 1) // 2))
                sp.wait_ge(stored[1], 48 * (GROUPS // 2))

            @block.gpsimd
            def _(pool):
                def turn(i, u, on):
                    if on(ENTER):
                        if later(i, 2):
                            hold(pool, rows_used, i - 1)
                        pool.tensor_copy(rank[:, u % 2], K.rank[:, bass.ds(i * G, G)]).then_inc(rank_ready, 1)
                        hold(pool, rank_ready, i + 1)
                        for j in range(G):
                            pool.indirect_dma_start(ym[:, u % 2, j, :], None, S.ys,
                                                    bass.IndirectOffsetOnAxis(ap=rank[:, u % 2, j:j + 1], axis=0)).then_inc(ym_in[u % 2], 16)

                turns(pool, turn)

            @block.tensor
            def _(pe):
                pe.wait_ge(weights_in, 96)
                small = K.ident[0:TP, 0:TP]

                def turn(i, u, on):
                    if on(ENTER):
                        hold(pe, slices_ready, i + 1)
                        if later(i, 1):
                            hold(pe, rows_used, i)
                        for j in range(G):
                            for k in range(2):
                                nc.tensor.transpose(psR[:, j, k * 128:(k + 1) * 128], sumsT[:, k, j * TP:(j + 1) * TP], K.ident[:, :])
                            last = nc.tensor.transpose(psR[:, j, D:D + HEADS + 1], denT[:, j * TP:(j + 1) * TP], K.ident[0:HEADS + 1, 0:HEADS + 1])
                        last.then_inc(rows_turned, 1)
                    if on(MIX):
                        s = (u - MIX) % 2
                        hold(pe, normed, i - MIX + 1)
                        if later(i, LEAVE + 1):
                            hold(pe, x1_copied, i - LEAVE)
                        for j in range(G):
                            for k in range(4):
                                row = (hl, ha)[k // 2][:, s, j, (k % 2) * 128:(k % 2 + 1) * 128]
                                last = nc.tensor.transpose(psT[:, k // 2, (k % 2) * GN + j * TP:(k % 2) * GN + (j + 1) * TP], row, small)
                        last.then_inc(g_turned, 1)
                        hold(pe, g_copied, i - MIX + 1)
                        if later(i, FEED + 1):
                            hold(pe, ff2_used, i - FEED)
                        for j in range(G):
                            for k in range(4):
                                last = nc.tensor.matmul(psG[:, j, 0:D], gT[:, k, j * TP:(j + 1) * TP], wgate[:, k], start=(k == 0), stop=(k == 3))
                        last.then_inc(gate_done, 1)
                    if on(FEED):
                        g = i - FEED
                        s = (u - FEED) % 2
                        hold(pe, h_ready, g + 1)
                        for j in range(G):
                            for k in range(2):
                                last = nc.tensor.transpose(psT[:, 0, k * GN + j * TP:k * GN + (j + 1) * TP], h[:, s, j, k * 128:(k + 1) * 128], small)
                        last.then_inc(h_turned, 1)
                        hold(pe, h_copied, g + 1)
                        for m in range(4):
                            for k in range(2):
                                last = nc.tensor.matmul(psF[:, m // 2, (m % 2) * GN:(m % 2 + 1) * GN], ff1[:, k, m * 128:(m + 1) * 128], hT[:, k],
                                                        start=(k == 0), stop=(k == 1))
                        last.then_inc(ff1_done, 1)
                        hold(pe, relu_ready, g + 1)
                        if on(MIX):
                            hold(pe, gate_ready, i - MIX + 1)
                        else:
                            hold(pe, ff2_used, g)
                        for j in range(G):
                            for k in range(4):
                                last = nc.tensor.matmul(psG[:, j, 0:D], rT[:, k, j * TP:(j + 1) * TP], ff2[:, k], start=(k == 0), stop=(k == 3))
                        last.then_inc(ff2_done, 1)
                    if on(LEAVE):
                        g = i - LEAVE
                        s = (u - LEAVE) % 2
                        hold(pe, x1_ready, g + 1)
                        if on(FEED):
                            hold(pe, h_copied, i - FEED + 1)
                        if not on(MIX):
                            hold(pe, x1_copied, g)
                        for j in range(G):
                            for k in range(2):
                                last = nc.tensor.transpose(psT[:, 1, k * GN + j * TP:k * GN + (j + 1) * TP], x1d[:, s, j, k * 128:(k + 1) * 128], small)
                        last.then_inc(x1_turned, 1)

                turns(pe, turn)

            @block.scalar
            def _(act):
                link = Link(act, link_a)
                halves = lambda t: t.rearrange("p (k n) -> p k n", k=2)
                act.wait_ge(weights_in, 96)

                def slices(g, first):
                    if not first:
                        hold(act, rows_turned, g)
                    act.copy(sumsT[:, :, :], K.sums[:, :, bass.ds(g * GN, GN)])
                    act.copy(denT[:, :], K.den[:, bass.ds(g * GN, GN)]).then_inc(slices_ready, 1)

                slices(0, True)

                def turn(i, u, on):
                    if u == 0:
                        link.restart()
                    if on(MIX):
                        g = i - MIX
                        act.wait_ge(g_turned, g + 1)
                        for k in range(2):
                            last = act.copy(gT[:, 2 * k:2 * k + 2], halves(psT[:, k, 0:2 * GN]))
                        last.then_inc(g_copied, 1)
                    if on(ENTER):
                        act.wait_ge(bound_ready, i + 1)
                        act.activation(eps_e[:, :, :], den[:, :, :], ACT.Exp, scale=-1.0, bias=K.emax[:, 0:1]).then_inc(eps_ready, 1)
                        if not (isinstance(i, int) and i + 1 >= GROUPS):
                            slices(i + 1, False)
                    if on(MIX):
                        g = i - MIX
                        act.wait_ge(gate_done, g + 1)
                        if later(i, 2):
                            act.wait_ge(h_ready, g)
                        act.activation(gate[:, :, :], psG[:, :, 0:D], ACT.Tanh, scale=0.5).then_inc(gate_ready, 1)
                    if on(ENTER):
                        act.wait_ge(pre_ready, i + 1)
                        act.activation(pos[:, :, :], pre[:, :, :], ACT.Relu)
                        act.activation(low[:, :, :], low[:, :, :], ACT.Exp).then_inc(elu_ready, 1)
                    if on(FEED):
                        g = i - FEED
                        act.wait_ge(h_turned, g + 1)
                        act.copy(hT[:, :, :], halves(psT[:, 0, 0:2 * GN])).then_inc(h_copied, 1)
                        act.wait_ge(ff1_done, g + 1)
                        for m in range(4):
                            last = act.activation(rT[:, m], psF[:, m // 2, (m % 2) * GN:(m % 2 + 1) * GN], ACT.Relu, bias=ff1_b[:, m:m + 1])
                        last.then_inc(relu_ready, 1)
                    if on(LEAVE):
                        g = i - LEAVE
                        hold(act, x1_turned, g + 1)
                        act.copy(K.sums[:, :, bass.ds(g * GN, GN)], halves(psT[:, 1, 0:2 * GN])).then_inc(x1_copied, 1)

                turns(act, turn)

            @block.vector
            def _(v):
                link = Link(v, link_v)
                v.wait_ge(weights_in, 96)

                def vec(n):
                    return vecs[:, n].unsqueeze(1).to_broadcast([TP, G, D])

                def layer_norm(out, t, gain=None, shift=None, signal=None):
                    for j in range(G):
                        last = v.bn_stats(stats[:, j], t[:, j])
                    link(last)
                    for j in range(G):
                        last = v.bn_aggr(mv[:, j], stats[:, j])
                    link(last)
                    link(v.tensor_scalar(var[:, :], mv[:, :, 1], EPS, None, ALU.add))
                    rsqrt(v, link, rstd[:, :], var[:, :], half[:, :], square[:, :])
                    for j in range(G):
                        last = v.tensor_scalar(out[:, j], t[:, j], mv[:, j, 0:1], rstd[:, j:j + 1], ALU.subtract, ALU.mult)
                    link(last)
                    if gain is not None:
                        link(v.tensor_tensor(out, out, vec(gain), ALU.mult))
                        last = v.tensor_tensor(out, out, vec(shift), ALU.add)
                        last.then_inc(signal, 1) if signal is not None else link(last)

                def turn(i, u, on):
                    if u == 0:
                        link.restart()
                    if on(ENTER):
                        xg, hag, hlg = x[:, u], ha[:, u % 2], hl[:, u % 2]
                        hold(v, x_in[u], (i - u + 4) * 4)
                        hold(v, tsc_in[u % 2], (i - u % 2 + 2) * 8)
                        if later(i, 2):
                            hold(v, g_turned, i - 1)
                        link(v.tensor_reduce(den[:, :, :], tsc[:, u % 2].rearrange("p j s h -> p j h s"), axis=AX.X, op=ALU.add))
                        link(v.tensor_tensor(den[:, :, :], den[:, :, :], K.smax[:, :].unsqueeze(1).to_broadcast([TP, G, HEADS]), ALU.add))
                        v.scalar_tensor_tensor(den[:, :, :], den[:, :, :], 0.2, den[:, :, :], ALU.mult, ALU.max).then_inc(bound_ready, 1)
                        v.wait_ge(ym_in[u % 2], (i - u % 2 + 2) * 8 * G)
                        link(v.tensor_tensor(hag, xg, ym[:, u % 2], ALU.add))
                        layer_norm(hag, hag, LG_G, LG_B)
                        hold(v, rows_turned, i + 1)
                        hold(v, eps_ready, i + 1)
                        if later(i, 4):
                            hold(v, stored[u % 2], (i - u % 2 - 2) * 24)
                        link(v.scalar_tensor_tensor(den[:, :, :], eps_e[:, :, :], 1e-16, psR[:, :, D:D + HEADS], ALU.mult, ALU.add))
                        link(v.tensor_scalar(var[:, :], psR[:, :, D + HEADS], 1.0, None, ALU.add))
                        rsqrt(v, link, dinv[:, u], var[:, :], half[:, :], square[:, :])
                        link(v.tensor_scalar(den[:, :, :], den[:, :, :], 1e-37, None, ALU.max))
                        link(v.reciprocal(den[:, :, :], den[:, :, :]))
                        v.tensor_tensor(pre[:, :, :].rearrange("p j (h f) -> p j h f", h=HEADS),
                                        psR[:, :, 0:D].rearrange("p j (h f) -> p j h f", h=HEADS),
                                        den[:, :, :].unsqueeze(3).to_broadcast([TP, G, HEADS, HD]), ALU.mult).then_inc(rows_used, 1)
                        hold(v, rows_used, i + 1)
                        link(v.tensor_tensor(pre[:, :, :], pre[:, :, :], xg, ALU.add))
                        link(v.tensor_tensor(pre[:, :, :], pre[:, :, :], vec(GAT_B), ALU.add))
                        v.tensor_scalar(low[:, :, :], pre[:, :, :], 0.0, None, ALU.min).then_inc(pre_ready, 1)
                    if on(MIX):
                        s = (u - MIX) % 2
                        if later(i, MIX + 2):
                            hold(v, h_turned, i - MIX - 1)
                        link(v.tensor_tensor(h[:, s], hl[:, s], ha[:, s], ALU.subtract))
                        hold(v, gate_ready, i - MIX + 1)
                        link(v.scalar_tensor_tensor(h[:, s], gate[:, :, :], 1.0, h[:, s], ALU.add, ALU.mult))
                        v.scalar_tensor_tensor(h[:, s], h[:, s], 0.5, ha[:, s], ALU.mult, ALU.add).then_inc(h_ready, 1)
                    if on(ENTER):
                        hold(v, elu_ready, i + 1)
                        link(v.scalar_tensor_tensor(hlg, low[:, :, :], -1.0, pos[:, :, :], ALU.add, ALU.add))
                        layer_norm(hlg, hlg, LL_G, LL_B, normed)
                    if on(FEED):
                        g = i - FEED
                        s = (u - FEED) % 2
                        if later(i, FEED + 2):
                            hold(v, stored[s], (g - s) * 24)
                            hold(v, x1_turned, g - 1)
                        hold(v, h_ready, g + 1)
                        link(v.tensor_tensor(f[:, :, :], h[:, s], vec(FF2_B), ALU.add))
                        hold(v, ff2_done, g + 1)
                        v.tensor_tensor(f[:, :, :], f[:, :, :], psG[:, :, 0:D], ALU.add).then_inc(ff2_used, 1)
                        hold(v, ff2_used, g + 1)
                        layer_norm(f[:, :, :], f[:, :, :], L2_G, L2_B)
                        link(v.tensor_tensor(f[:, :, :], f[:, :, :], x[:, (u - FEED) % 4], ALU.add))
                        layer_norm(x1[:, s], f[:, :, :])
                        for j in range(G):
                            last = v.tensor_scalar(x1d[:, s, j], x1[:, s, j], dinv[:, (u - FEED) % 4, j:j + 1], None, ALU.mult)
                        last.then_inc(x1_ready, 1)

                turns(v, turn)
        M.close()


def output_block(nc, A, S, K, out):
    CN = 2 * TP
    CHUNKS = N // CN
    with ExitStack() as stack:
        M = Parts(nc, stack, "out_")
        w = M.sb("w", [128, 2, D])
        vec = M.sb("vec", [128, 3, 2])
        dinv = M.sb("dinv", [128, N])
        g = M.sb("g", [128, 2, CN])
        o = M.sb("o", [128, 2, N])
        stats = M.sb("stats", [128, 2, CHUNKS, 6])
        mv = M.sb("mv", [128, 2, 2])
        gain = M.sb("gain", [128, 2])
        shift = M.sb("shift", [128, 2])
        act_o = M.sb("act_o", [128, 2, CN])
        x1 = M.sb("x1", [TP, 2, D])
        res = M.sb("res", [TP, 2, D])
        stat1 = M.sb("stat1", [TP, 2, 6])
        mv1 = M.sb("mv1", [TP, 2, 2])
        y = M.sb("y", [TP, 2, D])
        var, half, square = (M.sb(n, [128, 2]) for n in ("var", "half", "square"))
        rstd = M.sb("rstd", [TP, 2])
        psO = M.ps("psO", [128, 2, 512])
        psT = M.ps("psT", [TP, 2, 512])
        weights_in, dinv_in, g_ready, o_done, scaled, o_ready = (M.sem(n) for n in ("weights_in", "dinv_in", "g_ready", "o_done", "scaled", "o_ready"))
        norm_ready, relu_ready, turned, x1_in, y_ready, stored = (M.sem(n) for n in ("norm_ready", "relu_ready", "turned", "x1_in", "y_ready", "stored"))
        stat_ready, link_v, link_a, ticks = (M.sem(n) for n in ("stat_ready", "link_v", "link_a", "ticks"))

        def hold(eng, sem, value):
            eng.wait_ge(sem, value)
            eng.sem_inc(ticks, 1)

        def chunks(eng, step):
            step(0, True)
            with eng.Fori(1, CHUNKS) as c:
                step(c, False)

        def by_chunk(dram, c):
            return dram.rearrange("(g j p) c -> g p j c", j=2, p=TP)[bass.ds(c, 1)].rearrange("a p j c -> (a p) j c")

        with nc.Block() as block:
            @block.sync
            def _(sp):
                sp.dma_start(w[:, :, :], A.gcn_w.rearrange("(k p) n -> p k n", p=128)).then_inc(weights_in, 16)
                sp.dma_start(vec[:, :, :], A.colvecs).then_inc(weights_in, 16)
                sp.dma_start(dinv[:, :], S.dinv.partition_broadcast(128)).then_inc(dinv_in, 16)

                def step(c, first):
                    if not first:
                        hold(sp, y_ready, c)
                    sp.dma_start(x1[:, :, :], by_chunk(S.x1, c)).then_inc(x1_in, 16)
                    hold(sp, y_ready, c + 1)
                    sp.dma_start(by_chunk(out, c), y[:, :, :]).then_inc(stored, 16)

                chunks(sp, step)
                sp.wait_ge(stored, 16 * CHUNKS)

            @block.tensor
            def _(pe):
                pe.wait_ge(weights_in, 32)

                def product(c, first):
                    if not first:
                        hold(pe, scaled, c)
                    for m in range(2):
                        for k in range(2):
                            last = nc.tensor.matmul(psO[:, m, 0:CN], w[:, k, m * 128:(m + 1) * 128], K.sums[:, k, bass.ds(c * CN, CN)],
                                                    start=(k == 0), stop=(k == 1))
                    last.then_inc(o_done, 1)

                def turn(c, first):
                    hold(pe, relu_ready, c + 1)
                    if not first:
                        hold(pe, y_ready, c)
                    for j in range(2):
                        for k in range(2):
                            last = nc.tensor.transpose(psT[:, j, k * 128:(k + 1) * 128], act_o[:, k, j * TP:(j + 1) * TP], K.ident[:, :])
                    last.then_inc(turned, 1)

                chunks(pe, product)
                chunks(pe, turn)

            @block.scalar
            def _(act):
                def bias(c, first):
                    act.wait_ge(scaled, c + 1)
                    for k in range(2):
                        last = act.activation(o[:, k, bass.ds(c * CN, CN)], o[:, k, bass.ds(c * CN, CN)], ACT.Identity, bias=vec[:, 0, k:k + 1])
                    last.then_inc(o_ready, 1)

                def relu(c, first):
                    if not first:
                        act.wait_ge(turned, c)
                    for k in range(2):
                        last = act.activation(act_o[:, k], o[:, k, bass.ds(c * CN, CN)], ACT.Relu, scale=gain[:, k:k + 1], bias=shift[:, k:k + 1])
                    last.then_inc(relu_ready, 1)

                act.wait_ge(weights_in, 32)
                chunks(act, bias)
                act.wait_ge(norm_ready, 1)
                chunks(act, relu)

            @block.vector
            def _(v):
                link = Link(v, link_v)
                v.wait_ge(dinv_in, 16)

                def scale(c, first):
                    v.wait_ge(o_done, c + 1)
                    v.tensor_tensor(o[:, :, bass.ds(c * CN, CN)], psO[:, :, 0:CN],
                                    dinv[:, bass.ds(c * CN, CN)].unsqueeze(1).to_broadcast([128, 2, CN]), ALU.mult).then_inc(scaled, 1)

                chunks(v, scale)
                for c in range(CHUNKS):
                    v.wait_ge(o_ready, c + 1)
                    for k in range(2):
                        last = v.bn_stats(stats[:, k, c], o[:, k, c * CN:(c + 1) * CN])
                link(last)
                for k in range(2):
                    last = v.bn_aggr(mv[:, k], stats[:, k])
                link(last)
                link(v.tensor_scalar(var[:, :], mv[:, :, 1], EPS, None, ALU.add))
                rsqrt(v, link, gain[:, :], var[:, :], half[:, :], square[:, :])
                link(v.tensor_tensor(gain[:, :], gain[:, :], vec[:, 1], ALU.mult))
                link(v.tensor_tensor(shift[:, :], mv[:, :, 0], gain[:, :], ALU.mult))
                v.tensor_tensor(shift[:, :], vec[:, 2], shift[:, :], ALU.subtract).then_inc(norm_ready, 1)
                link.restart()

                def last_norm(c, first):
                    link.restart()
                    v.wait_ge(turned, c + 1)
                    v.wait_ge(x1_in, (c + 1) * 16)
                    link(v.tensor_tensor(res[:, :, :], x1[:, :, :], psT[:, :, 0:D], ALU.add))
                    for j in range(2):
                        last = v.bn_stats(stat1[:, j], res[:, j])
                    link(last)
                    for j in range(2):
                        last = v.bn_aggr(mv1[:, j], stat1[:, j])
                    link(last)
                    link(v.tensor_scalar(var[0:TP, :], mv1[:, :, 1], EPS, None, ALU.add))
                    rsqrt(v, link, rstd[:, :], var[0:TP, :], half[0:TP, :], square[0:TP, :])
                    if not first:
                        v.wait_ge(stored, c * 16)
                    for j in range(2):
                        last = v.tensor_scalar(y[:, j], res[:, j], mv1[:, j, 0:1], rstd[:, j:j + 1], ALU.subtract, ALU.mult)
                    last.then_inc(y_ready, 1)

                chunks(v, last_norm)
        M.close()


def build(nc, A, out):
    S, K = Named(), Named()
    S.proj = nc.dram_tensor("proj_rows", (N, ROW), F32).ap()
    S.stgt = nc.dram_tensor("target_scores", (NA, SPLITS * HEADS), BF16).ap()
    S.smax = nc.dram_tensor("source_maxima", (TP * HEADS,), F32).ap()
    S.low = nc.dram_tensor("window_lows", (NSB,), F32).ap()
    S.span = nc.dram_tensor("superblock_widths", (NSB,), F32).ap()
    S.deg = nc.dram_tensor("out_degrees", (NHIST,), F32).ap()
    S.key = nc.dram_tensor("keys", (N,), F32).ap()
    S.rank = nc.dram_tensor("ranks", (N,), I32).ap()
    S.xs = nc.dram_tensor("ordered_rows", (N, D), F32).ap()
    S.ys = nc.dram_tensor("mamba_rows", (N, D), F32).ap()
    S.x1 = nc.dram_tensor("x1_rows", (N, D), F32).ap()
    S.x1d = nc.dram_tensor("x1_scaled_rows", (N, D), F32).ap()
    S.dinv = nc.dram_tensor("degree_scales", (N,), F32).ap()
    S.emax = nc.dram_tensor("score_maxima", (TP,), F32).ap()
    S.den = nc.dram_tensor("weight_sums", (HEADS + 1, NA), F32).ap()
    with ExitStack() as stack:
        P = Parts(nc, stack, "")
        K.ident = P.sb("ident", [128, 128])
        K.iota = P.sb("iota", [128, 128])
        K.pidx = P.sb("pidx", [128, 1])
        K.steps = P.sb("steps", [1, 132])
        K.low = P.sb("low", [128, NSB])
        K.smax = P.sb("smax", [TP, HEADS])
        K.rounds = P.sb("rounds", [1, 1], I32)
        K.rank = P.sb("rank", [TP, TILES], I32)
        K.smaller = P.sb("smaller", [TP, 4 * TILES])
        K.ties = P.sb("ties", [TP, TILES])
        K.sums = P.sb("sums", [128, 2, NA])
        K.den_room = P.sb("den", [128, NA])
        K.den = K.den_room[0:HEADS + 1]
        K.emax = P.sb("emax", [TP, 1])
        tables_block(nc, A, S, K)
        edge_pass(nc, A, S, K, True)
        ranks_block(nc, A, S, K)
        mamba_block(nc, A, S, K)
        nodes_block(nc, A, S, K)
        edge_pass(nc, A, S, K, False)
        output_block(nc, A, S, K, out)


class Named:
    pass




def layout(inputs):
    import numpy as np

    g = {k: np.asarray(v) for k, v in inputs.items()}
    w = {k.split("_gnn_")[1] if "_gnn_" in k else k: v for k, v in g.items()}
    t = lambda a: np.ascontiguousarray(a.T)
    a_blk = np.zeros((D, 2 * HEADS), w["gat_a_src"].dtype)
    for h in range(HEADS):
        a_blk[h * HD:(h + 1) * HD, h] = w["gat_a_src"][h]
        a_blk[h * HD:(h + 1) * HD, HEADS + h] = w["gat_a_tgt"][h]
    halves = lambda a: np.ascontiguousarray(a.reshape(2, 128, -1).transpose(1, 0, 2))
    return {
        "x": w["x"], "xT": t(w["x"]), "src": w["src"], "dst": w["dst"], "node_vec": w["node_vec"],
        "src_cols": np.ascontiguousarray(w["src"].reshape(NSB, KB, TP).transpose(0, 2, 1)),
        "dst_cols": np.ascontiguousarray(w["dst"].reshape(NSB, KB, TP).transpose(0, 2, 1)),
        "gat_w": w["gat_w"], "gat_wT": t(w["gat_w"]), "a_blk": a_blk,
        "in_wT": t(w["in_proj_w"]), "x_wT": t(w["x_proj_w"]), "dt_wT": t(w["dt_proj_w"]), "out_wT": t(w["out_proj_w"]),
        "conv_w": halves(w["conv_w"]), "conv_b": halves(w["conv_b"]), "dt_b": halves(w["dt_proj_b"]),
        "a_log": halves(w["A_log"]), "d_param": halves(w["D_param"]),
        "wlT": t(w["wl"]), "wgT": t(w["wg"]), "ff1_wT": t(w["ff1_w"]), "ff2_wT": t(w["ff2_w"]),
        "ff1_b": t(w["ff1_b"].reshape(4, 128)),
        "rowvecs": np.stack([w[k] for k in ("gat_b", "ln_local_g", "ln_local_b", "ln_global_g", "ln_global_b",
                                            "ln2_g", "ln2_b", "ff2_b")]),
        "gcn_w": w["W"], "colvecs": np.ascontiguousarray(np.stack([w[k].reshape(2, 128) for k in ("b", "gamma", "beta")]).transpose(2, 0, 1)),
        "ident": np.eye(128, dtype=np.float32),
        "iota": np.tile(np.arange(128, dtype=np.float32), (128, 1)),
        "pidx": np.arange(128, dtype=np.float32)[:, None],
        "steps": (W * np.arange(132, dtype=np.float32))[None],
        "tri": np.tril(np.ones((TP, TP), np.float32), -1),
    }


def kernel(**inputs):
    import concourse.bacc as bacc
    from concourse.bass_utils import run_bass_kernel_spmd

    arrays = {k + "_d": v for k, v in layout(inputs).items()}
    nc = bacc.Bacc("TRN2", target_bir_lowering=False, num_devices=1)
    args = Named()
    for name, a in arrays.items():
        args.__dict__[name[:-2]] = nc.dram_tensor(name, a.shape, mybir.dt.from_np(a.dtype), kind="ExternalInput").ap()
    out = nc.dram_tensor("out_d", (N, D), F32, kind="ExternalOutput").ap()
    build(nc, args, out)
    r = run_bass_kernel_spmd(nc, [arrays], core_ids=[0])
    return r.results[0]["out_d"]
```

```python
from contextlib import ExitStack

import concourse.bass as bass
from concourse import mybir

F32 = mybir.dt.float32
BF16 = mybir.dt.bfloat16
I32 = mybir.dt.int32
ALU = mybir.AluOpType
ACT = mybir.ActivationFunctionType
AX = mybir.AxisListType

N, E, D = 6250, 200000, 256
HEADS, HD = 4, 64
TP = 125
TILES = N // TP
KB = 8
EDGES_SB = KB * TP
NSB = E // EDGES_SB
W = 48
NA = N + W + 6
ROW = D + HEADS
DSTATE, DCONV, DTR = 16, 4, 16
CH = 500
CT = CH // TP
NCH = -(-N // CH)
HI, LO = 98, 64
NHIST = HI * LO
SPLITS = 3
EPS = 1e-5
NEG = -3.0e38


class Link:

    def __init__(self, eng, sem):
        self.eng, self.sem, self.n = eng, sem, 0

    def __call__(self, ins):
        self.n += 1
        ins.then_inc(self.sem, 1)
        self.eng.wait_ge(self.sem, self.n)

    def note(self, ins):
        self.n += 1
        ins.then_inc(self.sem, 1)

    def need(self):
        self.eng.wait_ge(self.sem, self.n)

    def restart(self):
        self.eng.sem_clear(self.sem)
        self.n = 0


class Parts:

    def __init__(self, nc, stack, prefix):
        self.nc, self.stack, self.prefix, self.sems = nc, stack, prefix, []

    def sb(self, name, shape, dt=F32):
        return self.stack.enter_context(self.nc.sbuf_tensor(self.prefix + name, shape, dt))

    def ps(self, name, shape, dt=F32):
        return self.stack.enter_context(self.nc.psum_tensor(self.prefix + name, shape, dt))

    def sem(self, name):
        self.sems.append(self.nc.alloc_semaphore(self.prefix + name))
        return self.sems[-1]

    def close(self):
        self.nc.clear_and_free_semaphores(self.sems)
        self.nc.all_engine_barrier()


def rsqrt(v, link, out, value, half, square):
    MAGIC, STEPS = float(0x5F3759DF), 3
    link(v.tensor_scalar(out.bitcast(I32), value.bitcast(I32), 1, None, ALU.logical_shift_right))
    v.tensor_scalar(half, value, -0.5, None, ALU.mult)
    link(v.tensor_scalar(out.bitcast(I32), out.bitcast(I32), -1.0, MAGIC, ALU.mult, ALU.add))
    for _ in range(STEPS):
        link(v.tensor_tensor(square, out, out, ALU.mult))
        link(v.tensor_tensor(square, square, half, ALU.mult))
        link(v.scalar_tensor_tensor(out, square, 1.5, out, ALU.add, ALU.mult))


def tables_block(nc, A, S, K):
    G = 5
    GN = G * TP
    HC = 16
    HSTEPS = E // TP // HC
    with ExitStack() as stack:
        M = Parts(nc, stack, "tab_")
        gatw = M.sb("gatw", [128, 2, D])
        ablk = M.sb("ablk", [128, 2, 2 * HEADS])
        waug = M.sb("waug", [128, 2, D + 2 * HEADS])
        xt = M.sb("xt", [128, 2, 2, GN])
        rows = M.sb("rows", [TP, 2, G, D + 2 * HEADS])
        split = M.sb("split", [TP, 2, G, SPLITS, HEADS], BF16)
        rest = M.sb("rest", [TP, G, HEADS])
        smax5 = M.sb("smax5", [TP, G, HEADS])
        smax1 = M.sb("smax1", [TP, HEADS])
        smaxall = M.sb("smaxall", [TP, TP * HEADS])
        dst2 = M.sb("dst2", [NSB // 2, 2, EDGES_SB], I32)
        lowhigh = M.sb("lowhigh", [NSB // 2, 2, 2])
        span = M.sb("span", [NSB // 2, 2])
        spanrow = M.sb("spanrow", [1, NSB])
        widest = M.sb("widest", [1, 1])
        reach = M.sb("reach", [1, 132])
        nrounds = M.sb("nrounds", [1, 1])
        srcs = M.sb("srcs", [TP, E // TP], I32)
        hi = M.sb("hi", [TP, E // TP], I32)
        lo = M.sb("lo", [TP, E // TP], I32)
        hi_b = M.sb("hi_b", [TP, E // TP], BF16)
        lo_b = M.sb("lo_b", [TP, E // TP], BF16)
        place = M.sb("place", [TP, HI, HC], BF16)
        ohhi = M.sb("ohhi", [TP, 2, HI, HC], BF16)
        ohlo = M.sb("ohlo", [TP, 2, LO, HC], BF16)
        hist = M.sb("hist", [HI, LO])
        pad = M.sb("pad", [NA - N, SPLITS * HEADS], BF16)
        psw = M.ps("psw", [128, 2, 2 * HEADS])
        psr = [M.ps(f"psr{j}", [TP, D + 2 * HEADS]) for j in range(G)]
        psh = M.ps("psh", [HI, LO])

        const_in, weights_in, dst_in, src_in = (M.sem(n) for n in ("const_in", "weights_in", "dst_in", "src_in"))
        xt_in = [M.sem("xt_in0"), M.sem("xt_in1")]
        vw_done, vw_copied = M.sem("vw_done"), M.sem("vw_copied")
        proj_done, proj_copied, rows_maxed = M.sem("proj_done"), M.sem("proj_copied"), M.sem("rows_maxed")
        rows_out = [M.sem("rows_out0"), M.sem("rows_out1")]
        scores_out = [M.sem("scores_out0"), M.sem("scores_out1")]
        smax_ready, smax_out, smax_in = M.sem("smax_ready"), M.sem("smax_out"), M.sem("smax_in")
        span_ready, span_out, span_in, base_in = (M.sem(n) for n in ("span_ready", "span_out", "span_in", "base_in"))
        oh_ready, oh_used, hist_ready, hist_out = (M.sem(n) for n in ("oh_ready", "oh_used", "hist_ready", "hist_out"))
        link_v, pad_ready, pad_out = M.sem("link_v"), M.sem("pad_ready"), M.sem("pad_out")

        PAIRS = TILES // G // 2

        with nc.Block() as block:
            @block.sync
            def _(sp):
                for t, a in ((K.ident, A.ident), (K.iota, A.iota), (K.pidx, A.pidx), (K.steps, A.steps)):
                    sp.dma_start(t[:, :], a).then_inc(const_in, 16)
                sp.dma_start(gatw[:, :, :], A.gat_w.rearrange("(k p) n -> p k n", p=128)).then_inc(weights_in, 16)
                sp.dma_start(ablk[:, :, :], A.a_blk.rearrange("(k p) n -> p k n", p=128)).then_inc(weights_in, 16)
                sp.dma_start(waug[:, :, 0:D], A.gat_wT.rearrange("(k p) n -> p k n", p=128)).then_inc(weights_in, 16)
                sp.dma_start(srcs[:, :], A.src.rearrange("(p c) -> p c", p=TP)).then_inc(src_in, 16)
                sp.dma_start(dst2[:, :, :], A.dst.rearrange("(p j e) -> p j e", j=2, e=EDGES_SB)).then_inc(dst_in, 16)
                xT = A.xT.rearrange("(k p) n -> p k n", p=128)
                rows_dram = S.proj.rearrange("(g j p) c -> g p j c", j=G, p=TP)
                scores_dram = S.stgt[0:N, :].rearrange("(g j p) c -> g p j c", j=G, p=TP)
                for par in range(2):
                    sp.dma_start(xt[:, par], xT[:, :, par * GN:(par + 1) * GN]).then_inc(xt_in[par], 16)

                def step(i, last):
                    for par in range(2):
                        sp.wait_ge(proj_copied, i * (2 * G) + (par + 1) * G)
                        sp.dma_start(rows_dram[bass.ds(i * 2 + par, 1)].rearrange("a p j c -> (a p) j c"),
                                     rows[:, par, :, 0:ROW]).then_inc(rows_out[par], 16)
                        sp.wait_ge(rows_maxed, i * 2 + par + 1)
                        sp.dma_start(scores_dram[bass.ds(i * 2 + par, 1)].rearrange("a p j c -> (a p) j c"),
                                     split[:, par].rearrange("p j s h -> p j (s h)")).then_inc(scores_out[par], 16)
                        if not last:
                            sp.dma_start(xt[:, par], xT[:, :, bass.ds((i * 2 + par + 2) * GN, GN)]).then_inc(xt_in[par], 16)

                with sp.Fori(0, PAIRS - 1) as i:
                    step(i, False)
                step(PAIRS - 1, True)
                sp.wait_ge(pad_ready, 1)
                sp.dma_start(S.stgt[N:NA, :], pad[:, :]).then_inc(pad_out, 16)
                sp.wait_ge(pad_out, 16)
                sp.wait_ge(smax_ready, 1)
                sp.dma_start(S.smax.rearrange("(p h) -> p h", h=HEADS), smax1[:, :]).then_inc(smax_out, 16)
                sp.wait_ge(smax_out, 16)
                sp.dma_start(smaxall[:, :], S.smax.partition_broadcast(TP)).then_inc(smax_in, 16)
                sp.wait_ge(span_ready, 1)
                sp.dma_start(S.low.rearrange("(p j) -> p j", j=2), lowhigh[:, 0]).then_inc(span_out, 16)
                sp.dma_start(S.span.rearrange("(p j) -> p j", j=2), span[:, :]).then_inc(span_out, 16)
                sp.wait_ge(span_out, 32)
                sp.dma_start(K.low[:, :], S.low.partition_broadcast(128)).then_inc(base_in, 16)
                sp.dma_start(spanrow[:, :], S.span.rearrange("(a n) -> a n", a=1)).then_inc(span_in, 16)
                sp.wait_ge(hist_ready, 1)
                sp.dma_start(S.deg.rearrange("(h l) -> h l", l=LO), hist[:, :]).then_inc(hist_out, 16)
                sp.wait_ge(hist_out, 16)
                sp.wait_ge(base_in, 16)
                for par in range(2):
                    sp.wait_ge(rows_out[par], 16 * PAIRS)
                    sp.wait_ge(scores_out[par], 16 * PAIRS)

            @block.tensor
            def _(pe):
                pe.wait_ge(weights_in, 48)
                for half in range(2):
                    for k in range(2):
                        last = nc.tensor.matmul(psw[:, half], gatw[:, k, half * 128:(half + 1) * 128], ablk[:, k],
                                                start=(k == 0), stop=(k == 1))
                last.then_inc(vw_done, 1)
                pe.wait_ge(vw_copied, 1)

                def step(i, first):
                    for par in range(2):
                        pe.wait_ge(xt_in[par], (i + 1) * 16)
                        for j in range(G):
                            if not (first and par == 0):
                                pe.wait_ge(proj_copied, i * (2 * G) + (par - 1) * G + j + 1)
                            for k in range(2):
                                last = nc.tensor.matmul(psr[j][:, :], xt[:, par, k, j * TP:(j + 1) * TP], waug[:, k],
                                                        start=(k == 0), stop=(k == 1))
                            last.then_inc(proj_done, 1)

                step(0, True)
                with pe.Fori(1, PAIRS) as i:
                    step(i, False)

                def hist_step(i, par, first, final):
                    pe.wait_ge(oh_ready, i * 2 + par + 1)
                    for c in range(HC):
                        last = nc.tensor.matmul(psh[:, :], ohhi[:, par, :, c], ohlo[:, par, :, c],
                                                start=(first and c == 0), stop=(final and c == HC - 1))
                    last.then_inc(oh_used, 1)

                for par in range(2):
                    hist_step(0, par, par == 0, False)
                with pe.Fori(1, HSTEPS // 2 - 1) as i:
                    for par in range(2):
                        hist_step(i, par, False, False)
                for par in range(2):
                    hist_step(HSTEPS // 2 - 1, par, False, par == 1)

            @block.scalar
            def _(act):
                act.wait_ge(vw_done, 1)
                act.wait_ge(weights_in, 48)
                act.copy(waug[:, :, D:], psw[:, :, :]).then_inc(vw_copied, 1)

                def step(i, first):
                    for par in range(2):
                        if not first:
                            act.wait_ge(rows_out[par], i * 16)
                            act.wait_ge(scores_out[par], i * 16)
                            act.wait_ge(rows_maxed, i * 2 + par - 1)
                        for j in range(G):
                            act.wait_ge(proj_done, i * (2 * G) + par * G + j + 1)
                            act.copy(rows[:, par, j], psr[j][:, :]).then_inc(proj_copied, 1)

                step(0, True)
                with act.Fori(1, PAIRS) as i:
                    step(i, False)
                act.wait_ge(oh_used, HSTEPS)
                act.copy(hist[:, :], psh[:, :]).then_inc(hist_ready, 1)

            @block.vector
            def _(v):
                link = Link(v, link_v)
                v.wait_ge(const_in, 64)
                v.wait_ge(dst_in, 16)
                v.tensor_reduce(lowhigh[:, 0], dst2[:, :, :], axis=AX.X, op=ALU.min)
                link(v.tensor_reduce(lowhigh[:, 1], dst2[:, :, :], axis=AX.X, op=ALU.max))
                v.tensor_tensor(span[:, :], lowhigh[:, 1], lowhigh[:, 0], ALU.subtract).then_inc(span_ready, 1)
                v.wait_ge(src_in, 16)
                v.tensor_scalar(hi[:, :], srcs[:, :], 6, None, ALU.logical_shift_right)
                link(v.tensor_scalar(lo[:, :], srcs[:, :], LO - 1, None, ALU.bitwise_and))
                v.tensor_copy(hi_b[:, :], hi[:, :])
                v.tensor_copy(lo_b[:, :], lo[:, :])
                v.tensor_copy(place[:, :, :], K.iota[0:TP, 0:HI].unsqueeze(2).to_broadcast([TP, HI, HC]))
                link(v.memset(smax5[:, :, :], NEG))

                def row_max(i, first):
                    link.restart()
                    for par in range(2):
                        v.wait_ge(proj_copied, i * (2 * G) + (par + 1) * G)
                        if not first:
                            v.wait_ge(scores_out[par], i * 16)
                        left = rows[:, par, :, ROW:]
                        for c in range(SPLITS):
                            link(v.tensor_copy(split[:, par, :, c], left))
                            if c < SPLITS - 1:
                                link(v.tensor_tensor(rest[:, :, :], left, split[:, par, :, c], ALU.subtract))
                                left = rest[:, :, :]
                        v.tensor_tensor(smax5[:, :, :], smax5[:, :, :], rows[:, par, :, D:D + HEADS], ALU.max).then_inc(rows_maxed, 1)
                        v.wait_ge(rows_maxed, i * 2 + par + 1)

                v.memset(pad[:, :], 0.0).then_inc(pad_ready, 1)
                row_max(0, True)
                with v.Fori(1, PAIRS) as i:
                    row_max(i, False)
                link.restart()
                v.tensor_reduce(smax1[:, :], smax5[:, :, :].rearrange("p g h -> p h g"), axis=AX.X, op=ALU.max).then_inc(smax_ready, 1)

                def hist_step(i, par, first):
                    if not first:
                        v.wait_ge(oh_used, i * 2 + par - 1)
                    cols = bass.ds((i * 2 + par) * HC, HC)
                    v.tensor_tensor(ohhi[:, par], hi_b[:, cols].unsqueeze(1).to_broadcast([TP, HI, HC]), place[:, :, :], ALU.is_equal)
                    v.tensor_tensor(ohlo[:, par], lo_b[:, cols].unsqueeze(1).to_broadcast([TP, LO, HC]), place[:, 0:LO], ALU.is_equal
                                    ).then_inc(oh_ready, 1)

                for par in range(2):
                    hist_step(0, par, True)
                with v.Fori(1, HSTEPS // 2) as i:
                    for par in range(2):
                        hist_step(i, par, False)
                v.wait_ge(smax_in, 16)
                v.tensor_reduce(K.smax[:, :], smaxall[:, :].rearrange("p (q h) -> p h q", h=HEADS), axis=AX.X, op=ALU.max)
                v.wait_ge(span_in, 16)
                link(v.tensor_reduce(widest[:, :], spanrow[:, :], axis=AX.X, op=ALU.max))
                link(v.tensor_scalar(reach[:, :], K.steps[:, :], widest[:, 0:1], None, ALU.is_le))
                link(v.tensor_reduce(nrounds[:, :], reach[:, :], axis=AX.X, op=ALU.add))
                link(v.tensor_copy(K.rounds[:, :], nrounds[:, :]))
        M.close()


def ranks_block(nc, A, S, K):
    LOADS = 5
    LT = TILES // LOADS
    with ExitStack() as stack:
        M = Parts(nc, stack, "rank_")
        total = M.sb("total", [TP, TILES])
        xrows = M.sb("xrows", [TP, TILES, D])
        x_in = [M.sem(f"x_in{i}") for i in range(LOADS)]
        rank_ready, scattered, link_v = (M.sem(n) for n in ("rank_ready", "scattered", "link_v"))

        with nc.Block() as block:
            @block.sync
            def _(sp):
                for i in range(LOADS):
                    sp.dma_start(xrows[:, i * LT:(i + 1) * LT, :],
                                 A.x[i * LT * TP:(i + 1) * LT * TP].rearrange("(t p) c -> p t c", p=TP)).then_inc(x_in[i], 16)

            @block.gpsimd
            def _(pool):
                pool.wait_ge(rank_ready, 1)
                for t in range(TILES):
                    if t % LT == 0:
                        pool.wait_ge(x_in[t // LT], 16)
                    pool.indirect_dma_start(S.xs, bass.IndirectOffsetOnAxis(ap=K.rank[:, t:t + 1], axis=0),
                                            xrows[:, t, :], None).then_inc(scattered, 16)
                pool.wait_ge(scattered, 16 * TILES)

            @block.vector
            def _(v):
                link = Link(v, link_v)
                link(v.tensor_reduce(total[:, :], K.smaller[:, :].rearrange("p (t u) -> p t u", u=4), axis=AX.X, op=ALU.add))
                v.tensor_tensor(K.rank[:, :], total[:, :], K.ties[:, :], ALU.add).then_inc(rank_ready, 1)
        M.close()


def mamba_block(nc, A, S, K):
    LOG1P = [-0.0031760570127516985, 0.019542528316378593, -0.05637361481785774, 0.10543623566627502, -0.1526966691017151,
             0.1966327428817749, -0.24951615929603577, 0.33329710364341736, -0.49999892711639404, 1.0]
    PROJECT, GATES, SCAN, LEAVE = range(4)
    TURNS = NCH + LEAVE
    PEEL = LEAVE + 1
    LOOPS = (NCH - 2 - PEEL) // 2
    assert PEEL % 2 == 0
    BC = 32
    with ExitStack() as stack:
        M = Parts(nc, stack, "mam_")
        in_w = M.sb("in_w", [128, 2, 2 * D])
        x_w = M.sb("x_w", [128, 2, 128])
        dt_w = M.sb("dt_w", [DTR, D])
        out_w = M.sb("out_w", [128, 2, D])
        conv_w = M.sb("conv_w", [128, 2, DCONV])
        conv_b = M.sb("conv_b", [128, 2, 1])
        dt_b = M.sb("dt_b", [128, 2, 1])
        d_par = M.sb("d_par", [128, 2, 1])
        a_log = M.sb("a_log", [128, 2, DSTATE])
        a_neg = M.sb("a_neg", [128, 2, DSTATE])
        state = M.sb("state", [128, 2, DSTATE])
        pick = M.sb("pick", [128, BC], BF16)
        xr = M.sb("xr", [TP, CT, D])
        xT = M.sb("xT", [128, 2, 2, CH])
        xin = M.sb("xin", [128, 2, DCONV - 1 + CH])
        conv = M.sb("conv", [128, 2, CH])
        tconv = M.sb("tconv", [128, 2, CH])
        xc = M.sb("xc", [128, 2, 2, CH])
        z = M.sb("z", [128, 2, CH])
        tz = M.sb("tz", [128, 2, CH])
        zs = M.sb("zs", [128, 2, 2, CH])
        dt_rows = M.sb("dt_rows", [DTR, CH])
        parts = M.sb("parts", [128, 2, CH], BF16)
        rest = M.sb("rest", [128, CH])
        mag = M.sb("mag", [128, 2, CH])
        pos = M.sb("pos", [128, 2, CH])
        series = M.sb("series", [128, 2, CH])
        square = M.sb("square", [128, 2, CH])
        pair = K.den_room[:, 0:4 * 2 * CH].rearrange("p (q k n) -> p q k n", q=4, k=2)
        h = [K.den_room[:, at * 2 * CH:(at + 1) * 2 * CH].rearrange("p (k n) -> p k n", k=2) for at in (4, 5)]
        dt = M.sb("dt", [128, 2, 2, CH])
        dtx = M.sb("dtx", [128, 2, 2, CH])
        decay = M.sb("decay", [128, 2, 2, CH])
        bx = M.sb("bx", [128, 2, 2, CH])
        hc = M.sb("hc", [128, 2, 2, CH])
        y = M.sb("y", [128, 2, CH])
        yrows = M.sb("yrows", [TP, CT, D])
        psA = M.ps("psA", [128, 2, 512])
        psB = M.ps("psB", [128, 512])
        psC = M.ps("psC", [128, 512])
        psY = M.ps("psY", [128, 2, 512])
        psO = M.ps("psO", [TP, CT, D])

        sems = lambda *names: (M.sem(n) for n in names)
        params_in, pad_ready, init_ready, a_ready = sems("params_in", "pad_ready", "init_ready", "a_ready")
        x_in, x_turned, xT_ready, main_done, main_copied = sems("x_in", "x_turned", "xT_ready", "main_done", "main_copied")
        z_done, z_left, z_copied, zs_ready, conv_ready, tanh_ready, xc_ready = sems(
            "z_done", "z_left", "z_copied", "zs_ready", "conv_ready", "tanh_ready", "xc_ready")
        dbc_done, part1_ready, rest1_ready, part2_ready, rest2_ready, parts_ready = sems(
            "dbc_done", "part1_ready", "rest1_ready", "part2_ready", "rest2_ready", "parts_ready")
        dt_done, dt_left, mag_ready, pair_ready, dt_ready, dtx_ready = sems("dt_done", "dt_left", "mag_ready", "pair_ready", "dt_ready", "dtx_ready")
        decay_ready, b_done, c_done, bx_ready, scanned, hc_ready, y_summed = sems(
            "decay_ready", "b_done", "c_done", "bx_ready", "scanned", "hc_ready", "y_summed")
        y_left, y_ready, out_done, out_copied, stored = sems("y_left", "y_ready", "out_done", "out_copied", "stored")
        den_out, den_back = sems("den_out", "den_back")
        link_v, link_a, link_g, ticks = sems("link_v", "link_a", "link_g", "ticks")

        def hold(eng, sem, value):
            eng.wait_ge(sem, value)
            eng.sem_inc(ticks, 1)

        def turns(eng, turn):
            def run(i, u):
                known = isinstance(i, int)
                turn(i, u, lambda lag: not known or 0 <= i - lag < NCH,
                     lambda lag: N - (NCH - 1) * CH if known and i - lag == NCH - 1 else CH)

            for i in range(PEEL):
                run(i, i % 2)
            with eng.Fori(0, LOOPS) as q:
                for u in range(2):
                    run(q * 2 + (PEEL + u), u)
            for i in range(PEEL + 2 * LOOPS, TURNS):
                run(i, i % 2)

        def later(i, n):
            return not isinstance(i, int) or i >= n

        with nc.Block() as block:
            @block.sync
            def _(sp):
                sp.dma_start(S.den, K.den[:, :]).then_inc(den_out, 16)
                for t, a in ((in_w, A.in_wT), (out_w, A.out_wT)):
                    sp.dma_start(t[:, :, :], a.rearrange("(k p) n -> p k n", p=128)).then_inc(params_in, 16)
                x_cols = A.x_wT.rearrange("(k p) n -> p k n", p=128)
                sp.wait_ge(pad_ready, 1)
                sp.dma_start(x_w[:, :, 0:DTR], x_cols[:, :, 0:DTR]).then_inc(params_in, 16)
                for place in (32, 64, 96):
                    sp.dma_start(x_w[:, :, place:place + BC], x_cols[:, :, DTR:DTR + BC]).then_inc(params_in, 16)
                sp.dma_start(dt_w[:, :], A.dt_wT).then_inc(params_in, 16)
                for t, a in ((conv_w, A.conv_w), (conv_b, A.conv_b), (dt_b, A.dt_b), (d_par, A.d_param), (a_log, A.a_log)):
                    sp.dma_start(t[:, :, :], a).then_inc(params_in, 16)

                def rows_of(dram, c, tiles):
                    return dram[bass.ds(c * CH, tiles * TP)].rearrange("(j p) f -> p j f", p=TP)

                sp.dma_start(xr[:, :, :], rows_of(S.xs, 0, CT)).then_inc(x_in, 16)

                def turn(i, u, on, width):
                    if on(PROJECT) and not (isinstance(i, int) and i + 1 >= NCH):
                        tiles = width(PROJECT - 1) // TP
                        hold(sp, x_turned, i + 1)
                        sp.dma_start(xr[:, 0:tiles], rows_of(S.xs, i + 1, tiles)).then_inc(x_in, 16)
                    if on(LEAVE):
                        tiles = width(LEAVE) // TP
                        hold(sp, out_copied, i - LEAVE + 1)
                        sp.dma_start(rows_of(S.ys, i - LEAVE, tiles), yrows[:, 0:tiles]).then_inc(stored, 16)

                turns(sp, turn)
                sp.wait_ge(stored, 16 * NCH)
                sp.wait_ge(dtx_ready, NCH)
                sp.dma_start(K.den[:, :], S.den).then_inc(den_back, 16)
                sp.wait_ge(den_back, 16)

            @block.tensor
            def _(pe):
                pe.wait_ge(params_in, 16 * 12)
                pe.wait_ge(init_ready, 1)

                def turn(i, u, on, width):
                    a, b, c, e = (i - lag for lag in range(4))

                    def turn_rows():
                        w = width(PROJECT)
                        pe.wait_ge(x_in, (a + 1) * 16)
                        if later(i, 2):
                            pe.wait_ge(z_left, i - 1)
                        elif i == 1:
                            pe.wait_ge(main_copied, 1)
                        for j in range(w // TP):
                            for k in range(2):
                                last = nc.tensor.transpose(psA[:, k, j * TP:(j + 1) * TP], xr[:, j, k * 128:(k + 1) * 128],
                                                           K.ident[0:TP, 0:TP])
                        last.then_inc(x_turned, 1)

                    def project(part, m, slot, w):
                        for k in range(2):
                            last = nc.tensor.matmul(psA[:, m, 0:w], in_w[:, k, (2 * part + m) * 128:(2 * part + m + 1) * 128],
                                                    xT[:, slot, k, 0:w], start=(k == 0), stop=(k == 1))
                        return last

                    def project_main_0():
                        pe.wait_ge(xT_ready, a + 1)
                        project(0, 0, u, width(PROJECT))

                    def project_main_1():
                        project(0, 1, u, width(PROJECT)).then_inc(main_done, 1)

                    def project_z_0():
                        pe.wait_ge(dt_left, b + 1)
                        project(1, 0, 1 - u, width(GATES))

                    def project_z_1():
                        project(1, 1, 1 - u, width(GATES)).then_inc(z_done, 1)

                    def project_dbc():
                        w = width(GATES)
                        if on(PROJECT):
                            pe.wait_ge(main_copied, a + 1)
                        elif on(GATES):
                            pe.wait_ge(z_left, b)
                        pe.wait_ge(xc_ready, b + 1)
                        for k in range(2):
                            last = nc.tensor.matmul(psA[:, 0, 0:w], x_w[:, k], xc[:, 1 - u, k, 0:w], start=(k == 0), stop=(k == 1))
                        last.then_inc(dbc_done, 1)

                    def project_dt(m):
                        w = width(GATES)
                        return nc.tensor.matmul(psA[:, m, 0:w], dt_w[:, m * 128:(m + 1) * 128], dt_rows[:, 0:w], start=True, stop=True)

                    def project_dt_0():
                        pe.wait_ge(rest1_ready, b + 1)
                        project_dt(0)

                    def project_dt_1():
                        project_dt(1).then_inc(dt_done, 1)

                    def project_out(j):
                        for k in range(2):
                            last = nc.tensor.matmul(psO[:, j], y[:, k, j * TP:(j + 1) * TP], out_w[:, k], start=(k == 0), stop=(k == 1))
                        return last

                    def project_out_first():
                        pe.wait_ge(y_ready, e + 1)
                        if later(i, LEAVE + 1):
                            pe.wait_ge(out_copied, e)
                        for j in range(width(LEAVE) // TP // 2):
                            project_out(j)

                    def project_out_last():
                        tiles = width(LEAVE) // TP
                        for j in range(tiles // 2, tiles):
                            last = project_out(j)
                        last.then_inc(out_done, 1)

                    def spread(bank, n, row, w, done):
                        nc.tensor.matmul(bank[:, 0:w], pick[:, row:row + 1].to_broadcast([128, 128]),
                                         parts[:, u, 0:w], start=True, stop=True).then_inc(done, 1)

                    def spread_b(n):
                        if n or later(i, SCAN + 1):
                            pe.wait_ge(bx_ready, c * DSTATE + n)
                        spread(psB, n, n, width(SCAN), b_done)

                    def sum_state(chunk, n, w):
                        pe.wait_ge(hc_ready, chunk * DSTATE + n + 1)
                        for half in range(2):
                            last = nc.tensor.matmul(psY[:, half, 0:w], K.ident[:, :], hc[:, n % 2, half, 0:w],
                                                    start=(n == 0), stop=(n == DSTATE - 1), skip_group_check=True)
                        last.then_inc(y_summed, 1)

                    pieces = {n: [] for n in range(DSTATE)}
                    if on(PROJECT):
                        pieces[0].append(turn_rows)
                        pieces[1].append(project_main_0)
                        pieces[2].append(project_main_1)
                    if on(GATES):
                        pieces[3].append(project_dbc)
                        pieces[6].append(project_dt_0)
                        pieces[6].append(project_dt_1)
                        pieces[10].append(project_z_0)
                        pieces[11].append(project_z_1)
                    if on(LEAVE):
                        pieces[8].append(project_out_first)
                        pieces[9].append(project_out_last)
                    if on(SCAN):
                        pe.wait_ge(parts_ready, c + 1)
                        spread_b(0)
                    if on(LEAVE):
                        sum_state(e, DSTATE - 1, width(LEAVE))
                    for n in range(DSTATE):
                        if on(SCAN):
                            if n + 1 < DSTATE:
                                spread_b(n + 1)
                            if n or later(i, SCAN + 1):
                                pe.wait_ge(hc_ready, c * DSTATE + n)
                            spread(psC, n, DSTATE + n, width(SCAN), c_done)
                            if n:
                                if n == 1 and later(i, SCAN + 1):
                                    pe.wait_ge(y_left, c)
                                sum_state(c, n - 1, width(SCAN))
                        for piece in pieces[n]:
                            piece()

                turns(pe, turn)

            @block.scalar
            def _(act):
                link = Link(act, link_a)
                act.wait_ge(params_in, 16 * 12)
                act.wait_ge(den_out, 16)
                act.activation(a_neg[:, :, :], a_log[:, :, :], ACT.Exp).then_inc(a_ready, 1)
                act.wait_ge(init_ready, 1)

                def turn(i, u, on, width):
                    a, b, c, e = (i - lag for lag in range(4))
                    link.restart()

                    def copy_rows():
                        w = width(PROJECT)
                        act.wait_ge(x_turned, a + 1)
                        act.copy(xT[:, u, :, 0:w], psA[:, :, 0:w]).then_inc(xT_ready, 1)

                    def copy_main():
                        w = width(PROJECT)
                        if later(i, 1):
                            act.wait_ge(conv_ready, a)
                            link(act.copy(xin[:, :, 0:DCONV - 1], xin[:, :, CH:]))
                        act.wait_ge(main_done, a + 1)
                        act.copy(xin[:, :, DCONV - 1:DCONV - 1 + w], psA[:, :, 0:w]).then_inc(main_copied, 1)

                    def gate_conv():
                        w = width(GATES)
                        act.wait_ge(conv_ready, b + 1)
                        if later(i, 2):
                            act.wait_ge(xc_ready, b)
                        link(act.activation(tconv[:, :, 0:w], conv[:, :, 0:w], ACT.Tanh))
                        act.activation(tconv[:, :, 0:w], tconv[:, :, 0:w], ACT.Copy, bias=1.0).then_inc(tanh_ready, 1)

                    def copy_z():
                        w = width(GATES)
                        act.wait_ge(z_done, b + 1)
                        if later(i, 2):
                            act.wait_ge(zs_ready, b)
                        link(act.activation(tz[:, :, 0:w], psA[:, :, 0:w], ACT.Tanh, scale=0.5))
                        act.activation(z[:, :, 0:w], psA[:, :, 0:w], ACT.Copy, scale=0.5).then_inc(z_left, 1)
                        act.activation(tz[:, :, 0:w], tz[:, :, 0:w], ACT.Copy, bias=1.0).then_inc(z_copied, 1)

                    def part1():
                        w = width(GATES)
                        act.wait_ge(dbc_done, b + 1)
                        act.copy(dt_rows[:, 0:w], psA[0:DTR, 0, 0:w])
                        act.copy(parts[:, 1 - u, 0:w], psA[:, 0, 0:w]).then_inc(part1_ready, 1)

                    def part2():
                        w = width(GATES)
                        act.wait_ge(rest1_ready, b + 1)
                        act.copy(parts[64:128, 1 - u, 0:w], rest[64:128, 0:w]).then_inc(part2_ready, 1)

                    def part3():
                        w = width(GATES)
                        act.wait_ge(rest2_ready, b + 1)
                        act.copy(parts[96:128, 1 - u, 0:w], rest[96:128, 0:w]).then_inc(parts_ready, 1)

                    def magnitude():
                        w = width(GATES)
                        act.wait_ge(dt_done, b + 1)
                        if later(i, 2):
                            act.wait_ge(dt_ready, b)
                        for half in range(2):
                            last = act.activation(mag[:, half, 0:w], psA[:, half, 0:w], ACT.Abs, bias=dt_b[:, half])
                        link(last)
                        for half in range(2):
                            act.activation(pos[:, half, 0:w], psA[:, half, 0:w], ACT.Relu, bias=dt_b[:, half])
                        act.activation(mag[:, :, 0:w], mag[:, :, 0:w], ACT.Exp, scale=-1.0).then_inc(dt_left, 1)

                    def series_start():
                        w = width(GATES)
                        act.wait_ge(dt_left, b + 1)
                        act.activation(square[:, :, 0:w], mag[:, :, 0:w], ACT.Square)
                        act.activation(series[:, :, 0:w], mag[:, :, 0:w], ACT.Copy, scale=LOG1P[0], bias=LOG1P[1]).then_inc(mag_ready, 1)

                    def pairs(degrees):
                        w = width(GATES)
                        for q in degrees:
                            act.activation(pair[:, q, :, 0:w], mag[:, :, 0:w], ACT.Copy, scale=LOG1P[8 - 2 * q], bias=LOG1P[9 - 2 * q]
                                           ).then_inc(pair_ready, 1)

                    def copy_out():
                        tiles = width(LEAVE) // TP
                        act.wait_ge(out_done, e + 1)
                        if later(i, LEAVE + 1):
                            act.wait_ge(stored, e * 16)
                        act.copy(yrows[:, 0:tiles], psO[:, 0:tiles]).then_inc(out_copied, 1)

                    pieces = {n: [] for n in range(DSTATE)}
                    if on(PROJECT):
                        pieces[1].append(copy_rows)
                        pieces[3].append(copy_main)
                    if on(LEAVE):
                        pieces[11].append(copy_out)
                    if on(GATES):
                        for n, piece in ((0, gate_conv), (5, part1), (7, part2), (7, magnitude), (8, series_start), (9, lambda: pairs((3, 2))),
                                         (10, lambda: pairs((1, 0))), (11, part3), (13, copy_z)):
                            pieces[n].append(piece)
                    for n in range(DSTATE):
                        if on(SCAN):
                            w = width(SCAN)
                            if n == 0:
                                act.wait_ge(dt_ready, c + 1)
                            if n >= 2 or later(i, SCAN + 1):
                                act.wait_ge(scanned, c * DSTATE + n - 1)
                            for half in range(2):
                                last = act.activation(decay[:, n % 2, half, 0:w], dt[:, u, half, 0:w], ACT.Exp, scale=a_neg[:, half, n:n + 1])
                            last.then_inc(decay_ready, 1)
                        for piece in pieces[n]:
                            piece()

                turns(act, turn)

            @block.gpsimd
            def _(pool):
                link = Link(pool, link_g)
                pool.memset(x_w[:, :, :], 0.0).then_inc(pad_ready, 1)
                pool.wait_ge(init_ready, 1)
                pool.wait_ge(den_out, 16)

                def turn(i, u, on, width):
                    a, b, c, e = (i - lag for lag in range(4))
                    link.restart()
                    if on(GATES):
                        w = width(GATES)
                        hold(pool, tanh_ready, b + 1)
                        if later(i, LEAVE):
                            hold(pool, y_ready, b - 1)
                        pool.tensor_tensor(xc[:, 1 - u, :, 0:w], tconv[:, :, 0:w], conv[:, :, 0:w], ALU.mult).then_inc(xc_ready, 1)
                        hold(pool, mag_ready, b + 1)
                        s = series[:, :, 0:w]
                        for q in (3, 2, 1, 0):
                            link(pool.tensor_tensor(s, s, square[:, :, 0:w], ALU.mult))
                            hold(pool, pair_ready, b * 4 + 4 - q)
                            link(pool.tensor_tensor(s, s, pair[:, q, :, 0:w], ALU.add))
                        link(pool.tensor_tensor(s, s, mag[:, :, 0:w], ALU.mult))
                        if later(i, LEAVE):
                            hold(pool, decay_ready, (b - 1) * DSTATE)
                            hold(pool, bx_ready, (b - 1) * DSTATE)
                        pool.tensor_tensor(dt[:, 1 - u, :, 0:w], s, pos[:, :, 0:w], ALU.add).then_inc(dt_ready, 1)
                        hold(pool, dt_ready, b + 1)
                        pool.tensor_tensor(dtx[:, 1 - u, :, 0:w], dt[:, 1 - u, :, 0:w], xc[:, 1 - u, :, 0:w], ALU.mult).then_inc(dtx_ready, 1)
                        hold(pool, z_copied, b + 1)
                        pool.tensor_tensor(zs[:, 1 - u, :, 0:w], tz[:, :, 0:w], z[:, :, 0:w], ALU.mult).then_inc(zs_ready, 1)

                turns(pool, turn)

            @block.vector
            def _(v):
                link = Link(v, link_v)
                v.memset(state[:, :, :], 0.0)
                v.memset(xin[:, :, 0:DCONV - 1], 0.0)
                link(v.tensor_tensor(rest[:, 0:BC], K.ident[:, 32:64], K.ident[:, 64:96], ALU.add))
                v.tensor_tensor(pick[:, :], rest[:, 0:BC], K.ident[:, 96:128], ALU.add)
                v.wait_ge(params_in, 16 * 12)
                v.tensor_scalar(conv_w[:, :, :], conv_w[:, :, :], 0.5, None, ALU.mult)
                v.tensor_scalar(conv_b[:, :, :], conv_b[:, :, :], 0.5, None, ALU.mult)
                v.wait_ge(a_ready, 1)
                v.tensor_scalar(a_neg[:, :, :], a_neg[:, :, :], -1.0, None, ALU.mult).then_inc(init_ready, 1)
                v.wait_ge(init_ready, 1)

                def turn(i, u, on, width):
                    a, b, c, e = (i - lag for lag in range(4))
                    link.restart()

                    def rest1():
                        w = width(GATES)
                        v.wait_ge(part1_ready, b + 1)
                        v.tensor_tensor(rest[64:128, 0:w], psA[64:128, 0, 0:w], parts[64:128, 1 - u, 0:w], ALU.subtract).then_inc(rest1_ready, 1)

                    def rest2():
                        w = width(GATES)
                        v.wait_ge(part2_ready, b + 1)
                        v.tensor_tensor(rest[96:128, 0:w], rest[96:128, 0:w], parts[96:128, 1 - u, 0:w], ALU.subtract).then_inc(rest2_ready, 1)

                    def convolve():
                        w = width(PROJECT)
                        v.wait_ge(main_copied, a + 1)
                        if on(GATES):
                            v.wait_ge(xc_ready, b + 1)
                        for half in range(2):
                            last = v.tensor_scalar(conv[:, half, 0:w], xin[:, half, 3:3 + w], conv_w[:, half, 3:4], conv_b[:, half], ALU.mult, ALU.add)
                        link(last)
                        for k in range(DCONV - 1):
                            for half in range(2):
                                last = v.scalar_tensor_tensor(conv[:, half, 0:w], xin[:, half, k:k + w], conv_w[:, half, k:k + 1],
                                                              conv[:, half, 0:w], ALU.mult, ALU.add)
                            if k < DCONV - 2:
                                link(last)
                        last.then_inc(conv_ready, 1)

                    def finish():
                        w = width(LEAVE)
                        v.wait_ge(y_summed, (e + 1) * DSTATE)
                        v.wait_ge(zs_ready, e + 1)
                        if later(i, LEAVE + 1):
                            v.wait_ge(out_done, e)
                        for half in range(2):
                            last = v.scalar_tensor_tensor(y[:, half, 0:w], xc[:, 1 - u, half, 0:w], d_par[:, half], psY[:, half, 0:w], ALU.mult, ALU.add)
                        last.then_inc(y_left, 1)
                        v.wait_ge(y_left, e + 1)
                        v.tensor_tensor(y[:, :, 0:w], y[:, :, 0:w], zs[:, 1 - u, :, 0:w], ALU.mult).then_inc(y_ready, 1)

                    def drive(n):
                        w = width(SCAN)
                        v.wait_ge(b_done, c * DSTATE + n + 1)
                        v.tensor_tensor(bx[:, n % 2, :, 0:w], dtx[:, u, :, 0:w], psB[:, 0:w].unsqueeze(1).to_broadcast([128, 2, w]), ALU.mult
                                        ).then_inc(bx_ready, 1)

                    if on(SCAN):
                        v.wait_ge(dtx_ready, c + 1)
                        drive(0)
                    for n in range(DSTATE):
                        if on(SCAN):
                            w = width(SCAN)
                            at = c * DSTATE + n + 1
                            v.wait_ge(bx_ready, at)
                            v.wait_ge(decay_ready, at)
                            if n >= 2 or later(i, SCAN + 1):
                                v.wait_ge(hc_ready, at - 2)
                            for half in range(2):
                                last = v.tensor_tensor_scan(h[n % 2][:, half, 0:w], decay[:, n % 2, half, 0:w], bx[:, n % 2, half, 0:w],
                                                            state[:, half, n:n + 1], ALU.mult, ALU.add)
                            last.then_inc(scanned, 1)
                            if n + 1 < DSTATE:
                                drive(n + 1)
                        if n == 0 and on(LEAVE):
                            finish()
                        if n == 4 and on(PROJECT):
                            convolve()
                        if n == 5 and on(GATES):
                            rest1()
                        if n == 8 and on(GATES):
                            rest2()
                        if on(SCAN):
                            v.wait_ge(scanned, at)
                            v.tensor_copy(state[:, :, n:n + 1], h[n % 2][:, :, w - 1:w])
                            v.wait_ge(c_done, at)
                            if n >= 2 or later(i, SCAN + 1):
                                v.wait_ge(y_summed, at - 2)
                            v.tensor_tensor(hc[:, n % 2, :, 0:w], h[n % 2][:, :, 0:w], psC[:, 0:w].unsqueeze(1).to_broadcast([128, 2, w]), ALU.mult
                                            ).then_inc(hc_ready, 1)

                turns(v, turn)
        M.close()


def edge_pass(nc, A, S, K, weighted):
    CREDIT = 4
    DONE = lambda n: n + 1 + CREDIT
    QUADS = NSB // 4
    PIECES = [(0, 1562), (1562, 3124), (3124, 4686), (4686, N)]
    assert QUADS == TILES
    table = S.proj if weighted else S.x1d
    width = ROW if weighted else D
    cols = ROW + 1 if weighted else D
    with ExitStack() as stack:
        M = Parts(nc, stack, "gat_" if weighted else "gcn_")
        base = M.sb("base", [128, NSB])
        base_i = M.sb("base_i", [1, NSB], I32)
        src = M.sb("src", [TP, 4, KB], I32)
        dst = M.sb("dst", [TP, 4, KB], I32)
        rows = M.sb("rows", [TP, 4, KB, width])
        rel = M.sb("rel", [TP, 4, KB])
        sel = M.sb("sel", [TP, 4, KB, W])
        part = M.sb("part", [W, 2, cols])
        psA = [M.ps(f"psA{i}", [W, 512]) for i in range(2)]
        psT = [M.ps(f"psT{i}", [128, 512]) for i in range(2)]
        if weighted:
            dstrow = M.sb("dstrow", [W, 2, EDGES_SB], I32)
            tscore = M.sb("tscore", [W, 2, SPLITS * HEADS], BF16)
            selT = M.sb("selT", [W, 2, EDGES_SB], BF16)
            tsum = M.sb("tsum", [TP, KB, HEADS])
            wrows = M.sb("wrows", [TP, 2, KB, cols])
            below = M.sb("below", [TP, KB])
            above = M.sb("above", [TP, KB])
            outside = M.sb("outside", [TP, 4, KB])
            score = M.sb("score", [TP, KB, HEADS])
            bound = M.sb("bound", [TP, KB, HEADS])
            masked = M.sb("masked", [TP, KB, HEADS])
            expo = M.sb("expo", [TP, 2, KB, HEADS])
            emax = M.sb("emax", [TP, KB, HEADS])
            emax1 = M.sb("emax1", [TP, 1])
            emaxall = M.sb("emaxall", [TP, TP])
            degrow = M.sb("degrow", [TILES, TP])
            noise = M.sb("noise", [TILES, TP])
            keyrow = M.sb("keyrow", [TILES, TP])
            keycol = M.sb("keycol", [TP, TILES])
            keys = M.sb("keys", [TP, N])
            tri = M.sb("tri", [TP, TP])
            seen = M.sb("seen", [TP, PIECES[-1][1] - PIECES[-1][0]], BF16)
            lowered = M.sb("lowered", [TP, 2, TP])
            psb = [M.ps(f"psb{i}", [TP, KB, SPLITS, HEADS]) for i in range(2)]

        src_in = [M.sem(f"src_in{i}") for i in range(4)]
        dst_in = [M.sem(f"dst_in{i}") for i in range(4)]
        dstrow_in = [M.sem(f"dstrow_in{i}") for i in range(2)]
        tscore_in = [M.sem(f"tscore_in{i}") for i in range(2)]
        rows_in = [M.sem(f"rows_in{i}") for i in range(4)]
        base_ready, sel_ready, b_done, scored, w_ready, weighed = (
            M.sem(n) for n in ("base_ready", "sel_ready", "b_done", "scored", "w_ready", "weighed"))
        summed, copied, turned, added = (M.sem(n) for n in ("summed", "copied", "turned", "added"))
        emax_ready, emax_out, emax_in = (M.sem(n) for n in ("emax_ready", "emax_out", "emax_in"))
        link_v, ticks, credited = M.sem("link_v"), M.sem("ticks"), M.sem("credited")
        key_parts_in, key_ready, key_out, keys_in, col_done, col_copied = (
            M.sem(n) for n in ("key_parts_in", "key_ready", "key_out", "keys_in", "col_done", "col_copied"))
        rows_used = weighed if weighted else summed

        def in_rounds(eng, before, step, after):
            turns = eng.value_load(K.rounds[0:1, 0:1], min_val=1, max_val=-(-N // W))
            with eng.Fori(0, turns) as r:
                before(r)
                for u in range(4):
                    step(r * QUADS, 0, u)
                with eng.Fori(1, QUADS - 1) as q:
                    for u in range(4):
                        step(r * QUADS + q, q, u)
                for u in range(4):
                    step(r * QUADS + QUADS - 1, QUADS - 1, u)
                after(r)

        def nothing(r):
            pass

        def hold(eng, sem, value):
            eng.wait_ge(sem, value)
            eng.sem_inc(ticks, 1)

        with nc.Block() as block:
            @block.sync
            def _(sp):
                sp.wait_ge(credited, 1)

                def before(r):
                    hold(sp, base_ready, r + 1)

                def step(m, q, u):
                    s = q * 4 + u
                    n = m * 4 + u
                    hold(sp, summed, DONE(n - 4))
                    sp.dma_start(src[:, u], A.src_cols[bass.ds(s, 1)].rearrange("a p k -> (a p) k")).then_inc(src_in[u], 16)
                    sp.dma_start(dst[:, u], A.dst_cols[bass.ds(s, 1)].rearrange("a p k -> (a p) k")).then_inc(dst_in[u], 16)
                    if weighted:
                        hold(sp, b_done, DONE(n - 2))
                        at = sp.value_load(base_i[0:1, bass.ds(s, 1)], min_val=0, max_val=N)
                        sp.dma_start(dstrow[:, u % 2], A.dst[bass.ds(s * EDGES_SB, EDGES_SB)].partition_broadcast(W)
                                     ).then_inc(dstrow_in[u % 2], 16)
                        sp.dma_start(tscore[:, u % 2], S.stgt[bass.ds(at, W), :]).then_inc(tscore_in[u % 2], 16)

                in_rounds(sp, before, step, nothing)
                if weighted:
                    sp.wait_ge(emax_ready, 1)
                    sp.dma_start(S.emax.rearrange("(p a) -> p a", a=1), emax1[:, :]).then_inc(emax_out, 16)
                    sp.wait_ge(emax_out, 16)
                    sp.dma_start(emaxall[:, :], S.emax.partition_broadcast(TP)).then_inc(emax_in, 16)

            @block.gpsimd
            def _(pool):
                pool.wait_ge(credited, 1)

                def step(m, q, u):
                    s = q * 4 + u
                    hold(pool, src_in[u], (m + 1) * 16)
                    hold(pool, rows_used, DONE(m * 4 + u - 4))
                    for k in range(KB):
                        pool.indirect_dma_start(rows[:, u, k, :], None, table,
                                                bass.IndirectOffsetOnAxis(ap=src[:, u, k:k + 1], axis=0)).then_inc(rows_in[u], 16)

                in_rounds(pool, nothing, step, nothing)

            @block.tensor
            def _(pe):
                if weighted:
                    pe.wait_ge(key_ready, 1)
                    nc.tensor.transpose(psT[0][0:TP, 0:TILES], keyrow[:, :],
                                        K.ident[0:TILES, 0:TILES]).then_inc(col_done, 1)
                    pe.wait_ge(col_copied, 1)
                pe.wait_ge(credited, 1)

                def target_scores(m, u):
                    n = m * 4 + u
                    pe.wait_ge(sel_ready, n + 1)
                    pe.wait_ge(tscore_in[u % 2], (m * 2 + u // 2 + 1) * 16)
                    pe.wait_ge(scored, DONE(n - 2))
                    for k in range(KB):
                        last = nc.tensor.matmul(psb[u % 2][:, k], selT[:, u % 2, k * TP:(k + 1) * TP],
                                                tscore[:, u % 2], start=True, stop=True)
                    last.then_inc(b_done, 1)

                def before(r):
                    if weighted:
                        target_scores(r * QUADS, 0)

                def step(m, q, u):
                    s = q * 4 + u
                    n = m * 4 + u
                    if weighted and not (isinstance(s, int) and s == NSB - 1):
                        target_scores(m + (u + 1) // 4, (u + 1) % 4)
                    if weighted:
                        pe.wait_ge(weighed, DONE(n))
                    else:
                        pe.wait_ge(sel_ready, n + 1)
                        pe.wait_ge(rows_in[u], (m + 1) * 16 * KB)
                    pe.wait_ge(copied, DONE(n - 2))
                    for k in range(KB):
                        right = wrows[:, u % 2, k] if weighted else rows[:, u, k]
                        last = nc.tensor.matmul(psA[u % 2][:, 0:cols], sel[:, u, k], right, start=(k == 0), stop=(k == KB - 1))
                    last.then_inc(summed, 1)
                    hold(pe, added, DONE(n - 2))
                    hold(pe, copied, DONE(n))
                    for half in range(2):
                        last = nc.tensor.transpose(psT[u % 2][:, half * W:(half + 1) * W], part[:, u % 2, half * 128:(half + 1) * 128],
                                                   K.ident[0:W, 0:W])
                    if weighted:
                        last = nc.tensor.transpose(psT[u % 2][0:HEADS + 1, 2 * W:3 * W], part[:, u % 2, D:], K.ident[0:W, 0:W])
                    last.then_inc(turned, 1)

                in_rounds(pe, before, step, nothing)

            @block.scalar
            def _(act):
                if weighted:
                    act.dma_start(degrow[:, :], S.deg[0:N].rearrange("(t p) -> t p", p=TP)).then_inc(key_parts_in, 16)
                    act.dma_start(noise[:, :], A.node_vec.rearrange("(t p) -> t p", p=TP)).then_inc(key_parts_in, 16)
                    act.dma_start(tri[:, :], A.tri).then_inc(key_parts_in, 16)
                    act.wait_ge(key_ready, 1)
                    act.dma_start(S.key.rearrange("(t p) -> t p", p=TP), keyrow[:, :]).then_inc(key_out, 16)
                    act.wait_ge(col_done, 1)
                    act.copy(keycol[:, :], psT[0][0:TP, 0:TILES]).then_inc(col_copied, 1)
                    act.wait_ge(key_out, 16)
                act.wait_ge(credited, 1)

                def before(r):
                    if weighted:
                        hold(act, base_ready, r + 1)
                        act.dma_start(keys[:, :], S.key.partition_broadcast(TP)).then_inc(keys_in, 16)

                def copy_sums(n, u):
                    act.wait_ge(summed, DONE(n))
                    act.wait_ge(turned, DONE(n - 2))
                    act.copy(part[:, u % 2], psA[u % 2][:, 0:cols]).then_inc(copied, 1)

                def step(m, q, u):
                    n = m * 4 + u
                    if weighted:
                        act.wait_ge(scored, DONE(n))
                        act.wait_ge(summed, DONE(n - 2))
                        act.activation(wrows[:, u % 2, :, D:ROW], expo[:, u % 2], ACT.Exp).then_inc(w_ready, 1)
                    if not (isinstance(q, int) and q == 0 and u == 0):
                        copy_sums(n - 1, (u - 1) % 4)

                def after(r):
                    copy_sums((r + 1) * NSB - 1, 3)

                in_rounds(act, before, step, after)

            @block.vector
            def _(v):
                link = Link(v, link_v)
                for sem in (summed, b_done, copied, turned, added, scored, w_ready, weighed):
                    v.sem_inc(sem, CREDIT)
                link(v.tensor_copy(base[:, :], K.low[:, :]))
                link(v.tensor_copy(base_i[:, :], base[0:1, :]))
                v.sem_inc(base_ready, 1)
                v.sem_inc(credited, 1)
                if weighted:
                    v.wait_ge(key_parts_in, 48)
                    v.tensor_tensor(keyrow[:, :], degrow[:, :], noise[:, :], ALU.add).then_inc(key_ready, 1)
                    v.memset(wrows[:, :, :, ROW:], 1.0)
                    v.memset(emax[:, :, :], NEG)
                    v.memset(K.den[:, :], 0.0)
                    link(v.memset(K.sums[:, :, :], 0.0))
                    v.wait_ge(col_copied, 1)

                def rank_piece(t, u):
                    a, b = PIECES[u]
                    key = keycol[:, bass.ds(t, 1)]
                    link.note(v.tensor_scalar(seen[:, 0:b - a], keys[:, a:b], key, 0.0, ALU.is_lt, ALU.add,
                                              accum_out=K.smaller[:, bass.ds(t * 4 + u, 1)]))
                    if u == 3:
                        own = keys[:, bass.ds(t * TP, TP)]
                        v.tensor_scalar(lowered[:, 0], own, 2.0 ** -24, None, ALU.mult)
                        link.note(v.tensor_scalar(lowered[:, 1], own, 0.0, -1e-30, ALU.is_equal, ALU.mult))
                        link.need()
                        link(v.scalar_tensor_tensor(seen[:, 0:TP], own, key, tri[:, :], ALU.is_equal, ALU.mult,
                                                    accum_out=K.ties[:, bass.ds(t, 1)]))
                        link(v.scalar_tensor_tensor(lowered[:, 0], own, -2.0 ** -24, lowered[:, 0], ALU.mult, ALU.min))
                        link(v.tensor_tensor(own, own, lowered[:, 0], ALU.add))
                        link(v.tensor_tensor(own, own, lowered[:, 1], ALU.add))

                def select(m, s, u, stage):
                    n = m * 4 + u
                    if stage == 0:
                        v.wait_ge(dst_in[u], (m + 1) * 16)
                        v.wait_ge(summed, DONE(n - 4))
                        link.note(v.tensor_scalar(rel[:, u], dst[:, u], base[0:TP, bass.ds(s, 1)], None, ALU.subtract))
                    elif stage == 1 and weighted:
                        v.tensor_scalar(below[:, :], rel[:, u], 0.0, NEG / 4, ALU.is_lt, ALU.mult)
                        link.note(v.tensor_scalar(above[:, :], rel[:, u], float(W - 1), NEG / 4, ALU.is_gt, ALU.mult))
                    elif stage == 2 and weighted:
                        link.note(v.tensor_tensor(outside[:, u], below[:, :], above[:, :], ALU.add))
                    elif stage == 3:
                        out = v.tensor_tensor(sel[:, u], rel[:, u].unsqueeze(2).to_broadcast([TP, KB, W]),
                                              K.iota[0:TP, 0:W].unsqueeze(1).to_broadcast([TP, KB, W]), ALU.is_equal)
                        if weighted:
                            v.wait_ge(dstrow_in[u % 2], (m * 2 + u // 2 + 1) * 16)
                            v.wait_ge(b_done, DONE(n - 2))
                            out = v.tensor_scalar(selT[:, u % 2], dstrow[:, u % 2], base[0:W, bass.ds(s, 1)], K.pidx[0:W, 0:1],
                                                  ALU.subtract, ALU.is_equal)
                        out.then_inc(sel_ready, 1)

                def scores(m, s, u, stage):
                    n = m * 4 + u
                    b = tsum[:, :, :]
                    if stage == 0:
                        v.wait_ge(b_done, DONE(n))
                        link.note(v.tensor_reduce(b, psb[u % 2][:, :, :, :].rearrange("p k c h -> p k h c"), axis=AX.X, op=ALU.add))
                    elif stage == 1:
                        v.tensor_tensor(bound[:, :, :], b, K.smax[:, :].unsqueeze(1).to_broadcast([TP, KB, HEADS]), ALU.add)
                        v.wait_ge(rows_in[u], (m + 1) * 16 * KB)
                        link.note(v.tensor_tensor(score[:, :, :], rows[:, u, :, D:ROW], b, ALU.add))
                    elif stage == 2:
                        v.scalar_tensor_tensor(bound[:, :, :], bound[:, :, :], 0.2, bound[:, :, :], ALU.mult, ALU.max)
                        link.note(v.scalar_tensor_tensor(score[:, :, :], score[:, :, :], 0.2, score[:, :, :], ALU.mult, ALU.max))
                    elif stage == 3:
                        v.wait_ge(w_ready, DONE(n - 2))
                        v.tensor_tensor(expo[:, u % 2], score[:, :, :], bound[:, :, :], ALU.subtract).then_inc(scored, 1)
                        link.note(v.tensor_tensor(masked[:, :, :], score[:, :, :], outside[:, u].unsqueeze(2).to_broadcast([TP, KB, HEADS]), ALU.add))
                    elif stage == 4:
                        link.note(v.tensor_tensor(emax[:, :, :], emax[:, :, :], masked[:, :, :], ALU.max))

                def window(s):
                    return v.value_load(base_i[0:1, bass.ds(s, 1)], min_val=0, max_val=N)

                def add_sums(m, u, at):
                    n = m * 4 + u
                    hold(v, turned, DONE(n))
                    hold(v, added, DONE(n - 1))
                    there = K.sums[:, :, bass.ds(at, W)]
                    if weighted:
                        v.tensor_tensor(K.den[:, bass.ds(at, W)], K.den[:, bass.ds(at, W)], psT[u % 2][0:HEADS + 1, 2 * W:3 * W], ALU.add)
                    v.tensor_tensor(there, there, psT[u % 2][:, 0:2 * W].rearrange("p (k w) -> p k w", k=2), ALU.add).then_inc(added, 1)

                def weigh(m, s, u):
                    v.wait_ge(w_ready, DONE(m * 4 + u))
                    v.tensor_tensor(wrows[:, u % 2, :, 0:D].rearrange("p k (h f) -> p k h f", h=HEADS),
                                    rows[:, u, :, 0:D].rearrange("p k (h f) -> p k h f", h=HEADS),
                                    wrows[:, u % 2, :, D:ROW].unsqueeze(3).to_broadcast([TP, KB, HEADS, HD]), ALU.mult).then_inc(weighed, 1)

                def before(r):
                    link.restart()
                    for u in range(2):
                        for stage in range(4):
                            select(r * QUADS, u, u, stage)
                            link.need()
                    if weighted:
                        hold(v, keys_in, (r + 1) * 16)

                def step(m, q, u):
                    s = q * 4 + u
                    known = isinstance(s, int)
                    if u == 0:
                        link.restart()
                    for stage in range(5):
                        if weighted:
                            scores(m, s, u, stage)
                        if not (known and s >= NSB - 2):
                            select(m + (u + 2) // 4, s + 2, (u + 2) % 4, stage)
                        if weighted or stage == 0:
                            link.need()
                    if weighted:
                        weigh(m, s, u)
                    at = None if known and s == 0 else window(s - 1)
                    if weighted:
                        rank_piece(q, u)
                    if at is not None:
                        add_sums(m - (1 if u == 0 else 0), (u - 1) % 4, at)
                    if known and s == NSB - 1:
                        add_sums(m, u, window(s))

                def after(r):
                    link.restart()
                    link(v.tensor_scalar(base[:, :], base[:, :], float(W), float(N), ALU.add, ALU.min))
                    v.tensor_copy(base_i[:, :], base[0:1, :]).then_inc(base_ready, 1)

                in_rounds(v, before, step, after)
                if weighted:
                    link.restart()
                    v.tensor_reduce(emax1[:, :], emax[:, :, :], axis=AX.XY, op=ALU.max).then_inc(emax_ready, 1)
                    v.wait_ge(emax_in, 16)
                    link(v.tensor_reduce(K.emax[:, :], emaxall[:, :], axis=AX.X, op=ALU.max))
        M.close()


def nodes_block(nc, A, S, K):
    G = 2
    GN = G * TP
    GROUPS = N // GN
    ENTER, MIX, FEED, LEAVE = range(4)
    TURNS = GROUPS + LEAVE
    assert TURNS % 4 == 0
    with ExitStack() as stack:
        M = Parts(nc, stack, "node_")
        wgate = M.sb("wgate", [128, 4, D])
        ff1 = M.sb("ff1", [128, 2, 2 * D])
        ff2 = M.sb("ff2", [128, 4, D])
        ff1_b = M.sb("ff1_b", [128, 4])
        vecs = M.sb("vecs", [TP, 8, D])
        x = M.sb("x", [TP, 4, G, D])
        ym = M.sb("ym", [TP, 2, G, D])
        tsc = M.sb("tsc", [TP, 2, G, SPLITS, HEADS], BF16)
        rank = M.sb("rank", [TP, 2, G], I32)
        sumsT = M.sb("sumsT", [128, 2, GN])
        denT = M.sb("denT", [HEADS + 1, GN])
        eps_e = M.sb("eps_e", [TP, G, HEADS])
        den = M.sb("den", [TP, G, HEADS])
        dinv = M.sb("dinv", [TP, 4, G])
        pre = M.sb("pre", [TP, G, D])
        low = M.sb("low", [TP, G, D])
        pos = M.sb("pos", [TP, G, D])
        hl = M.sb("hl", [TP, 2, G, D])
        ha = M.sb("ha", [TP, 2, G, D])
        gate = M.sb("gate", [TP, G, D])
        h = M.sb("h", [TP, 2, G, D])
        f = M.sb("f", [TP, G, D])
        x1 = M.sb("x1", [TP, 2, G, D])
        x1d = M.sb("x1d", [TP, 2, G, D])
        gT = M.sb("gT", [128, 4, GN])
        hT = M.sb("hT", [128, 2, GN])
        rT = M.sb("rT", [128, 4, GN])
        stats = M.sb("stats", [TP, 5, G, 6])
        mv = M.sb("mv", [TP, 5, G, 2])
        var, rstd, half, square = (M.sb(n, [TP, 5, G]) for n in ("var", "rstd", "half", "square"))
        GLOBAL, DEGREE, FORWARD, LOCAL, LAST = range(5)
        psR = M.ps("psR", [TP, G, 512])
        psT = M.ps("psT", [128, 2, 512])
        psG = M.ps("psG", [TP, G, 512])
        psF = M.ps("psF", [128, 2, 512])
        GAT_B, LL_G, LL_B, LG_G, LG_B, L2_G, L2_B, FF2_B = range(8)

        weights_in, rank_ready = (M.sem(n) for n in ("weights_in", "rank_ready"))
        stored = [M.sem(f"stored{i}") for i in range(2)]
        x_in = [M.sem(f"x_in{i}") for i in range(4)]
        tsc_in = [M.sem(f"tsc_in{i}") for i in range(2)]
        ym_in = [M.sem(f"ym_in{i}") for i in range(2)]
        slices_ready, rows_turned, bound_ready, eps_ready, rows_used = (
            M.sem(n) for n in ("slices_ready", "rows_turned", "bound_ready", "eps_ready", "rows_used"))
        pre_ready, elu_ready, normed, g_turned, g_copied = (M.sem(n) for n in ("pre_ready", "elu_ready", "normed", "g_turned", "g_copied"))
        gate_done, gate_ready, h_ready, h_turned, h_copied = (M.sem(n) for n in ("gate_done", "gate_ready", "h_ready", "h_turned", "h_copied"))
        ff1_done, relu_ready, ff2_done, ff2_used, x1_ready, x1_turned, x1_copied = (M.sem(n) for n in (
            "ff1_done", "relu_ready", "ff2_done", "ff2_used", "x1_ready", "x1_turned", "x1_copied"))
        link_v, ticks = (M.sem(n) for n in ("link_v", "ticks"))

        def hold(eng, sem, value):
            eng.wait_ge(sem, value)
            eng.sem_inc(ticks, 1)

        def turns(eng, turn):
            def run(i, u):
                known = isinstance(i, int)
                turn(i, u, lambda lag: not known or 0 <= i - lag < GROUPS)

            for u in range(4):
                run(u, u)
            with eng.Fori(1, TURNS // 4 - 1) as q:
                for u in range(4):
                    run(q * 4 + u, u)
            for u in range(4):
                run(TURNS - 4 + u, u)

        def by_group(dram, g):
            return dram.rearrange("(g j p) c -> g p j c", j=G, p=TP)[bass.ds(g, 1)].rearrange("a p j c -> (a p) j c")

        def later(i, n):
            return not isinstance(i, int) or i >= n

        with nc.Block() as block:
            @block.sync
            def _(sp):
                for t, a in ((wgate[:, 0:2], A.wlT), (wgate[:, 2:4], A.wgT), (ff1[:, :, :], A.ff1_wT), (ff2[:, :, :], A.ff2_wT)):
                    sp.dma_start(t, a.rearrange("(k p) n -> p k n", p=128)).then_inc(weights_in, 16)
                sp.dma_start(ff1_b[:, :], A.ff1_b).then_inc(weights_in, 16)
                sp.dma_start(vecs[:, :, :], A.rowvecs.partition_broadcast(TP)).then_inc(weights_in, 16)

                def load(g, u):
                    sp.dma_start(x[:, u], by_group(A.x, g)).then_inc(x_in[u], 16)
                    sp.dma_start(tsc[:, u % 2].rearrange("p j s h -> p j (s h)"), by_group(S.stgt[0:N], g)).then_inc(tsc_in[u % 2], 16)

                load(0, 0)

                def turn(i, u, on):
                    if on(ENTER) and not (isinstance(i, int) and i + 1 >= GROUPS):
                        if later(i, 1):
                            hold(sp, bound_ready, i)
                        if later(i, 3):
                            hold(sp, x1_ready, i - 2)
                        load(i + 1, (u + 1) % 4)
                    if on(FEED):
                        g = i - FEED
                        hold(sp, x1_ready, g + 1)
                        sp.dma_start(by_group(S.x1, g), x1[:, u % 2]).then_inc(stored[(u - FEED) % 2], 16)
                        sp.dma_start(by_group(S.x1d, g), x1d[:, u % 2]).then_inc(stored[(u - FEED) % 2], 16)
                        with nc.allow_non_contiguous_dma(reason="one value a node"):
                            sp.dma_start(by_group(S.dinv.rearrange("(n c) -> n c", c=1), g),
                                         dinv[:, (u - FEED) % 4].unsqueeze(2)).then_inc(stored[(u - FEED) % 2], 16)

                turns(sp, turn)
                sp.wait_ge(stored[0], 48 * ((GROUPS + 1) // 2))
                sp.wait_ge(stored[1], 48 * (GROUPS // 2))

            @block.gpsimd
            def _(pool):
                def turn(i, u, on):
                    if on(ENTER):
                        if later(i, 2):
                            hold(pool, rows_used, i - 1)
                        pool.tensor_copy(rank[:, u % 2], K.rank[:, bass.ds(i * G, G)]).then_inc(rank_ready, 1)
                        hold(pool, rank_ready, i + 1)
                        for j in range(G):
                            pool.indirect_dma_start(ym[:, u % 2, j, :], None, S.ys,
                                                    bass.IndirectOffsetOnAxis(ap=rank[:, u % 2, j:j + 1], axis=0)).then_inc(ym_in[u % 2], 16)

                turns(pool, turn)

            @block.tensor
            def _(pe):
                pe.wait_ge(weights_in, 96)
                small = K.ident[0:TP, 0:TP]

                def turn(i, u, on):
                    if on(ENTER):
                        hold(pe, slices_ready, i + 1)
                        if later(i, 1):
                            hold(pe, rows_used, i)
                        for j in range(G):
                            for k in range(2):
                                nc.tensor.transpose(psR[:, j, k * 128:(k + 1) * 128], sumsT[:, k, j * TP:(j + 1) * TP], K.ident[:, :])
                            last = nc.tensor.transpose(psR[:, j, D:D + HEADS + 1], denT[:, j * TP:(j + 1) * TP], K.ident[0:HEADS + 1, 0:HEADS + 1])
                        last.then_inc(rows_turned, 1)
                    if on(LEAVE):
                        g = i - LEAVE
                        s = (u - LEAVE) % 2
                        hold(pe, x1_ready, g + 1)
                        if later(i, LEAVE + 1):
                            hold(pe, x1_copied, g)
                        for j in range(G):
                            for k in range(2):
                                last = nc.tensor.transpose(psT[:, 1, k * GN + j * TP:k * GN + (j + 1) * TP], x1d[:, s, j, k * 128:(k + 1) * 128], small)
                        last.then_inc(x1_turned, 1)
                    if on(MIX):
                        g = i - MIX
                        s = (u - MIX) % 2
                        hold(pe, normed, g + 1)
                        if on(LEAVE) and later(i, LEAVE):
                            hold(pe, x1_copied, i - LEAVE + 1)
                        for j in range(G):
                            for k in range(4):
                                row = (hl, ha)[k // 2][:, s, j, (k % 2) * 128:(k % 2 + 1) * 128]
                                last = nc.tensor.transpose(psT[:, k // 2, (k % 2) * GN + j * TP:(k % 2) * GN + (j + 1) * TP], row, small)
                        last.then_inc(g_turned, 1)
                        hold(pe, g_copied, g + 1)
                        if later(i, FEED):
                            hold(pe, ff2_used, g)
                        for j in range(G):
                            for k in range(4):
                                last = nc.tensor.matmul(psG[:, j, 0:D], gT[:, k, j * TP:(j + 1) * TP], wgate[:, k], start=(k == 0), stop=(k == 3))
                        last.then_inc(gate_done, 1)
                        hold(pe, h_ready, g + 1)
                        for j in range(G):
                            for k in range(2):
                                last = nc.tensor.transpose(psT[:, 0, k * GN + j * TP:k * GN + (j + 1) * TP], h[:, s, j, k * 128:(k + 1) * 128], small)
                        last.then_inc(h_turned, 1)
                        hold(pe, h_copied, g + 1)
                        for m in range(4):
                            for k in range(2):
                                last = nc.tensor.matmul(psF[:, m // 2, (m % 2) * GN:(m % 2 + 1) * GN], ff1[:, k, m * 128:(m + 1) * 128], hT[:, k],
                                                        start=(k == 0), stop=(k == 1))
                        last.then_inc(ff1_done, 1)
                        hold(pe, relu_ready, g + 1)
                        for j in range(G):
                            for k in range(4):
                                last = nc.tensor.matmul(psG[:, j, 0:D], rT[:, k, j * TP:(j + 1) * TP], ff2[:, k], start=(k == 0), stop=(k == 3))
                        last.then_inc(ff2_done, 1)

                turns(pe, turn)

            @block.scalar
            def _(act):
                halves = lambda t: t.rearrange("p (k n) -> p k n", k=2)
                act.wait_ge(weights_in, 96)

                def slices(g, first):
                    if not first:
                        hold(act, rows_turned, g)
                    act.copy(sumsT[:, :, :], K.sums[:, :, bass.ds(g * GN, GN)])
                    act.copy(denT[:, :], K.den[:, bass.ds(g * GN, GN)]).then_inc(slices_ready, 1)

                slices(0, True)

                def turn(i, u, on):
                    if on(LEAVE):
                        g = i - LEAVE
                        hold(act, x1_turned, g + 1)
                        act.copy(K.sums[:, :, bass.ds(g * GN, GN)], halves(psT[:, 1, 0:2 * GN])).then_inc(x1_copied, 1)
                    if on(MIX):
                        g = i - MIX
                        act.wait_ge(g_turned, g + 1)
                        for k in range(2):
                            last = act.copy(gT[:, 2 * k:2 * k + 2], halves(psT[:, k, 0:2 * GN]))
                        last.then_inc(g_copied, 1)
                    if on(ENTER):
                        act.wait_ge(bound_ready, i + 1)
                        act.activation(eps_e[:, :, :], den[:, :, :], ACT.Exp, scale=-1.0, bias=K.emax[:, 0:1]).then_inc(eps_ready, 1)
                        if not (isinstance(i, int) and i + 1 >= GROUPS):
                            slices(i + 1, False)
                    if on(MIX):
                        g = i - MIX
                        act.wait_ge(gate_done, g + 1)
                        if later(i, 2):
                            act.wait_ge(h_ready, g)
                        act.activation(gate[:, :, :], psG[:, :, 0:D], ACT.Tanh, scale=0.5).then_inc(gate_ready, 1)
                        act.wait_ge(h_turned, g + 1)
                        act.copy(hT[:, :, :], halves(psT[:, 0, 0:2 * GN])).then_inc(h_copied, 1)
                    if on(ENTER):
                        act.wait_ge(pre_ready, i + 1)
                        act.activation(pos[:, :, :], pre[:, :, :], ACT.Relu)
                        act.activation(low[:, :, :], low[:, :, :], ACT.Exp).then_inc(elu_ready, 1)
                    if on(MIX):
                        g = i - MIX
                        act.wait_ge(ff1_done, g + 1)
                        for m in range(4):
                            last = act.activation(rT[:, m], psF[:, m // 2, (m % 2) * GN:(m % 2 + 1) * GN], ACT.Relu, bias=ff1_b[:, m:m + 1])
                        last.then_inc(relu_ready, 1)

                turns(act, turn)

            @block.vector
            def _(v):
                link = Link(v, link_v)
                v.wait_ge(weights_in, 96)

                def vec(n):
                    return vecs[:, n].unsqueeze(1).to_broadcast([TP, G, D])

                def moments(at, t):
                    for j in range(G):
                        last = v.bn_stats(stats[:, at, j], t[:, j])
                    link(last)
                    for j in range(G):
                        last = v.bn_aggr(mv[:, at, j], stats[:, at, j])
                    link(last)
                    link.note(v.tensor_scalar(var[:, at], mv[:, at, :, 1], EPS, None, ALU.add))

                def roots(first, end):
                    link.need()
                    rsqrt(v, link, rstd[:, first:end], var[:, first:end], half[:, first:end], square[:, first:end])

                def centre(at, out, t):
                    for j in range(G):
                        last = v.tensor_scalar(out[:, j], t[:, j], mv[:, at, j, 0:1], rstd[:, at, j:j + 1], ALU.subtract, ALU.mult)
                    link.note(last)

                def turn(i, u, on):
                    if u % 2 == 0:
                        link.restart()
                    slot, mix, feed = u % 2, (u - MIX) % 2, (u - FEED) % 2
                    xg, hag, hlg = x[:, u], ha[:, slot], hl[:, slot]
                    if on(ENTER):
                        hold(v, x_in[u], (i - u + 4) * 4)
                        hold(v, tsc_in[slot], (i - slot + 2) * 8)
                        if later(i, 2):
                            hold(v, g_turned, i - 1)
                        link(v.tensor_reduce(den[:, :, :], tsc[:, slot].rearrange("p j s h -> p j h s"), axis=AX.X, op=ALU.add))
                        link(v.tensor_tensor(den[:, :, :], den[:, :, :], K.smax[:, :].unsqueeze(1).to_broadcast([TP, G, HEADS]), ALU.add))
                        v.scalar_tensor_tensor(den[:, :, :], den[:, :, :], 0.2, den[:, :, :], ALU.mult, ALU.max).then_inc(bound_ready, 1)
                        v.wait_ge(ym_in[slot], (i - slot + 2) * 8 * G)
                        link(v.tensor_tensor(hag, xg, ym[:, slot], ALU.add))
                        moments(GLOBAL, hag)
                    if on(FEED):
                        g = i - FEED
                        link(v.tensor_tensor(f[:, :, :], h[:, feed], vec(FF2_B), ALU.add))
                        hold(v, ff2_done, g + 1)
                        v.tensor_tensor(f[:, :, :], f[:, :, :], psG[:, :, 0:D], ALU.add).then_inc(ff2_used, 1)
                        hold(v, ff2_used, g + 1)
                        moments(FORWARD, f[:, :, :])
                    if on(ENTER):
                        hold(v, rows_turned, i + 1)
                        hold(v, eps_ready, i + 1)
                        link.note(v.tensor_scalar(var[:, DEGREE], psR[:, :, D + HEADS], 1.0, None, ALU.add))
                        v.scalar_tensor_tensor(den[:, :, :], eps_e[:, :, :], 1e-16, psR[:, :, D:D + HEADS], ALU.mult, ALU.add)
                    if on(ENTER) or on(FEED):
                        roots(GLOBAL if on(ENTER) else FORWARD, LOCAL if on(FEED) else FORWARD)
                    if on(ENTER):
                        if later(i, 4):
                            hold(v, stored[slot], (i - slot - 2) * 24)
                        v.tensor_copy(dinv[:, u], rstd[:, DEGREE])
                        centre(GLOBAL, hag, hag)
                    if on(FEED):
                        centre(FORWARD, f, f)
                    if on(ENTER):
                        link.note(v.tensor_scalar(den[:, :, :], den[:, :, :], 1e-37, None, ALU.max))
                        link.need()
                        link.note(v.reciprocal(den[:, :, :], den[:, :, :]))
                        v.tensor_tensor(hag, hag, vec(LG_G), ALU.mult)
                        link.need()
                        v.tensor_tensor(pre[:, :, :].rearrange("p j (h f) -> p j h f", h=HEADS),
                                        psR[:, :, 0:D].rearrange("p j (h f) -> p j h f", h=HEADS),
                                        den[:, :, :].unsqueeze(3).to_broadcast([TP, G, HEADS, HD]), ALU.mult).then_inc(rows_used, 1)
                    if on(FEED):
                        link.need()
                        link.note(v.tensor_tensor(f[:, :, :], f[:, :, :], vec(L2_G), ALU.mult))
                    if on(ENTER):
                        hold(v, rows_used, i + 1)
                        link.note(v.tensor_tensor(pre[:, :, :], pre[:, :, :], xg, ALU.add))
                        link.note(v.tensor_tensor(hag, hag, vec(LG_B), ALU.add))
                        link.need()
                        link(v.tensor_tensor(pre[:, :, :], pre[:, :, :], vec(GAT_B), ALU.add))
                        v.tensor_scalar(low[:, :, :], pre[:, :, :], 0.0, None, ALU.min).then_inc(pre_ready, 1)
                    if on(MIX):
                        g = i - MIX
                        if later(i, MIX + 2):
                            hold(v, h_turned, g - 1)
                        link(v.tensor_tensor(h[:, mix], hl[:, mix], ha[:, mix], ALU.subtract))
                        hold(v, gate_ready, g + 1)
                        link(v.scalar_tensor_tensor(h[:, mix], gate[:, :, :], 1.0, h[:, mix], ALU.add, ALU.mult))
                        v.scalar_tensor_tensor(h[:, mix], h[:, mix], 0.5, ha[:, mix], ALU.mult, ALU.add).then_inc(h_ready, 1)
                    if on(FEED):
                        link.need()
                        link(v.tensor_tensor(f[:, :, :], f[:, :, :], vec(L2_B), ALU.add))
                        link(v.tensor_tensor(f[:, :, :], f[:, :, :], x[:, (u - FEED) % 4], ALU.add))
                        moments(LAST, f[:, :, :])
                    if on(ENTER):
                        hold(v, elu_ready, i + 1)
                        link(v.scalar_tensor_tensor(hlg, low[:, :, :], -1.0, pos[:, :, :], ALU.add, ALU.add))
                        moments(LOCAL, hlg)
                    if on(ENTER) or on(FEED):
                        roots(LOCAL if on(ENTER) else LAST, LAST + 1 if on(FEED) else LAST)
                    if on(ENTER):
                        centre(LOCAL, hlg, hlg)
                    if on(FEED):
                        if later(i, FEED + 2):
                            hold(v, stored[feed], ((i - FEED) - feed) * 24)
                            hold(v, x1_turned, (i - FEED) - 1)
                        centre(LAST, x1[:, feed], f)
                    if on(ENTER):
                        link.need()
                        link(v.tensor_tensor(hlg, hlg, vec(LL_G), ALU.mult))
                        v.tensor_tensor(hlg, hlg, vec(LL_B), ALU.add).then_inc(normed, 1)
                    if on(FEED):
                        link.need()
                        for j in range(G):
                            last = v.tensor_scalar(x1d[:, feed, j], x1[:, feed, j], dinv[:, (u - FEED) % 4, j:j + 1], None, ALU.mult)
                        last.then_inc(x1_ready, 1)

                turns(v, turn)
        M.close()


def output_block(nc, A, S, K, out):
    CN = 2 * TP
    CHUNKS = N // CN
    GC = 5
    GROUPS = CHUNKS // GC
    GT = 2 * GC
    assert CHUNKS == GC * GROUPS and GROUPS % 2 == 1 and CHUNKS % 2 == 1
    with ExitStack() as stack:
        M = Parts(nc, stack, "out_")
        w = M.sb("w", [128, 2, D])
        vec = M.sb("vec", [128, 3, 2])
        dinv = M.sb("dinv", [128, N])
        o = M.sb("o", [128, 2, N])
        stats = M.sb("stats", [128, 2, CHUNKS, 6])
        mv = M.sb("mv", [128, 2, 2])
        gain = M.sb("gain", [128, 2])
        shift = M.sb("shift", [128, 2])
        act_o = M.sb("act_o", [128, 2, 2, CN])
        x1 = M.sb("x1", [TP, 2, GT, D])
        y = M.sb("y", [TP, 2, GT, D])
        stat1 = M.sb("stat1", [TP, GT, 6])
        mv1 = M.sb("mv1", [TP, GT, 2])
        var, half, square = (M.sb(n, [128, 2]) for n in ("var", "half", "square"))
        var1, rstd1, half1, square1 = (M.sb(n, [TP, GT]) for n in ("var1", "rstd1", "half1", "square1"))
        psO = M.ps("psO", [128, 2, 2, 512])
        psT = M.ps("psT", [TP, 2, 2, D])
        weights_in, dinv_in, o_done, scaled, o_ready = (M.sem(n) for n in ("weights_in", "dinv_in", "o_done", "scaled", "o_ready"))
        norm_ready, relu_ready, turned, added, y_ready = (M.sem(n) for n in ("norm_ready", "relu_ready", "turned", "added", "y_ready"))
        x1_in, stored = ([M.sem(f"{n}{i}") for i in range(2)] for n in ("x1_in", "stored"))
        link_v, ticks = (M.sem(n) for n in ("link_v", "ticks"))

        def hold(eng, sem, value):
            eng.wait_ge(sem, value)
            eng.sem_inc(ticks, 1)

        def pairs(eng, count, step):
            step(0, 0)
            with eng.Fori(0, count // 2) as q:
                for u in range(2):
                    step(q * 2 + (1 + u), 1 - u)

        def later(c, n):
            return not isinstance(c, int) or c >= n

        def by_group(dram, q):
            return dram.rearrange("(g t p) c -> g p t c", t=GT, p=TP)[bass.ds(q, 1)].rearrange("a p t c -> (a p) t c")

        with nc.Block() as block:
            @block.sync
            def _(sp):
                sp.dma_start(w[:, :, :], A.gcn_w.rearrange("(k p) n -> p k n", p=128)).then_inc(weights_in, 16)
                sp.dma_start(vec[:, :, :], A.colvecs).then_inc(weights_in, 16)
                sp.dma_start(dinv[:, :], S.dinv.partition_broadcast(128)).then_inc(dinv_in, 16)

                def load(q, slot):
                    sp.dma_start(x1[:, slot], by_group(S.x1, q)).then_inc(x1_in[slot], 16)

                load(0, 0)
                load(1, 1)

                def step(q, slot):
                    hold(sp, y_ready, q + 1)
                    sp.dma_start(by_group(out, q), y[:, slot]).then_inc(stored[slot], 16)
                    if not (isinstance(q, int) and q + 2 >= GROUPS):
                        load(q + 2, slot)

                step(0, 0)
                with sp.Fori(0, GROUPS // 2 - 1) as q:
                    for u in range(2):
                        step(q * 2 + (1 + u), 1 - u)
                for q in (GROUPS - 2, GROUPS - 1):
                    step(q, q % 2)
                sp.wait_ge(stored[0], 16 * (GROUPS // 2 + 1))
                sp.wait_ge(stored[1], 16 * (GROUPS // 2))

            @block.tensor
            def _(pe):
                pe.wait_ge(weights_in, 32)

                def product(c, slot):
                    if later(c, 1):
                        hold(pe, scaled, c)
                    for m in range(2):
                        for k in range(2):
                            last = nc.tensor.matmul(psO[:, slot, m, 0:CN], w[:, k, m * 128:(m + 1) * 128], K.sums[:, k, bass.ds(c * CN, CN)],
                                                    start=(k == 0), stop=(k == 1))
                    last.then_inc(o_done, 1)

                def turn(q, slot):
                    for n in range(GC):
                        c = q * GC + n
                        s = (slot + n) % 2
                        hold(pe, relu_ready, c + 1)
                        if later(q, 1) or n >= 2:
                            hold(pe, added, c - 1)
                        for j in range(2):
                            for k in range(2):
                                last = nc.tensor.transpose(psT[:, s, j, k * 128:(k + 1) * 128], act_o[:, s, k, j * TP:(j + 1) * TP], K.ident[:, :])
                        last.then_inc(turned, 1)

                pairs(pe, CHUNKS, product)
                pairs(pe, GROUPS, turn)

            @block.scalar
            def _(act):
                def bias(c, slot):
                    act.wait_ge(scaled, c + 1)
                    for k in range(2):
                        last = act.activation(o[:, k, bass.ds(c * CN, CN)], o[:, k, bass.ds(c * CN, CN)], ACT.Identity, bias=vec[:, 0, k:k + 1])
                    last.then_inc(o_ready, 1)

                def relu(q, slot):
                    for n in range(GC):
                        c = q * GC + n
                        if later(q, 1) or n >= 2:
                            act.wait_ge(turned, c - 1)
                        for k in range(2):
                            last = act.activation(act_o[:, (slot + n) % 2, k], o[:, k, bass.ds(c * CN, CN)], ACT.Relu,
                                                  scale=gain[:, k:k + 1], bias=shift[:, k:k + 1])
                        last.then_inc(relu_ready, 1)

                act.wait_ge(weights_in, 32)
                pairs(act, CHUNKS, bias)
                act.wait_ge(norm_ready, 1)
                pairs(act, GROUPS, relu)

            @block.vector
            def _(v):
                link = Link(v, link_v)
                v.wait_ge(dinv_in, 16)

                def measure(c):
                    v.wait_ge(o_ready, c + 1)
                    for k in range(2):
                        last = v.bn_stats(stats[:, k, bass.ds(c, 1)].rearrange("p a s -> p (a s)"), o[:, k, bass.ds(c * CN, CN)])
                    return last

                def scale(c, slot):
                    v.wait_ge(o_done, c + 1)
                    v.tensor_tensor(o[:, :, bass.ds(c * CN, CN)], psO[:, slot, :, 0:CN],
                                    dinv[:, bass.ds(c * CN, CN)].unsqueeze(1).to_broadcast([128, 2, CN]), ALU.mult).then_inc(scaled, 1)
                    if later(c, 1):
                        measure(c - 1)

                pairs(v, CHUNKS, scale)
                link(measure(CHUNKS - 1))
                for k in range(2):
                    last = v.bn_aggr(mv[:, k], stats[:, k])
                link(last)
                link(v.tensor_scalar(var[:, :], mv[:, :, 1], EPS, None, ALU.add))
                rsqrt(v, link, gain[:, :], var[:, :], half[:, :], square[:, :])
                link(v.tensor_tensor(gain[:, :], gain[:, :], vec[:, 1], ALU.mult))
                link(v.tensor_tensor(shift[:, :], mv[:, :, 0], gain[:, :], ALU.mult))
                v.tensor_tensor(shift[:, :], vec[:, 2], shift[:, :], ALU.subtract).then_inc(norm_ready, 1)
                link.restart()

                def last_norm(q, slot):
                    link.restart()
                    hold(v, x1_in[slot], (q - slot + 2) * 8)
                    if later(q, 2):
                        hold(v, stored[slot], (q - slot) * 8)
                    for n in range(GC):
                        c = q * GC + n
                        rows = y[:, slot, 2 * n:2 * n + 2]
                        v.wait_ge(turned, c + 1)
                        v.tensor_tensor(rows, x1[:, slot, 2 * n:2 * n + 2], psT[:, (slot + n) % 2], ALU.add).then_inc(added, 1)
                        v.wait_ge(added, c + 1)
                        for j in range(2):
                            last = v.bn_stats(stat1[:, 2 * n + j], y[:, slot, 2 * n + j])
                    link(last)
                    for t in range(GT):
                        last = v.bn_aggr(mv1[:, t], stat1[:, t])
                    link(last)
                    link(v.tensor_scalar(var1[:, :], mv1[:, :, 1], EPS, None, ALU.add))
                    rsqrt(v, link, rstd1[:, :], var1[:, :], half1[:, :], square1[:, :])
                    for t in range(GT):
                        last = v.tensor_scalar(y[:, slot, t], y[:, slot, t], mv1[:, t, 0:1], rstd1[:, t:t + 1], ALU.subtract, ALU.mult)
                    last.then_inc(y_ready, 1)

                last_norm(0, 0)
                last_norm(1, 1)
                last_norm(2, 0)
                with v.Fori(0, GROUPS // 2 - 1) as q:
                    for u in range(2):
                        last_norm(q * 2 + (3 + u), 1 - u)
        M.close()


def build(nc, A, out):
    S, K = Named(), Named()
    S.proj = nc.dram_tensor("proj_rows", (N, ROW), F32).ap()
    S.stgt = nc.dram_tensor("target_scores", (NA, SPLITS * HEADS), BF16).ap()
    S.smax = nc.dram_tensor("source_maxima", (TP * HEADS,), F32).ap()
    S.low = nc.dram_tensor("window_lows", (NSB,), F32).ap()
    S.span = nc.dram_tensor("superblock_widths", (NSB,), F32).ap()
    S.deg = nc.dram_tensor("out_degrees", (NHIST,), F32).ap()
    S.key = nc.dram_tensor("keys", (N,), F32).ap()
    S.rank = nc.dram_tensor("ranks", (N,), I32).ap()
    S.xs = nc.dram_tensor("ordered_rows", (N, D), F32).ap()
    S.ys = nc.dram_tensor("mamba_rows", (N, D), F32).ap()
    S.x1 = nc.dram_tensor("x1_rows", (N, D), F32).ap()
    S.x1d = nc.dram_tensor("x1_scaled_rows", (N, D), F32).ap()
    S.dinv = nc.dram_tensor("degree_scales", (N,), F32).ap()
    S.emax = nc.dram_tensor("score_maxima", (TP,), F32).ap()
    S.den = nc.dram_tensor("weight_sums", (HEADS + 1, NA), F32).ap()
    with ExitStack() as stack:
        P = Parts(nc, stack, "")
        K.ident = P.sb("ident", [128, 128])
        K.iota = P.sb("iota", [128, 128])
        K.pidx = P.sb("pidx", [128, 1])
        K.steps = P.sb("steps", [1, 132])
        K.low = P.sb("low", [128, NSB])
        K.smax = P.sb("smax", [TP, HEADS])
        K.rounds = P.sb("rounds", [1, 1], I32)
        K.rank = P.sb("rank", [TP, TILES], I32)
        K.smaller = P.sb("smaller", [TP, 4 * TILES])
        K.ties = P.sb("ties", [TP, TILES])
        K.sums = P.sb("sums", [128, 2, NA])
        K.den_room = P.sb("den", [128, NA])
        K.den = K.den_room[0:HEADS + 1]
        K.emax = P.sb("emax", [TP, 1])
        tables_block(nc, A, S, K)
        edge_pass(nc, A, S, K, True)
        ranks_block(nc, A, S, K)
        mamba_block(nc, A, S, K)
        nodes_block(nc, A, S, K)
        edge_pass(nc, A, S, K, False)
        output_block(nc, A, S, K, out)


class Named:
    pass


def layout(inputs):
    import numpy as np

    g = {k: np.asarray(v) for k, v in inputs.items()}
    w = {k.split("_gnn_")[1] if "_gnn_" in k else k: v for k, v in g.items()}
    t = lambda a: np.ascontiguousarray(a.T)
    a_blk = np.zeros((D, 2 * HEADS), w["gat_a_src"].dtype)
    for h in range(HEADS):
        a_blk[h * HD:(h + 1) * HD, h] = w["gat_a_src"][h]
        a_blk[h * HD:(h + 1) * HD, HEADS + h] = w["gat_a_tgt"][h]
    halves = lambda a: np.ascontiguousarray(a.reshape(2, 128, -1).transpose(1, 0, 2))
    return {
        "x": w["x"], "xT": t(w["x"]), "src": w["src"], "dst": w["dst"], "node_vec": w["node_vec"],
        "src_cols": np.ascontiguousarray(w["src"].reshape(NSB, KB, TP).transpose(0, 2, 1)),
        "dst_cols": np.ascontiguousarray(w["dst"].reshape(NSB, KB, TP).transpose(0, 2, 1)),
        "gat_w": w["gat_w"], "gat_wT": t(w["gat_w"]), "a_blk": a_blk,
        "in_wT": t(w["in_proj_w"]), "x_wT": t(w["x_proj_w"]), "dt_wT": t(w["dt_proj_w"]), "out_wT": t(w["out_proj_w"]),
        "conv_w": halves(w["conv_w"]), "conv_b": halves(w["conv_b"]), "dt_b": halves(w["dt_proj_b"]),
        "a_log": halves(w["A_log"]), "d_param": halves(w["D_param"]),
        "wlT": t(w["wl"]), "wgT": t(w["wg"]), "ff1_wT": t(w["ff1_w"]), "ff2_wT": t(w["ff2_w"]),
        "ff1_b": t(w["ff1_b"].reshape(4, 128)),
        "rowvecs": np.stack([w[k] for k in ("gat_b", "ln_local_g", "ln_local_b", "ln_global_g", "ln_global_b",
                                            "ln2_g", "ln2_b", "ff2_b")]),
        "gcn_w": w["W"], "colvecs": np.ascontiguousarray(np.stack([w[k].reshape(2, 128) for k in ("b", "gamma", "beta")]).transpose(2, 0, 1)),
        "ident": np.eye(128, dtype=np.float32),
        "iota": np.tile(np.arange(128, dtype=np.float32), (128, 1)),
        "pidx": np.arange(128, dtype=np.float32)[:, None],
        "steps": (W * np.arange(132, dtype=np.float32))[None],
        "tri": np.tril(np.ones((TP, TP), np.float32), -1),
    }


def kernel(**inputs):
    import concourse.bacc as bacc
    from concourse.bass_utils import run_bass_kernel_spmd

    arrays = {k + "_d": v for k, v in layout(inputs).items()}
    nc = bacc.Bacc("TRN2", target_bir_lowering=False, num_devices=1)
    args = Named()
    for name, a in arrays.items():
        args.__dict__[name[:-2]] = nc.dram_tensor(name, a.shape, mybir.dt.from_np(a.dtype), kind="ExternalInput").ap()
    out = nc.dram_tensor("out_d", (N, D), F32, kind="ExternalOutput").ap()
    build(nc, args, out)
    r = run_bass_kernel_spmd(nc, [arrays], core_ids=[0])
    return r.results[0]["out_d"]
```
